# Optimizing a Trainium2 kernel written in Bass

```python
import numpy as np
import jax
import jax.numpy as jnp

def _softmax(x, axis=-1):
    return jax.nn.softmax(x, axis=axis)

def _gelu(x):
    return jax.nn.gelu(x, approximate=True)

def _silu(x):
    return jax.nn.silu(x)

def _sigmoid(x):
    return jax.nn.sigmoid(x)

def _layernorm(x, axis=-1, eps=1e-05):
    m = jnp.mean(x, axis=axis, keepdims=True)
    v = jnp.var(x, axis=axis, keepdims=True)
    return (x - m) / jnp.sqrt(v + eps)

def _scatter_add(tgt, idx, src, axis=0):
    return tgt.at[idx].add(src)

def _segment_sum(src, seg, n):
    return jax.ops.segment_sum(src, seg, n)
kernel_name = 'mk_decoder_preln_d1_seqx_r4_322f53'

def setup_inputs(seed: int=0):
    np.random.seed(seed)
    _w = jnp.asarray

    def _rec_inputs():
        import jax
        import jax.numpy as jnp
        _rk = jax.random.key(seed)
        x = -0.0005146 + 1 * jax.random.normal(jax.random.fold_in(_rk, 1), (2, 1024, 256), jnp.float32)
        _lenS = 1024 - jax.random.randint(jax.random.fold_in(_rk, 7), (2,), 0, max(1, 1024 // 4) + 1, jnp.int32)
        _lenS2 = 77 - jax.random.randint(jax.random.fold_in(_rk, 8), (2,), 0, max(1, 77 // 4) + 1, jnp.int32)
        _ctx_1024P = jax.random.normal(jax.random.fold_in(_rk, 11), (2, 16, 256), jnp.float32)
        _ctx_1024c = jax.random.dirichlet(jax.random.fold_in(_rk, 511), 0.3 * jnp.ones((16,), jnp.float32), (2, 77))
        _ctx_1024t = jnp.einsum('bsk,bkd->bsd', _ctx_1024c, _ctx_1024P)
        _ctx_1024t = _ctx_1024t * jax.lax.rsqrt(jnp.mean(jnp.square(_ctx_1024t)) + 1e-12) * 0.953939
        ctx_1024 = -0.000392918 + 0.999932 * (_ctx_1024t + 0.3 * jax.random.normal(jax.random.fold_in(_rk, 611), (2, 77, 256), jnp.float32))
        return (x, ctx_1024)
    x, ctx_1024 = _rec_inputs()

    def _L0_attn_setup():
        import jax, jax.numpy as jnp
        import numpy as np
        B, S, D, DOUT = (4, 1024, 256, 256)
        key = jax.random.key(seed)
        k1, k2 = jax.random.split(key)
        x = jax.random.normal(k1, (B, S, D), dtype=jnp.float32)
        kernel = jax.random.normal(k2, (3, D, DOUT), dtype=jnp.float32) * 0.02
        return {'x': x, 'kernel': kernel}
    _L0_attn_all = _L0_attn_setup()
    _L0_attn_in = {k: v for k, v in _L0_attn_all.items() if k in ('kernel',)}
    del _L0_attn_all

    def _L0_xattn_setup():
        import jax, jax.numpy as jnp
        import numpy as np
        DIM = 256
        DIM_HEAD = 64
        HEADS = 16
        INNER = DIM_HEAD * HEADS
        EPS = 1e-05

        def layer_norm(x, g, b):
            m = jnp.mean(x, axis=-1, keepdims=True)
            v = jnp.mean(jnp.square(x - m), axis=-1, keepdims=True)
            return (x - m) * jax.lax.rsqrt(v + EPS) * g + b
        key = jax.random.key(seed)
        ks = jax.random.split(key, 8)
        B, N_IMG, N_LAT = (4, 1024, 128)
        std = 1.0 / np.sqrt(DIM)
        return {'image_embeds': jax.random.normal(ks[0], (B, N_IMG, DIM), dtype=jnp.float32), 'latents': jax.random.normal(ks[1], (B, N_LAT, DIM), dtype=jnp.float32), 'ln1_g': jnp.ones((DIM,), jnp.float32), 'ln1_b': jnp.zeros((DIM,), jnp.float32), 'ln2_g': jnp.ones((DIM,), jnp.float32), 'ln2_b': jnp.zeros((DIM,), jnp.float32), 'Wq': jax.random.normal(ks[2], (DIM, INNER), dtype=jnp.float32) * std, 'Wkv': jax.random.normal(ks[3], (DIM, 2 * INNER), dtype=jnp.float32) * std, 'Wo': jax.random.normal(ks[4], (INNER, DIM), dtype=jnp.float32) * std}
    _L0_xattn_all = _L0_xattn_setup()
    _L0_xattn_in = {k: v for k, v in _L0_xattn_all.items() if k in ('ln1_g', 'ln1_b', 'ln2_g', 'ln2_b', 'Wq', 'Wkv', 'Wo')}
    del _L0_xattn_all

    def _L0_ffn_setup():
        import jax, jax.numpy as jnp
        import numpy as np
        TEMPERATURE = 1.0
        TOPK = 2
        key = jax.random.key(seed)
        ks = jax.random.split(key, 6)
        S, B, H, F, E = (512, 4, 256, 1024, 8)
        x = jax.random.normal(ks[0], (S, B, H), dtype=jnp.float32)
        gate_w = jax.random.normal(ks[1], (E, H), dtype=jnp.float32) * (1.0 / np.sqrt(H))
        w1 = jax.random.normal(ks[2], (E, H, F), dtype=jnp.float32) * (1.0 / np.sqrt(H))
        b1 = jnp.zeros((E, F), dtype=jnp.float32)
        w2 = jax.random.normal(ks[3], (E, F, H), dtype=jnp.float32) * (1.0 / np.sqrt(F))
        b2 = jnp.zeros((E, H), dtype=jnp.float32)
        return {'x': x, 'gate_w': gate_w, 'w1': w1, 'b1': b1, 'w2': w2, 'b2': b2}
    _L0_ffn_all = _L0_ffn_setup()
    _L0_ffn_in = {k: v for k, v in _L0_ffn_all.items() if k in ('gate_w', 'w1', 'b1', 'w2', 'b2')}
    del _L0_ffn_all
    return {'x': x, 'ctx_1024': ctx_1024, 'L0_attn_kernel': _L0_attn_in['kernel'], 'L0_xattn_ln1_g': _L0_xattn_in['ln1_g'], 'L0_xattn_ln1_b': _L0_xattn_in['ln1_b'], 'L0_xattn_ln2_g': _L0_xattn_in['ln2_g'], 'L0_xattn_ln2_b': _L0_xattn_in['ln2_b'], 'L0_xattn_Wq': _L0_xattn_in['Wq'], 'L0_xattn_Wkv': _L0_xattn_in['Wkv'], 'L0_xattn_Wo': _L0_xattn_in['Wo'], 'L0_ffn_gate_w': _L0_ffn_in['gate_w'], 'L0_ffn_w1': _L0_ffn_in['w1'], 'L0_ffn_b1': _L0_ffn_in['b1'], 'L0_ffn_w2': _L0_ffn_in['w2'], 'L0_ffn_b2': _L0_ffn_in['b2']}

def reference(x, ctx_1024, L0_attn_kernel, L0_xattn_ln1_g, L0_xattn_ln1_b, L0_xattn_ln2_g, L0_xattn_ln2_b, L0_xattn_Wq, L0_xattn_Wkv, L0_xattn_Wo, L0_ffn_gate_w, L0_ffn_w1, L0_ffn_b1, L0_ffn_w2, L0_ffn_b2):
    import jax
    import jax.numpy as jnp

    def _L0_attn_ref(x, kernel):
        import jax, jax.numpy as jnp
        import numpy as np
        B, S, D, DOUT = (4, 1024, 256, 256)
        k = jnp.einsum('bsd,de->bse', x, kernel[0])
        q = jnp.einsum('bsd,de->bse', x, kernel[1])
        v = jnp.einsum('bsd,de->bse', x, kernel[2])
        dk = jnp.sqrt(jnp.float32(DOUT))
        scores = jnp.einsum('bqe,bke->bqk', q, k) / dk
        weights = jax.nn.softmax(scores, axis=-1)
        return jnp.einsum('bqk,bke->bqe', weights, v)

    def _L0_xattn_ref(image_embeds, latents, ln1_g, ln1_b, ln2_g, ln2_b, Wq, Wkv, Wo):
        import jax, jax.numpy as jnp
        import numpy as np
        DIM = 256
        DIM_HEAD = 64
        HEADS = 16
        INNER = DIM_HEAD * HEADS
        EPS = 1e-05

        def layer_norm(x, g, b):
            m = jnp.mean(x, axis=-1, keepdims=True)
            v = jnp.mean(jnp.square(x - m), axis=-1, keepdims=True)
            return (x - m) * jax.lax.rsqrt(v + EPS) * g + b
        B, S_lat, _ = latents.shape
        x = layer_norm(image_embeds, ln1_g, ln1_b)
        l = layer_norm(latents, ln2_g, ln2_b)
        q = l @ Wq
        kv_in = jnp.concatenate([x, l], axis=1)
        kv = kv_in @ Wkv
        k, v = jnp.split(kv, 2, axis=-1)

        def to_heads(t):
            return t.reshape(t.shape[0], t.shape[1], HEADS, DIM_HEAD).transpose(0, 2, 1, 3)
        q, k, v = (to_heads(q), to_heads(k), to_heads(v))
        scale = 1.0 / np.sqrt(np.sqrt(DIM_HEAD))
        w = jnp.einsum('bhqd,bhkd->bhqk', q * scale, k * scale)
        w = jax.nn.softmax(w.astype(jnp.float32), axis=-1).astype(q.dtype)
        out = jnp.einsum('bhqk,bhkd->bhqd', w, v)
        out = out.transpose(0, 2, 1, 3).reshape(B, S_lat, INNER)
        return out @ Wo

    def _L0_ffn_ref(x, gate_w, w1, b1, w2, b2):
        import jax, jax.numpy as jnp
        import numpy as np
        TEMPERATURE = 1.0
        TOPK = 2
        s, b, h = x.shape
        x_flat = x.reshape(s * b, h)
        logits = x_flat @ gate_w.T
        probs = jax.nn.softmax(logits / TEMPERATURE, axis=-1)
        topk_probs, topk_idx = jax.lax.top_k(probs, TOPK)
        hidden = jax.nn.relu(jnp.einsum('th,ehf->tef', x_flat, w1) + b1[None])
        all_out = jnp.einsum('tef,efh->teh', hidden, w2) + b2[None]
        gathered = jnp.take_along_axis(all_out, topk_idx[:, :, None], axis=1)
        y_flat = jnp.sum(gathered * topk_probs[:, :, None], axis=1)
        return y_flat.reshape(s, b, h)
    x = x + _L0_attn_ref(_layernorm(x, axis=-1), L0_attn_kernel)
    x = x + _L0_xattn_ref(ctx_1024, _layernorm(x, axis=-1), L0_xattn_ln1_g, L0_xattn_ln1_b, L0_xattn_ln2_g, L0_xattn_ln2_b, L0_xattn_Wq, L0_xattn_Wkv, L0_xattn_Wo)
    x = x + _L0_ffn_ref(_layernorm(x, axis=-1), L0_ffn_gate_w, L0_ffn_w1, L0_ffn_b1, L0_ffn_w2, L0_ffn_b2)
    return x

_drawn_inputs = setup_inputs


def setup_inputs(seed=0):
    import zlib

    import numpy as np

    out = dict(_drawn_inputs(seed))
    spreads = {'L0_xattn_ln1_g': (1.0, 0.2),
     'L0_xattn_ln1_b': (0.0, 0.289),
     'L0_xattn_ln2_g': (1.0, 0.2),
     'L0_xattn_ln2_b': (0.0, 0.1),
     'L0_ffn_b1': (0.0, 0.268),
     'L0_ffn_b2': (0.0, 0.1)}
    factors = {}
    for name, (base, spread) in spreads.items():
        noise = np.random.default_rng([zlib.crc32(name.encode()), seed]).standard_normal(out[name].shape)
        drawn = base * np.exp(spread * noise) if base else spread * noise
        out[name] = jnp.asarray(drawn.astype(out[name].dtype))
    for name, factor in factors.items():
        out[name] = (out[name] * factor).astype(out[name].dtype)
    return out
```

```python
import concourse.bass as bass
from concourse import mybir
from contextlib import ExitStack

F32 = mybir.dt.float32
F16 = mybir.dt.float16
I32 = mybir.dt.int32
U32 = mybir.dt.uint32
ALU = mybir.AluOpType
ACT = mybir.ActivationFunctionType
AX = mybir.AxisListType

STAGES = 3
DEBUG = None


def build(nc, x_in, ctx_in, attn_w, ln1_g, ln1_b, ln2_g, ln2_b, wq_in, wkv_in, wo_in,
          gate_in, w1_in, b1_in, w2_in, b2_in, out):
    P = 128
    B, S, D = x_in.shape
    C = ctx_in.shape[1]
    NT = B * S // P
    TB = S // P
    KD = D // P
    SK = S + C
    EPS = 1e-5
    BANK = 512
    CH = 512
    NG = 4

    ARENA = 152 * 512

    es = ExitStack()
    with es:
        def sb(name, shape, dt):
            return es.enter_context(nc.sbuf_tensor(name, shape, dt))

        def sem(name):
            return es.enter_context(nc.semaphore(name))

        x = sb("x", [P, NT, D], F32)
        l_sb = sb("l_sb", [P, 2 * KD * B * SK], F16)
        lT = [l_sb[:, h * KD * B * SK:(h + 1) * KD * B * SK].rearrange("p (k b n) -> p k b n", k=KD, b=B)
              for h in range(2)]
        identf = sb("identf", [P, P], F32)
        stats = sb("stats", [P, NT, 6], F32)
        mv = sb("mv", [P, NT, 2], F32)
        veps = sb("veps", [P, NT], F32)
        rstd = sb("rstd", [P, NT], F32)
        half = sb("half", [P, NT], F32)
        arena = sb("arena", [P, ARENA], F16)
        ps = es.enter_context(nc.psum_tensor("ps", [P, 8, BANK], F32))

        cursor = [0]

        def room(shape, dt):
            n = 1
            for s in shape:
                n *= s
            size = n * (4 if dt is F32 else 2) // 2
            at = cursor[0]
            cursor[0] = at + -(-size // 16) * 16
            assert cursor[0] <= ARENA, cursor
            v = arena[:, at:at + size]
            if dt is F32:
                v = v.bitcast(F32)
            names = "abcd"[:len(shape)]
            if len(shape) > 1:
                v = v.rearrange(f"p ({' '.join(names)}) -> p {' '.join(names)}",
                                **{m: s for m, s in zip(names[1:], shape[1:])})
            return v

        E, F = b1_in.shape
        MF = F // P
        W1_F16 = KD * F
        W2_F16 = MF * D
        w1 = arena[:, 0:2 * E * W1_F16]
        w2 = arena[:, 2 * E * W1_F16:2 * E * (W1_F16 + W2_F16)]
        EARLY = E - 1
        ATTN = 28 * 1024
        cursor[0] = ATTN

        wraw = room([3, KD, D], F32)
        wa = [room([3, KD, D], F16) for _ in range(2)]
        xn = [room([D], F32) for _ in range(4)]
        qT = [room([KD, S], F16) for _ in range(2)]
        kT = [room([KD, S], F16) for _ in range(2)]
        va = [room([TB, D], F16) for _ in range(2)]
        p32 = [room([S], F32) for _ in range(2)]
        pT = [[room([TB, P], F16) for _ in range(2)] for _ in range(2)]
        negmax = room([TB], F32)
        nmax = room([TB], F32)
        den = room([TB], F32)
        rden = room([TB], F32)

        HD = 64
        HW = 2 * HD
        NP = wq_in.shape[1] // HW
        KT = TB + 1
        A_SLOTS = 2 * KT
        cursor[0] = ATTN
        wxraw = room([3, KD, HW], F32)
        woraw = room([D], F32)
        wx = [room([3, KD, HW], F16) for _ in range(2)]
        wo = [room([D], F16) for _ in range(2)]
        qn = [room([S], F16) for _ in range(2)]
        kn = [room([SK], F16) for _ in range(2)]
        qA = [[room([S], F16) for _ in range(2)] for _ in range(B)]
        qB = [[room([S], F16) for _ in range(2)] for _ in range(B)]
        kA = [[room([SK], F16) for _ in range(2)] for _ in range(B)]
        kB = [[room([SK], F16) for _ in range(2)] for _ in range(B)]
        vh = [room([KT, 2, HD + 1], F16) for _ in range(B)]
        vl = [room([KT, 2, HD], F16) for _ in range(B)]
        px = [room([S], F32) for _ in range(2)]
        PR = 4
        pr = [[room([S], F16) for _ in range(2)] for _ in range(PR)]
        pc = [room([S], F16) for _ in range(2)]
        o32 = room([TB, HW], F32)
        oT = [room([TB, P], F16) for _ in range(2)]
        mx3 = sb("mx3", [P, 2 * TB, 3], F32)
        m16 = sb("m16", [P, 2 * TB], F32)
        mT = sb("mT", [2 * TB, P], F16)
        rden8 = sb("rden8", [P, TB], F32)
        ROW_B1 = 4 * KD
        ROW_GATE = ROW_B1 + E * MF
        ROWS = ROW_GATE + E * KD
        rows_sb = sb("rows_sb", [ROWS, P], F32)
        cols_sb = sb("cols_sb", [P, ROWS], F32)

        def gain_shift(which, k):
            at = which * 2 * KD + k
            return dict(scale=cols_sb[:, at:at + 1], bias=cols_sb[:, at + KD:at + KD + 1])

        zn = [px[0][:, i * D:(i + 1) * D] for i in range(4)]
        yn = [px[1][:, i * D:(i + 1) * D] for i in range(4)]
        t32 = [pr[i][0].rearrange("p (n) -> p n", n=S).bitcast(F32) for i in range(2)]
        ctx_sb = sb("ctx_sb", [C, B, D], F32)
        cstats = sb("cstats", [C, B, 6], F32)
        cmv = sb("cmv", [C, B, 2], F32)
        cveps = sb("cveps", [C, B], F32)
        crstd = sb("crstd", [C, B], F32)
        cz = sb("cz", [C, B, D], F32)
        ct32 = sb("ct32", [P, KD, B, C], F32)

        cursor[0] = 2 * E * (W1_F16 + W2_F16)
        xb = [room([D], F32) for _ in range(2)]
        xbT = [[room([KD, P], F16) for _ in range(2)] for _ in range(2)]
        h32 = [room([MF, P], F32) for _ in range(2)]
        hT = [[room([MF, P], F16) for _ in range(2)] for _ in range(2)]
        yb = [room([D], F32) for _ in range(2)]
        cursor[0] = 2 * E * (W1_F16 + W2_F16)
        gT = [[room([KD, 2 * P], F16) for _ in range(2)] for _ in range(2)]
        probs8 = room([NT, E], F32)
        ex8 = room([NT, E], F32)
        mx8 = room([NT], F32)
        sum8 = room([NT], F32)
        rec8 = room([NT], F32)
        top8 = sb("top8", [P, NT, 8], F32)
        idx8 = sb("idx8", [P, NT, 8], U32)
        idxf = room([NT, 2], F32)
        oh = [room([NT, E], F32) for _ in range(2)]
        wm = room([NT, E], F32)
        wm1 = room([NT, E], F32)
        mask = room([NT, E], F16)
        tot = room([E, NT], F32)
        inc = room([E, NT], F32)
        slotf = room([NT, E], F32)
        sl = [room([NT, E], F32) for _ in range(2)]
        sfl = room([2, NT], F32)
        nblk = room([3, E], F32)
        wmT = room([2 * P], F32)
        slot_u = sb("slot_u", [P, 2, NT], U32)
        nblk_i = sb("nblk_i", [P, 2, E], I32)
        SLOTS_MAX = NT * P * 2 // P + E - 1
        eid_f = sb("eid_f", [1, SLOTS_MAX, E], F32)
        eid_s = sb("eid_s", [1, 2, SLOTS_MAX], F32)
        eid = sb("eid", [1, SLOTS_MAX], I32)
        iota8 = sb("iota8", [P, E], F32)
        jot = sb("jot", [1, SLOTS_MAX], F32)
        upper = sb("upper", [P, P], F16)
        ones16 = sb("ones16", [P, P], F16)
        noreset = sb("noreset", [P, E, NT], F32)
        b2_sb = sb("b2_sb", [E, D], F32)
        b1cur = sb("b1cur", [P, 2, MF], F32)
        gate = [sb(f"gate_{h}", [P, E, KD], F16) for h in range(2)]
        zero = sb("zero", [P, D], F32)
        raw = [sb(f"raw{i}", [P, 2 * CH], F32) for i in range(2)]
        xn3 = [l_sb[:, t * 2 * D:(t + 1) * 2 * D].bitcast(F32) for t in range(NT)]
        yt = [h32[i // 2].rearrange("p m n -> p (m n)")[:, i % 2 * 2 * D:(i % 2 + 1) * 2 * D].rearrange("p (a d) -> p a d", a=2) for i in range(4)]
        xg = nc.dram_tensor("xg", (SLOTS_MAX * P, D), F32, kind="Internal").ap()
        yg = nc.dram_tensor("yg", (SLOTS_MAX * P, D), F32, kind="Internal").ap()

        x_loaded = [sem(f"x_loaded_{g}") for g in range(NT // NG)]
        wa_loaded = sem("wa_loaded")
        wa_split = sem("wa_split")
        consts = sem("consts")
        consts0 = sem("consts0")
        stat_a = sem("stat_a")
        var_ready = sem("var_ready")
        rstd_ready = sem("rstd_ready")
        xn_ready = sem("xn_ready")
        xnT_filled = sem("xnT_filled")
        xnT_hi = sem("xnT_hi")
        xnT_done = sem("xnT_done")
        proj_filled = sem("proj_filled")
        proj_hi = sem("proj_hi")
        proj_done = sem("proj_done")
        a_scores = sem("a_scores")
        a_negmax = sem("a_negmax")
        a_max = sem("a_max")
        a_probs = sem("a_probs")
        a_pT = sem("a_pT")
        a_pT_hi = sem("a_pT_hi")
        a_pT_lo = sem("a_pT_lo")
        a_out = sem("a_out")
        a_rden = sem("a_rden")
        a_added = sem("a_added")
        out_done = sem("out_done")
        rows_loaded = sem("rows_loaded")
        cols_filled = sem("cols_filled")
        cols_ready = sem("cols_ready")
        ctx_loaded = sem("ctx_loaded")
        c_stat = sem("c_stat")
        c_rstd = sem("c_rstd")
        c_norm = sem("c_norm")
        c_filled = sem("c_filled")
        c_t32 = sem("c_t32")
        c_hi = sem("c_hi")
        c_done = sem("c_done")
        z_stat = sem("z_stat")
        z_var = sem("z_var")
        z_rstd = sem("z_rstd")
        z_first = sem("z_first")
        z_norm = sem("z_norm")
        z_filled = sem("z_filled")
        z_t32 = sem("z_t32")
        z_hi = sem("z_hi")
        z_done = sem("z_done")
        x_consts0 = sem("x_consts0")
        x_consts = sem("x_consts")
        wx_loaded = sem("wx_loaded")
        wo_loaded = sem("wo_loaded")
        wx_split = sem("wx_split")
        wo_split = sem("wo_split")
        task_filled = sem("task_filled")
        task_hi = sem("task_hi")
        task_done = sem("task_done")
        m_reduced = sem("m_reduced")
        qk_spread = sem("qk_spread")
        m_spread = sem("m_spread")
        scores = sem("scores")
        probs = sem("probs")
        raw_loaded = [sem(f"raw_loaded{i}") for i in range(2)]
        late_loaded = [sem(f"late_loaded{i}") for i in range(2)]
        raw_hi = sem("raw_hi")
        raw_split = sem("raw_split")
        late_hi = sem("late_hi")
        late_split = sem("late_split")
        f_consts0 = sem("f_consts0")
        f_consts = sem("f_consts")
        zero_set = sem("zero_set")
        xg_zeroed = sem("xg_zeroed")
        b2_loaded = sem("b2_loaded")
        g_stat = sem("g_stat")
        g_var = sem("g_var")
        g_rstd = sem("g_rstd")
        g_norm = sem("g_norm")
        g_filled = sem("g_filled")
        g_hi = sem("g_hi")
        g_lo = sem("g_lo")
        g_logits = sem("g_logits")
        gate_split = sem("gate_split")
        ex_ready = sem("ex_ready")
        ex_done = sem("ex_done")
        route = sem("route")
        mask_ready = sem("mask_ready")
        counted = sem("counted")
        slots_ready = sem("slots_ready")
        eid_ready = sem("eid_ready")
        wm_ready = sem("wm_ready")
        wmT_filled = sem("wmT_filled")
        wmT_ready = sem("wmT_ready")
        b2_filled = sem("b2_filled")
        b2_added = sem("b2_added")
        scattered = sem("scattered")
        xb_loaded = [sem(f"xb_loaded{i}") for i in range(2)]
        e_T = sem("e_T")
        e_T_hi = sem("e_T_hi")
        e_T_lo = sem("e_T_lo")
        e_h = sem("e_h")
        e_h32 = sem("e_h32")
        e_hT_hi = sem("e_hT_hi")
        e_hT_lo = sem("e_hT_lo")
        e_y = sem("e_y")
        e_yb = sem("e_yb")
        e_bias = sem("e_bias")
        y_stored = [sem(f"y_stored{i}") for i in range(2)]
        gathered = [sem(f"gathered{i}") for i in range(4)]
        combined = sem("combined")
        probs_hi = sem("probs_hi")
        probs_lo = sem("probs_lo")
        mixed = sem("mixed")
        o_rden = sem("o_rden")
        o_done = sem("o_done")

        LAG = 2
        IT = 2 * A_SLOTS
        MC = 3
        MW = SK // MC
        PREP = ([("q", c) for c in range(2)] + [("k", c) for c in range(MC)] + [("v", i) for i in range(3)]
                + [("max", h, j, c) for h in range(2) for j in range(TB) for c in range(MC)] + [("m",)])
        FINISH = [("oT", i) for i in range(2)] + [("wo", i) for i in range(TB // 2)]
        HI_TASKS = ("q", "k", "v", "oT")

        def unit_tasks(finish, prep):
            out = []
            if prep is not None:
                at = [(0, 1), (0, 0), (0, 0), (1, 1), (1, 0), (2, 1), (2, 0), (2, 0)]
                maxima = [((6 + n * 26 // 48) // 2, 1 - n * 26 // 48 % 2) for n in range(48)]
                out += [(*w, (prep, *t)) for w, t in zip(at + maxima + [(16, 1)], PREP)]
            if finish is not None:
                at = [(3, 1), (3, 0), (4, 1), (4, 0), (5, 1), (5, 0)]
                out += [(*w, (finish, *t)) for w, t in zip(at, FINISH)]
            return sorted(out, key=lambda w: (w[0], -w[1]))

        def iteration_tasks(first, last):
            a = unit_tasks(None if first else 1, 1)
            b = unit_tasks(0, None if last else 0)
            return a + [(s + A_SLOTS, before, t) for s, before, t in b]

        LAST_TASK = 2 * NP * (len(PREP) + len(FINISH))

        class Iteration:

            def __init__(self, hp, first, last):
                self.hp, self.first, self.last = hp, first, last
                self.slots = hp * IT
                self.units = hp * 2
                n, f = len(PREP), len(FINISH)
                self.task0 = n if first else hp * 2 * (n + f) + n - f
                self.hi0 = 8 if first else hp * 20 + 6
                self.tasks, hi = [], 0
                for i, (s, before, t) in enumerate(iteration_tasks(first, last)):
                    self.tasks.append((s, before, t, i, hi))
                    hi += t[1] in HI_TASKS

            def of(self, slot, before):
                return [w[2:] for w in self.tasks if w[0] == slot and w[1] == before]

            def number(self, b, *task):
                return next(i for _, _, t, i, _ in self.tasks if t == (b, *task)) + self.task0 + 1

        PROLOGUE = [((0, *t), i, min(i, 8)) for i, t in enumerate(PREP)]

        def bank(task0, i):
            return 6 + (i + (task0 if isinstance(task0, int) else 1)) % 2

        def wait(eng, sem, value):
            if not isinstance(value, int) or value > 0:
                eng.wait_ge(sem, value)

        def lat_slot(n):
            return n // TB * KT + n % TB

        def over_pairs(eng, body):
            body(Iteration(0, True, False))
            with eng.Fori(1, NP - 1) as hp:
                body(Iteration(hp, False, False))
            body(Iteration(NP - 1, False, True))

        LOOPED = (SLOTS_MAX - 2) // 2 * 2

        def over_blocks(eng, body):
            for j in range(2):
                body(j, j, False)
            with eng.Fori(1, LOOPED // 2) as i:
                for c in range(2):
                    body(i * 2 + c, c, True)
            for j in range(LOOPED, SLOTS_MAX):
                body(j, j % 2, False)

        def chunk(n):
            if n < 2 * E:
                e, k = n // 2, n % 2
                src = w1_in[e, k * P:(k + 1) * P, :]
                at = [((e * 2 + h) * KD + k) * F for h in range(2)]
                return src, [w1[:, a:a + F] for a in at]
            e, g = (n - 2 * E) // 2, n % 2
            src = w2_in[e, g * 4 * P:(g + 1) * 4 * P, :].rearrange("(m p) d -> p m d", p=P)
            at = [((e * 2 + h) * MF + g * 4) * D for h in range(2)]
            return src, [w2[:, a:a + 4 * D] for a in at]

        EARLY_CHUNKS = 2 * EARLY
        CHUNKS = 4 * E

        def raw_as(n):
            r = raw[n % 2][:, :]
            return r if n < 2 * E else r.rearrange("p (m d) -> p m d", d=D)

        block = es.enter_context(nc.Block())
        x_v = x_in.rearrange("b (t p) d -> p (b t) d", p=P)
        out_v = out.rearrange("b (t p) d -> p (b t) d", p=P)

        @block.sync
        def _(sp):
            for g in range(NT // NG):
                sp.dma_start(x[:, g * NG:(g + 1) * NG, :], x_v[:, g * NG:(g + 1) * NG, :]).then_inc(x_loaded[g], 16)
            sp.dma_start(wraw, attn_w.rearrange("w (k p) e -> p w k e", p=P)).then_inc(wa_loaded, 16)
            for i, row in enumerate((ln1_g, ln1_b, ln2_g, ln2_b)):
                sp.dma_start(rows_sb[i * KD:(i + 1) * KD, :], row.rearrange("(k p) -> k p", p=P)).then_inc(rows_loaded, 16)
            sp.dma_start(rows_sb[ROW_B1:ROW_GATE, :], b1_in.rearrange("e (m p) -> (e m) p", p=P)).then_inc(rows_loaded, 16)
            sp.dma_start(rows_sb[ROW_GATE:ROWS, :], gate_in.rearrange("e (k p) -> (e k) p", p=P)).then_inc(rows_loaded, 16)
            sp.dma_start(ctx_sb[:, :, :], ctx_in.rearrange("b c d -> c b d")).then_inc(ctx_loaded, 16)

            wq_v = wq_in.rearrange("(k p) n -> p k n", p=P)
            wkv_v = wkv_in.rearrange("(k p) n -> p k n", p=P)

            def at_pair(hp, start=0):
                at = hp * HW + start
                return slice(at, at + HW) if isinstance(hp, int) else bass.ds(sp.snap(at), HW)

            def load_wx(hp, free):
                where = [at_pair(hp), at_pair(hp), at_pair(hp, NP * HW)]
                wait(sp, wx_split, free)
                for i, (src, cols) in enumerate(zip((wq_v, wkv_v, wkv_v), where)):
                    sp.dma_start(wxraw[:, i, :, :], src[:, :, cols]).then_inc(wx_loaded, 16)

            def load_wo(hp):
                rows = at_pair(hp)
                wait(sp, wo_split, hp * 2)
                sp.dma_start(woraw, wo_in[rows, :]).then_inc(wo_loaded, 16)

            def spread_qk(b, last_task):
                sp.wait_ge(task_done, last_task)
                lo, hi = slice(0, HD), slice(HD, P)
                for dst, src in ((qA[b][0][lo], qn[0][lo]), (qA[b][0][hi], qn[1][lo]),
                                 (qA[b][1][lo], qn[1][hi]), (qA[b][1][hi], qn[0][hi]),
                                 (qB[b][0][lo], qn[0][lo]), (qB[b][1][hi], qn[0][hi]),
                                 (kA[b][0][lo], kn[0][lo]), (kA[b][0][hi], kn[0][lo]),
                                 (kA[b][1][lo], kn[0][hi]), (kA[b][1][hi], kn[0][hi]),
                                 (kB[b][0][lo], kn[1][lo]), (kB[b][1][hi], kn[1][hi])):
                    sp.dma_start(dst, src).then_inc(qk_spread, 16)

            def spread_m(b, m_task):
                sp.wait_ge(task_done, m_task)
                for h, row in ((0, HD), (1, 0)):
                    sp.dma_start(qB[b][h][row:row + 1, :].rearrange("a (j n) -> a j n", n=P),
                                 mT[h * TB:(h + 1) * TB, :]).then_inc(m_spread, 16)

            sp.dma_start(b2_sb[:, :], b2_in).then_inc(b2_loaded, 16)
            sp.wait_ge(a_added, NT)
            load_wx(0, 0)
            sp.wait_ge(x_consts, 1)
            spread_qk(0, 5)
            spread_m(0, len(PREP))

            def pair(it):
                if not it.last:
                    load_wx(it.hp + 1, (it.hp + 1) * 2)
                load_wo(it.hp)
                spread_qk(1, it.number(1, "k", MC - 1))
                spread_m(1, it.number(1, "m"))
                if not it.last:
                    spread_qk(0, it.number(0, "k", MC - 1))
                    spread_m(0, it.number(0, "m"))
            over_pairs(sp, pair)
            sp.wait_ge(task_done, LAST_TASK)
            for n in range(EARLY_CHUNKS, CHUNKS):
                sp.wait_ge(raw_split, min(n - 1, EARLY_CHUNKS))
                if n - 2 >= EARLY_CHUNKS:
                    sp.wait_ge(late_split, n - 1 - EARLY_CHUNKS)
                sp.dma_start(raw_as(n), chunk(n)[0]).then_inc(late_loaded[n % 2], 16)
            sp.wait_ge(scattered, 2 * NT * 16)

            def rows_of(j):
                return slice(j * P, (j + 1) * P) if isinstance(j, int) else bass.ds(sp.snap(j * P), P)

            for j in range(2):
                sp.dma_start(xb[j], xg[rows_of(j), :]).then_inc(xb_loaded[j], 16)

            def block_io(j, c, looped):
                if looped or j + 2 < SLOTS_MAX:
                    rows = rows_of(j + 2)
                    sp.wait_ge(e_T, j + 1)
                    sp.dma_start(xb[c], xg[rows, :]).then_inc(xb_loaded[c], 16)
                rows = rows_of(j)
                sp.wait_ge(e_yb, j + 1)
                sp.dma_start(yg[rows, :], yb[c]).then_inc(y_stored[c], 16)
            over_blocks(sp, block_io)
            for g in range(NT // 2):
                sp.wait_ge(combined, 2 * (g * 2 + 2))
                sp.dma_start(out_v[:, g * 2:g * 2 + 2, :], x[:, g * 2:g * 2 + 2, :]).then_inc(out_done, 16)
            sp.wait_ge(out_done, NT // 2 * 16)

        def split_early(pool, n):
            pool.wait_ge(raw_loaded[n % 2], (n // 2 + 1) * 16)
            dst = [d.rearrange("p (m d) -> p m d", d=D) if n >= 2 * E else d for d in chunk(n)[1]]
            pool.tensor_copy(dst[0], raw_as(n)).then_inc(raw_hi, 1)
            pool.wait_ge(raw_hi, n + 1)
            pool.tensor_tensor(dst[1], raw_as(n), dst[0], ALU.subtract).then_inc(raw_split, 1)

        @block.gpsimd
        def _(pool):
            pool.memset(identf[:, :], 0.0).then_inc(consts0, 1)
            pool.memset(half[:, :], -0.5).then_inc(consts0, 1)
            pool.wait_ge(consts0, 2)
            pool.affine_select(out=identf[:, :], in_=identf[:, :], compare_op=ALU.not_equal, fill=1.0,
                               base=0, pattern=[[-1, P]], channel_multiplier=1).then_inc(consts, 1)
            pool.memset(zero[:, :], 0.0).then_inc(zero_set, 1)
            pool.wait_ge(zero_set, 1)
            pool.dma_start(xg.rearrange("(j p) d -> p j d", p=P), zero[:, None, :].to_broadcast([P, SLOTS_MAX, D])).then_inc(xg_zeroed, 16)
            pool.iota(iota8[:, :], pattern=[[1, E]], base=0, channel_multiplier=0,
                      allow_small_or_imprecise_dtypes=True).then_inc(f_consts, 1)
            pool.iota(jot[:, :], pattern=[[1, SLOTS_MAX]], base=0, channel_multiplier=0,
                      allow_small_or_imprecise_dtypes=True).then_inc(f_consts, 1)
            pool.memset(ones16[:, :], 1.0).then_inc(f_consts0, 1)
            pool.memset(noreset[:, :, :], 1.0).then_inc(f_consts0, 1)
            pool.wait_ge(f_consts0, 2)
            pool.memset(noreset[:, :, 0:1], 0.0).then_inc(f_consts, 1)
            pool.affine_select(out=upper[:, :], in_=ones16[:, :], compare_op=ALU.is_gt, fill=0.0,
                               base=0, pattern=[[1, P]], channel_multiplier=-1).then_inc(f_consts, 1)
            for g in range(NT // NG):
                pool.wait_ge(var_ready, g + 1)
                pool.tensor_tensor(rstd[:, g * NG:(g + 1) * NG], veps[:, g * NG:(g + 1) * NG],
                                   half[:, g * NG:(g + 1) * NG], ALU.pow).then_inc(rstd_ready, 1)

            pool.wait_ge(c_stat, 2 * B + 1)
            pool.tensor_tensor(crstd[:, :], cveps[:, :], half[0:C, 0:B], ALU.pow).then_inc(c_rstd, 1)
            for g in range(NT // NG):
                for _ in range(2):
                    n = 2 * g + _
                    pool.wait_ge(z_var, n + 1)
                    pool.tensor_tensor(rstd[:, g * NG:(g + 1) * NG], veps[:, g * NG:(g + 1) * NG],
                                       half[:, g * NG:(g + 1) * NG], ALU.pow).then_inc(z_rstd, 1)

            for n in range(EARLY_CHUNKS):
                if n >= 2:
                    pool.wait_ge(raw_split, n - 1)
                pool.dma_start(raw_as(n), chunk(n)[0]).then_inc(raw_loaded[n % 2], 16)
                if n >= 1:
                    split_early(pool, n - 1)
            split_early(pool, EARLY_CHUNKS - 1)
            for g in range(NT // NG):
                pool.wait_ge(g_var, g + 1)
                pool.tensor_tensor(rstd[:, g * NG:(g + 1) * NG], veps[:, g * NG:(g + 1) * NG],
                                   half[:, g * NG:(g + 1) * NG], ALU.pow).then_inc(g_rstd, 1)
            pool.wait_ge(slots_ready, 1)
            pool.wait_ge(xg_zeroed, 16)
            for t in range(NT):
                for a in range(2):
                    pool.indirect_dma_start(out=xg[:, :], out_offset=bass.IndirectOffsetOnAxis(ap=slot_u[:, a, t:t + 1], axis=0),
                                            in_=xn3[t], in_offset=None).then_inc(scattered, 16)
            pool.wait_ge(y_stored[0], (SLOTS_MAX + 1) // 2 * 16)
            pool.wait_ge(y_stored[1], SLOTS_MAX // 2 * 16)
            for t in range(NT):
                if t >= 4:
                    pool.wait_ge(combined, 2 * (t - 3))
                for a in range(2):
                    pool.indirect_dma_start(out=yt[t % 4][:, a, :], out_offset=None, in_=yg[:, :],
                                            in_offset=bass.IndirectOffsetOnAxis(ap=slot_u[:, a, t:t + 1], axis=0)).then_inc(gathered[t % 4], 16)

        PROJ = 12

        @block.scalar
        def _(act):
            def hi_of_xnT():
                for t in range(0, NT, 2):
                    act.wait_ge(xnT_filled, t // 2 + 1)
                    b, j = t // TB, t % TB
                    act.activation(lT[0][:, :, b, j * P:(j + 2) * P],
                                   ps[:, t // 2 % 2, :].rearrange("p (k n) -> p k n", k=KD),
                                   ACT.Copy).then_inc(xnT_hi, 1)
            hi_of_xnT()
            act.wait_ge(cols_filled, 1)
            act.activation(cols_sb[:, :], ps[:, 3, 0:ROWS], ACT.Copy).then_inc(cols_ready, 1)
            act.wait_ge(cols_ready, 1)
            act.wait_ge(c_filled, 1)
            for b in range(B):
                for k in range(KD):
                    act.activation(ct32[:, k, b, :], ps[:, 2, :].rearrange("p (k b n) -> p k b n", k=KD, b=B)[:, k, b, 0:C],
                                   ACT.Identity, **gain_shift(0, k)).then_inc(c_t32, 1)
            with act.Fori(0, B) as b:
                for n in range(PROJ):
                    act.wait_ge(proj_filled, b * PROJ + n + 1)
                    if n < 8:
                        dst = (qT, kT)[n // 4][0][:, n % 4 // 2, n % 2 * CH:(n % 2 + 1) * CH]
                        src = ps[:, 6 + n % 2, :]
                    else:
                        dst = va[0][:, (n - 8) * 2:(n - 8) * 2 + 2, :]
                        src = ps[:, 6 + n % 2, :].rearrange("p (j d) -> p j d", j=2)
                    act.activation(dst, src, ACT.Copy).then_inc(proj_hi, 1)

                def exp(j):
                    act.wait_ge(a_max, b * TB + j + 1)
                    if j < 2:
                        act.wait_ge(a_pT, b * TB)
                    else:
                        act.wait_ge(a_pT, b * TB + j - 1)
                    act.activation(p32[j % 2], ps[:, j % 2 * 2:j % 2 * 2 + 2, :], ACT.Exp, scale=1.0 / 16,
                                   bias=nmax[:, j:j + 1], accum_out=den[:, j:j + 1]).then_inc(a_probs, 1)
                exp(0)
                exp(1)
                for j in range(TB):
                    act.wait_ge(a_pT, b * TB + j + 1)
                    if j >= 2:
                        act.wait_ge(a_out, b * TB + j - 1)
                    act.activation(pT[j % 2][0], ps[:, 4:6, :].rearrange("p a (c n) -> p (a c) n", n=P),
                                   ACT.Copy).then_inc(a_pT_hi, 1)
                    if j + 2 < TB:
                        exp(j + 2)

            for t in range(0, NT, 2):
                act.wait_ge(z_filled, t // 2 + 1)
                if t >= 4:
                    act.wait_ge(z_done, t // 2 - 1)
                for k in range(KD):
                    act.activation(t32[t // 2 % 2][:, k * 2 * P:(k + 1) * 2 * P], ps[:, t // 2 % 2, k * 2 * P:(k + 1) * 2 * P],
                                   ACT.Identity, **gain_shift(1, k)).then_inc(z_t32, 1)

            def task(it_task0, it_hi0, t, i, hi, units):
                b, kind = t[0], t[1]
                src = ps[:, bank(it_task0, i), :]
                if kind in HI_TASKS:
                    act.wait_ge(task_filled, it_task0 + i + 1)
                if kind == "q":
                    if t[2] == 0:
                        wait(act, qk_spread, units * 192)
                    act.activation(qn[0][:, t[2] * CH:(t[2] + 1) * CH], src, ACT.Copy).then_inc(task_hi, 1)
                elif kind == "k":
                    act.activation(kn[0][:, t[2] * MW:(t[2] + 1) * MW], src[:, 0:MW], ACT.Copy).then_inc(task_hi, 1)
                elif kind == "v":
                    if t[2] == 0:
                        wait(act, mixed, (units - 1) * A_SLOTS)
                    if t[2] < 2:
                        act.activation(vh[b][:, t[2] * 4:t[2] * 4 + 4, :, 0:HD],
                                       src.rearrange("p (j h d) -> p j h d", j=4, h=2), ACT.Copy).then_inc(task_hi, 1)
                    else:
                        act.activation(vh[b][0:C, TB, :, 0:HD], src[0:C, 0:HW].rearrange("p (h d) -> p h d", h=2),
                                       ACT.Copy).then_inc(task_hi, 1)
                elif kind == "oT":
                    act.activation(oT[0][:, t[2] * 4:t[2] * 4 + 4, :], src.rearrange("p (j n) -> p j n", n=P),
                                   ACT.Copy).then_inc(task_hi, 1)

            act.wait_ge(x_consts, 1)
            for t, i, hi in PROLOGUE:
                task(0, 0, t, i, hi, 0)

            def probs_of(it, s):
                n = it.slots + s
                head, kt = s // KT, s % KT
                rows = slice(0, P if kt < TB else C)
                act.wait_ge(scores, n + 1)
                wait(act, probs_lo, n - 1)
                act.activation(px[s % 2][rows], ps[rows, s % 2 * 2:s % 2 * 2 + 2, :], ACT.Exp,
                               scale=0.125).then_inc(probs, 1)
                if kt < TB:
                    dst = pr[(head * TB + kt) % PR][0]
                    wait(act, mixed, it.slots + lat_slot(head * TB + kt - PR) + 1)
                else:
                    dst = pc[0]
                    wait(act, mixed, n - KT + 1)
                act.wait_ge(probs, n + 1)
                act.activation(dst[rows], px[s % 2][rows], ACT.Copy).then_inc(probs_hi, 1)

            def pair(it):
                for s in range(IT):
                    units = it.units + 1 + (s >= A_SLOTS)
                    for t, i, hi in it.of(s, 1):
                        task(it.task0, it.hi0, t, i, hi, units)
                    probs_of(it, s)
                    for t, i, hi in it.of(s, 0):
                        task(it.task0, it.hi0, t, i, hi, units)
            over_pairs(act, pair)
            for i, t in enumerate(FINISH):
                task(LAST_TASK - len(FINISH), 0, (1, *t), i, 0, 2 * NP)

            act.wait_ge(task_done, LAST_TASK)
            for g in range(NT // 2):
                act.wait_ge(g_filled, g + 1)
                wait(act, g_logits, 2 * (g - 1))
                act.activation(gT[g % 2][0], ps[:, g % 2, :].rearrange("p (k n) -> p k n", k=KD),
                               ACT.Copy).then_inc(g_hi, 1)
            act.wait_ge(ex_ready, 1)
            act.activation(probs8, ex8, ACT.Exp).then_inc(ex_done, 1)
            for t in range(NT):
                act.wait_ge(wmT_filled, t + 1)
                wait(act, b2_filled, t - 1)
                act.activation(wmT[0:E, t % 2 * P:(t % 2 + 1) * P], ps[0:E, (3, 6)[t % 2], 0:P], ACT.Copy).then_inc(wmT_ready, 1)
            for n in range(EARLY_CHUNKS, CHUNKS):
                act.wait_ge(late_loaded[n % 2], ((n - EARLY_CHUNKS) // 2 + 1) * 16)
                dst = chunk(n)[1][0]
                act.activation(dst if n < 2 * E else dst.rearrange("p (m d) -> p m d", d=D), raw_as(n), ACT.Copy).then_inc(late_hi, 1)

            def turn_hi(j, c, looped):
                act.wait_ge(e_T, j + 1)
                wait(act, e_h, j - 1)
                act.activation(xbT[c][0], ps[:, c, 0:2 * P].rearrange("p (k n) -> p k n", k=KD), ACT.Copy).then_inc(e_T_hi, 1)

            def hidden(j, c):
                act.wait_ge(e_h, j + 1)
                act.wait_ge(e_bias, j + 1)
                wait(act, e_hT_lo, j - 1)
                for m in range(MF):
                    op = act.activation(h32[c][:, m, :], ps[:, 2 + c * 2 + m // 4, m % 4 * P:(m % 4 + 1) * P], ACT.Relu,
                                        bias=b1cur[:, c, m:m + 1])
                op.then_inc(e_h32, 1)

            turn_hi(0, 0, False)
            turn_hi(1, 1, False)
            hidden(0, 0)

            def block_act(j, c, looped):
                if looped or j + 2 < SLOTS_MAX:
                    turn_hi(j + 2, c, looped)
                if looped or j + 1 < SLOTS_MAX:
                    hidden(j + 1, 1 - c)
                act.wait_ge(e_y, j + 1)
                wait(act, y_stored[c], (j - c) * 8)
                act.activation(yb[c], ps[:, 6 + c, 0:D], ACT.Copy).then_inc(e_yb, 1)
            over_blocks(act, block_act)

        @block.vector
        def _(dve):
            def ln_stats():
                for g in range(NT // NG):
                    dve.wait_ge(x_loaded[g], 16)
                    for t in range(g * NG, (g + 1) * NG):
                        dve.bn_stats(stats[:, t, :], x[:, t, :]).then_inc(stat_a, 1)
                    for t in range(g * NG, (g + 1) * NG):
                        dve.wait_ge(stat_a, g * NG * 2 + t - g * NG + 1)
                        dve.bn_aggr(mv[:, t, :], stats[:, t, :]).then_inc(stat_a, 1)
                    dve.wait_ge(stat_a, (g + 1) * NG * 2)
                    dve.tensor_scalar(veps[:, g * NG:(g + 1) * NG], mv[:, g * NG:(g + 1) * NG, 1], EPS, None,
                                      ALU.add).then_inc(var_ready, 1)
            ln_stats()
            dve.wait_ge(wa_loaded, 16)
            dve.tensor_copy(wa[0], wraw).then_inc(wa_split, 1)
            dve.wait_ge(wa_split, 1)
            dve.tensor_tensor(wa[1], wraw, wa[0], ALU.subtract).then_inc(wa_split, 1)

            def lo_of_xnT(t):
                dve.wait_ge(xnT_hi, t // 2 + 1)
                b, j = t // TB, t % TB
                dve.tensor_tensor(lT[1][:, :, b, j * P:(j + 2) * P],
                                  ps[:, t // 2 % 2, :].rearrange("p (k n) -> p k n", k=KD),
                                  lT[0][:, :, b, j * P:(j + 2) * P], ALU.subtract).then_inc(xnT_done, 1)
            for t in range(0, NT, 2):
                dve.wait_ge(rstd_ready, t // NG + 1)
                if t >= 4:
                    dve.wait_ge(xnT_filled, (t - 4) // 2 + 1)
                for u in (t, t + 1):
                    dve.tensor_scalar(xn[u % 4], x[:, u, :], mv[:, u, 0:1], rstd[:, u:u + 1],
                                      ALU.subtract, ALU.mult).then_inc(xn_ready, 1)
                if t >= 2:
                    lo_of_xnT(t - 2)
            lo_of_xnT(NT - 2)
            dve.wait_ge(ctx_loaded, 16)
            for b in range(B):
                dve.bn_stats(cstats[:, b, :], ctx_sb[:, b, :]).then_inc(c_stat, 1)
            for b in range(B):
                dve.wait_ge(c_stat, b + 1)
                dve.bn_aggr(cmv[:, b, :], cstats[:, b, :]).then_inc(c_stat, 1)
            dve.wait_ge(c_stat, 2 * B)
            dve.tensor_scalar(cveps[:, :], cmv[:, :, 1], EPS, None, ALU.add).then_inc(c_stat, 1)
            dve.wait_ge(c_rstd, 1)
            for b in range(B):
                dve.tensor_scalar(cz[:, b, :], ctx_sb[:, b, :], cmv[:, b, 0:1], crstd[:, b:b + 1],
                                  ALU.subtract, ALU.mult).then_inc(c_norm, 1)
            dve.wait_ge(c_t32, KD * B)
            dve.tensor_copy(lT[0][:, :, :, S:SK], ct32[:, :, :, :]).then_inc(c_hi, 1)
            dve.wait_ge(c_hi, 1)
            dve.tensor_tensor(lT[1][:, :, :, S:SK], ct32[:, :, :, :], lT[0][:, :, :, S:SK], ALU.subtract).then_inc(c_done, 1)
            with dve.Fori(0, B) as b:
                for n in range(PROJ):
                    dve.wait_ge(proj_hi, b * PROJ + n + 1)
                    if n < 8:
                        dst = [h[:, n % 4 // 2, n % 2 * CH:(n % 2 + 1) * CH] for h in (qT, kT)[n // 4]]
                        src = ps[:, 6 + n % 2, :]
                    else:
                        dst = [h[:, (n - 8) * 2:(n - 8) * 2 + 2, :] for h in va]
                        src = ps[:, 6 + n % 2, :].rearrange("p (j d) -> p j d", j=2)
                    dve.tensor_tensor(dst[1], src, dst[0], ALU.subtract).then_inc(proj_done, 1)

                def rowmax(j):
                    dve.wait_ge(a_scores, b * TB + j + 1)
                    dve.tensor_reduce(negmax[:, j:j + 1], ps[:, j % 2 * 2:j % 2 * 2 + 2, :], AX.XY, ALU.max,
                                      negate=True).then_inc(a_negmax, 1)
                    dve.wait_ge(a_negmax, b * TB + j + 1)
                    dve.tensor_scalar(nmax[:, j:j + 1], negmax[:, j:j + 1], 1.0 / 16, None,
                                      ALU.mult).then_inc(a_max, 1)
                rowmax(0)
                rowmax(1)
                for j in range(TB):
                    dve.wait_ge(a_pT_hi, b * TB + j + 1)
                    dve.tensor_tensor(pT[j % 2][1], ps[:, 4:6, :].rearrange("p a (c n) -> p (a c) n", n=P),
                                      pT[j % 2][0], ALU.subtract).then_inc(a_pT_lo, 1)
                    if j + 2 < TB:
                        rowmax(j + 2)
                    dve.reciprocal(rden[:, j:j + 1], den[:, j:j + 1]).then_inc(a_rden, 1)
                    dve.wait_ge(a_rden, b * TB + j + 1)
                    dve.wait_ge(a_out, b * TB + j + 1)
                    xt = x[:, bass.ds(b * TB + j, 1), :].rearrange("p a d -> p (a d)")
                    dve.scalar_tensor_tensor(out=xt, in0=ps[:, 6 + j % 2, 0:D], scalar=rden[:, j:j + 1],
                                             in1=xt, op0=ALU.mult, op1=ALU.add).then_inc(a_added, 1)

            dve.wait_ge(a_added, NT)
            z = [0]

            def stat(op, *a):
                z[0] += 1
                op(*a).then_inc(z_stat, 1)

            for g in range(NT // NG):
                tiles = range(g * NG, (g + 1) * NG)
                gs = slice(g * NG, (g + 1) * NG)
                for turn in range(2):
                    for t in tiles:
                        stat(dve.bn_stats, stats[:, t, :], x[:, t, :] if turn == 0 else yn[t % 4])
                    for t in tiles:
                        dve.wait_ge(z_stat, z[0] - NG + 1)
                        stat(dve.bn_aggr, mv[:, t, :], stats[:, t, :])
                    dve.wait_ge(z_stat, z[0])
                    dve.tensor_scalar(veps[:, gs], mv[:, gs, 1], EPS, None, ALU.add).then_inc(z_var, 1)
                    dve.wait_ge(z_rstd, 2 * g + turn + 1)
                    for t in tiles:
                        if turn == 0:
                            dve.tensor_scalar(yn[t % 4], x[:, t, :], mv[:, t, 0:1], rstd[:, t:t + 1],
                                              ALU.subtract, ALU.mult).then_inc(z_first, 1)
                        else:
                            wait(dve, z_filled, (t - 4) // 2 + 1)
                            dve.tensor_scalar(zn[t % 4], yn[t % 4], mv[:, t, 0:1], rstd[:, t:t + 1],
                                              ALU.subtract, ALU.mult).then_inc(z_norm, 1)
                    if turn == 0:
                        dve.wait_ge(z_first, (g + 1) * NG)
                for t in tiles[::2]:
                    b, j = t // TB, t % TB
                    src = t32[t // 2 % 2].rearrange("p (k n) -> p k n", k=KD)
                    dst = [lT[h][:, :, b, j * P:(j + 2) * P] for h in range(2)]
                    dve.wait_ge(z_t32, t + 2)
                    dve.tensor_copy(dst[0], src).then_inc(z_hi, 1)
                    dve.wait_ge(z_hi, t // 2 + 1)
                    dve.tensor_tensor(dst[1], src, dst[0], ALU.subtract).then_inc(z_done, 1)

            n = 0
            for b in range(B):
                for h, rows in ((0, slice(HD, P)), (1, slice(0, HD))):
                    for buf in (kB[b][h], qB[b][h]):
                        dve.memset(buf[rows], 0.0).then_inc(x_consts0, 1)
                for v in (vh[b], vl[b]):
                    dve.memset(v[HD:P, TB, :, :], 0.0).then_inc(x_consts0, 1)
                dve.memset(pc[b][HD:P], 0.0).then_inc(x_consts0, 1)
                n += 7
            dve.wait_ge(x_consts0, n)
            for b in range(B):
                for h, row in ((0, HD), (1, 0)):
                    dve.memset(kB[b][h][row:row + 1], -8.0).then_inc(x_consts0, 1)
                dve.memset(vh[b][:, 0:TB, :, HD:HD + 1], 1.0).then_inc(x_consts0, 1)
                dve.memset(vh[b][0:C, TB, :, HD:HD + 1], 1.0).then_inc(x_consts0, 1)
                n += 4
            dve.wait_ge(x_consts0, n)
            dve.memset(rden8[:, :], 0.0).then_inc(x_consts, 1)

            def split_wx(hp):
                dve.wait_ge(wx_loaded, (hp + 1) * 48)
                dve.tensor_copy(wx[0], wxraw).then_inc(wx_split, 1)
                dve.wait_ge(wx_split, hp * 2 + 1)
                dve.tensor_tensor(wx[1], wxraw, wx[0], ALU.subtract).then_inc(wx_split, 1)

            def split_wo(hp):
                dve.wait_ge(wo_loaded, (hp + 1) * 16)
                dve.tensor_copy(wo[0], woraw).then_inc(wo_split, 1)
                dve.wait_ge(wo_split, hp * 2 + 1)
                dve.tensor_tensor(wo[1], woraw, wo[0], ALU.subtract).then_inc(wo_split, 1)

            def task(it_task0, it_hi0, t, i, hi, units):
                b, kind = t[0], t[1]
                src = ps[:, bank(it_task0, i), :]
                if kind in HI_TASKS:
                    dve.wait_ge(task_hi, it_hi0 + hi + 1)
                else:
                    dve.wait_ge(task_filled, it_task0 + i + 1)
                if kind == "q":
                    cols = slice(t[2] * CH, (t[2] + 1) * CH)
                    op = dve.tensor_tensor(qn[1][:, cols], src, qn[0][:, cols], ALU.subtract)
                elif kind == "k":
                    cols = slice(t[2] * MW, (t[2] + 1) * MW)
                    op = dve.tensor_tensor(kn[1][:, cols], src[:, 0:MW], kn[0][:, cols], ALU.subtract)
                elif kind == "v" and t[2] < 2:
                    js = slice(t[2] * 4, t[2] * 4 + 4)
                    op = dve.tensor_tensor(vl[b][:, js, :, :], src.rearrange("p (j h d) -> p j h d", j=4, h=2),
                                           vh[b][:, js, :, 0:HD], ALU.subtract)
                elif kind == "v":
                    op = dve.tensor_tensor(vl[b][0:C, TB, :, :], src[0:C, 0:HW].rearrange("p (h d) -> p h d", h=2),
                                           vh[b][0:C, TB, :, 0:HD], ALU.subtract)
                elif kind == "oT":
                    js = slice(t[2] * 4, t[2] * 4 + 4)
                    op = dve.tensor_tensor(oT[1][:, js, :], src.rearrange("p (j n) -> p j n", n=P),
                                           oT[0][:, js, :], ALU.subtract)
                elif kind == "max":
                    _, _, h, j, c = t
                    op = dve.tensor_reduce(mx3[:, h * TB + j, c:c + 1], src[:, 0:MW], AX.X, ALU.max)
                elif kind == "m":
                    wait(dve, m_spread, units * 32)
                    op = dve.tensor_scalar(mT[:, :], src[0:2 * TB, 0:P], 0.125, None, ALU.mult)
                elif kind == "wo":
                    xt = x[:, b * TB + t[2] * 2:b * TB + t[2] * 2 + 2, :]
                    op = dve.tensor_tensor(xt, src.rearrange("p (a d) -> p a d", a=2), xt, ALU.add)
                op.then_inc(task_done, 1)
                if kind == "max" and t[2:] == (1, TB - 1, MC - 1):
                    dve.wait_ge(task_done, it_task0 + i + 1)
                    dve.tensor_reduce(m16[:, :], mx3[:, :, :], AX.X, ALU.max).then_inc(m_reduced, 1)

            def low_half(it, s):
                n = it.slots + s
                head, kt = s // KT, s % KT
                rows = slice(0, P if kt < TB else C)
                if kt < TB:
                    dst = pr[(head * TB + kt) % PR]
                    wait(dve, mixed, it.slots + lat_slot(head * TB + kt - PR) + 1)
                else:
                    dst = pc
                    wait(dve, mixed, n - KT + 1)
                wait(dve, probs_hi, n + 1)
                dve.tensor_tensor(dst[1][rows], px[s % 2][rows], dst[0][rows], ALU.subtract).then_inc(probs_lo, 1)

            def head_out(it, head):
                n = it.units * 2 + head
                dve.wait_ge(mixed, it.slots + (head + 1) * KT)
                acc = ps[:, 4:6, 0:4 * (HD + 1)].rearrange("p a (j d) -> p a j d", d=HD + 1)
                dve.reciprocal(rden8[:, :].rearrange("p (a j) -> p a j", a=2), acc[:, :, :, HD]).then_inc(o_rden, 1)
                dve.wait_ge(o_rden, n + 1)
                for a in range(2):
                    dve.tensor_tensor(o32[:, a * 4:a * 4 + 4, head % 2 * HD:(head % 2 + 1) * HD], acc[:, a, :, 0:HD],
                                      rden8[:, a * 4:a * 4 + 4, None].to_broadcast([P, 4, HD]), ALU.mult).then_inc(o_done, 1)

            split_wx(0)
            for t, i, hi in PROLOGUE:
                task(0, 0, t, i, hi, 0)

            def pair(it):
                for s in range(IT):
                    units = it.units + 1 + (s >= A_SLOTS)
                    for t, i, hi in it.of(s, 1):
                        task(it.task0, it.hi0, t, i, hi, units)
                    if s > 0:
                        low_half(it, s - 1)
                    for head in range(4):
                        if s == head * KT + KT + LAG - 1:
                            head_out(it, head)
                    if s == 1 and not it.first:
                        head_out(Iteration(it.hp - 1, False, False), 3)
                    for t, i, hi in it.of(s, 0):
                        task(it.task0, it.hi0, t, i, hi, units)
                    if s == 10:
                        if not it.last:
                            split_wx(it.hp + 1)
                        split_wo(it.hp)
                low_half(it, IT - 1)
            over_pairs(dve, pair)
            head_out(Iteration(NP - 1, False, True), 3)
            for i, t in enumerate(FINISH):
                task(LAST_TASK - len(FINISH), 20 * NP - 2, (1, *t), i, i, 2 * NP)

            dve.wait_ge(task_done, LAST_TASK)
            dve.tensor_copy(gate[0][:, :, :], cols_sb[:, ROW_GATE:ROWS].rearrange("p (e k) -> p e k", k=KD)).then_inc(gate_split, 1)
            dve.wait_ge(gate_split, 1)
            dve.tensor_tensor(gate[1][:, :, :], cols_sb[:, ROW_GATE:ROWS].rearrange("p (e k) -> p e k", k=KD),
                              gate[0][:, :, :], ALU.subtract).then_inc(gate_split, 1)
            for g in range(NT // NG):
                tiles = range(g * NG, (g + 1) * NG)
                gs = slice(g * NG, (g + 1) * NG)
                for t in tiles:
                    dve.bn_stats(stats[:, t, :], x[:, t, :]).then_inc(g_stat, 1)
                for t in tiles:
                    dve.wait_ge(g_stat, g * NG * 2 + t - g * NG + 1)
                    dve.bn_aggr(mv[:, t, :], stats[:, t, :]).then_inc(g_stat, 1)
                dve.wait_ge(g_stat, (g + 1) * NG * 2)
                dve.tensor_scalar(veps[:, gs], mv[:, gs, 1], EPS, None, ALU.add).then_inc(g_var, 1)

            def gate_lo(g):
                dve.wait_ge(g_hi, g + 1)
                dve.tensor_tensor(gT[g % 2][1], ps[:, g % 2, :].rearrange("p (k n) -> p k n", k=KD),
                                  gT[g % 2][0], ALU.subtract).then_inc(g_lo, 1)
            for t in range(NT):
                dve.wait_ge(g_rstd, t // NG + 1)
                dve.tensor_scalar(xn3[t], x[:, t, :], mv[:, t, 0:1], rstd[:, t:t + 1],
                                  ALU.subtract, ALU.mult).then_inc(g_norm, 1)
                if t % 2 == 1 and t >= 3:
                    gate_lo(t // 2 - 1)
            gate_lo(NT // 2 - 1)

            step = [0]

            def then(ins):
                step[0] += 1
                ins.then_inc(route, 1)
                dve.wait_ge(route, step[0])

            dve.wait_ge(g_logits, NT)
            lg = ps[:, 2, 0:NT * E].rearrange("p (t e) -> p t e", e=E)
            along_e = lambda v: v[:, :, None].to_broadcast([P, NT, E])
            then(dve.tensor_reduce(mx8, lg, AX.X, ALU.max))
            dve.tensor_tensor(ex8, lg, along_e(mx8), ALU.subtract).then_inc(ex_ready, 1)
            dve.wait_ge(ex_done, 1)
            then(dve.tensor_reduce(sum8, probs8, AX.X, ALU.add))
            then(dve.reciprocal(rec8, sum8))
            then(dve.tensor_tensor(ex8, probs8, along_e(rec8), ALU.mult))
            for t in range(NT):
                ins = dve.max(top8[:, t, :], ex8[:, t, :])
            then(ins)
            for t in range(NT):
                ins = dve.max_index(out=idx8[:, t, :], in_max=top8[:, t, :], in_values=ex8[:, t, :])
            then(ins)
            then(dve.tensor_copy(idxf, idx8[:, :, 0:2]))
            dve.wait_ge(f_consts, 4)
            for a in range(2):
                then(dve.tensor_tensor(oh[a], iota8[:, None, :].to_broadcast([P, NT, E]), along_e(idxf[:, :, a]), ALU.is_equal))
            dve.tensor_tensor(mask, oh[0], oh[1], ALU.add).then_inc(mask_ready, 1)
            then(dve.tensor_tensor(wm, oh[0], along_e(top8[:, :, 0]), ALU.mult))
            then(dve.tensor_tensor(wm1, oh[1], along_e(top8[:, :, 1]), ALU.mult))
            dve.tensor_tensor(wm, wm, wm1, ALU.add).then_inc(wm_ready, 1)
            dve.wait_ge(counted, 1)
            before = ps[:, 0, 0:NT * E].rearrange("p (t e) -> p t e", e=E)
            total = ps[:, 0, NT * E:2 * NT * E].rearrange("p (t e) -> p e t", e=E)
            then(dve.tensor_copy(tot, total))
            flat = lambda v: v.rearrange("p e t -> p (e t)")
            then(dve.tensor_tensor_scan(flat(inc), flat(noreset[:, :, :]), flat(tot), 0.0, ALU.mult, ALU.add))
            then(dve.tensor_scalar(nblk_i[:, 0, :], inc[:, :, NT - 1], float(P - 1), None, ALU.add))
            then(dve.tensor_scalar(nblk_i[:, 1, :], nblk_i[:, 0, :], 7, None, ALU.arith_shift_right))
            then(dve.tensor_copy(nblk[:, 0, :], nblk_i[:, 1, :]))
            then(dve.tensor_tensor_scan(nblk[:, 1, :], noreset[:, 0:1, 1:1 + E].rearrange("p a e -> p (a e)"), nblk[:, 0, :], 0.0, ALU.mult, ALU.add))
            then(dve.tensor_tensor(nblk[:, 2, :], nblk[:, 1, :], nblk[:, 0, :], ALU.subtract))
            then(dve.tensor_scalar(nblk[:, 2, :], nblk[:, 2, :], float(P), None, ALU.mult))
            then(dve.tensor_tensor(inc, inc, tot, ALU.subtract))
            then(dve.tensor_tensor(inc, inc, nblk[:, 2, :][:, :, None].to_broadcast([P, E, NT]), ALU.add))
            then(dve.tensor_tensor(slotf, before, inc.rearrange("p e t -> p t e"), ALU.add))
            for a in range(2):
                then(dve.tensor_tensor(sl[a], oh[a], slotf, ALU.mult))
                then(dve.tensor_reduce(sfl[:, a, :], sl[a], AX.X, ALU.add))
            dve.tensor_copy(slot_u[:, :, :], sfl).then_inc(slots_ready, 1)
            then(dve.tensor_tensor(eid_f[:, :, :], jot[:, :, None].to_broadcast([1, SLOTS_MAX, E]),
                                   nblk[0:1, 1, :][:, None, :].to_broadcast([1, SLOTS_MAX, E]), ALU.is_ge))
            then(dve.tensor_reduce(eid_s[:, 0, :], eid_f[:, :, :], AX.X, ALU.add))
            then(dve.tensor_scalar(eid[:, :], eid_s[:, 0, :], float(E - 1), None, ALU.min))
            dve.memset(eid_s[:, 1, :], 0.0).then_inc(eid_ready, 1)
            for t in range(0, NT, 2):
                dve.wait_ge(b2_filled, t + 2)
                dve.tensor_tensor(x[:, t:t + 2, :], ps[:, 4 + t // 2 % 2, :].rearrange("p (a d) -> p a d", a=2),
                                  x[:, t:t + 2, :], ALU.add).then_inc(b2_added, 1)
            for n in range(EARLY_CHUNKS, CHUNKS):
                dve.wait_ge(late_hi, n + 1 - EARLY_CHUNKS)
                dst = [d if n < 2 * E else d.rearrange("p (m d) -> p m d", d=D) for d in chunk(n)[1]]
                dve.tensor_tensor(dst[1], raw_as(n), dst[0], ALU.subtract).then_inc(late_split, 1)

            def turn_lo(j, c):
                dve.wait_ge(e_T_hi, j + 1)
                dve.tensor_tensor(xbT[c][1], ps[:, c, 0:2 * P].rearrange("p (k n) -> p k n", k=KD), xbT[c][0],
                                  ALU.subtract).then_inc(e_T_lo, 1)

            def bias(j, c):
                wait(dve, e_h32, j - 1)
                e = dve.value_load(eid[0:1, j:j + 1] if isinstance(j, int) else eid[0:1, bass.ds(j, 1)], min_val=0, max_val=E - 1)
                dve.tensor_copy(b1cur[:, c, :], cols_sb[:, bass.ds(e * MF + ROW_B1, MF)]).then_inc(e_bias, 1)

            def split_hidden(j, c):
                dve.wait_ge(e_h32, j + 1)
                wait(dve, e_y, j - 1)
                dve.tensor_copy(hT[c][0], h32[c]).then_inc(e_hT_hi, 1)
                dve.wait_ge(e_hT_hi, j + 1)
                dve.tensor_tensor(hT[c][1], h32[c], hT[c][0], ALU.subtract).then_inc(e_hT_lo, 1)

            turn_lo(0, 0)
            bias(0, 0)
            turn_lo(1, 1)
            split_hidden(0, 0)

            def block_dve(j, c, looped):
                if looped or j + 1 < SLOTS_MAX:
                    bias(j + 1, 1 - c)
                if looped or j + 2 < SLOTS_MAX:
                    turn_lo(j + 2, c)
                if looped or j + 1 < SLOTS_MAX:
                    split_hidden(j + 1, 1 - c)
            over_blocks(dve, block_dve)
            for t in range(NT):
                dve.wait_ge(gathered[t % 4], (t // 4 + 1) * 32)
                for a in range(2):
                    if a == 1:
                        dve.wait_ge(combined, 2 * t + 1)
                    dve.scalar_tensor_tensor(out=x[:, t, :], in0=yt[t % 4][:, a, :], scalar=top8[:, t, a:a + 1],
                                             in1=x[:, t, :], op0=ALU.mult, op1=ALU.add).then_inc(combined, 1)

        @block.tensor
        def _(pe):
            pe.wait_ge(consts, 1)
            for t in range(0, NT, 2):
                pe.wait_ge(xn_ready, t + 2)
                if t >= 4:
                    pe.wait_ge(xnT_done, (t - 4) // 2 + 1)
                for k in range(KD):
                    for u in (t, t + 1):
                        mm = pe.transpose(ps[:, t // 2 % 2, k * 2 * P + u % 2 * P:k * 2 * P + u % 2 * P + P],
                                          xn[u % 4][:, k * P:(k + 1) * P], identf[:, :])
                mm.then_inc(xnT_filled, 1)
            pe.wait_ge(xnT_done, NT // 2)
            pe.wait_ge(rows_loaded, 6 * 16)
            pe.transpose(ps[:, 3, 0:ROWS], rows_sb[:, :], identf[0:ROWS, 0:ROWS]).then_inc(cols_filled, 1)
            pe.wait_ge(c_norm, B)
            for b in range(B):
                for k in range(KD):
                    mm = pe.transpose(ps[:, 2, :].rearrange("p (k b n) -> p k b n", k=KD, b=B)[:, k, b, 0:C],
                                      cz[:, b, k * P:(k + 1) * P], identf[0:C, 0:C])
            mm.then_inc(c_filled, 1)
            pe.wait_ge(wa_split, 2)
            EXACT = ((0, 0), (1, 0), (0, 1))

            with pe.Fori(0, B) as b:
                def tokens(half, k, at, n):
                    return lT[half][:, k, bass.ds(b, 1), at:at + n].rearrange("p a n -> p (a n)")
                for n in range(PROJ):
                    if n < 2:
                        pe.wait_ge(a_added, b * TB)
                        pe.wait_ge(proj_done, b * PROJ)
                    else:
                        pe.wait_ge(proj_done, b * PROJ + n - 1)
                    if n < 8:
                        w, m, c = (1, 0)[n // 4], n % 4 // 2, n % 2
                        parts = [(h, k) for h in EXACT for k in range(KD)]
                        for i, ((hw, hx), k) in enumerate(parts):
                            mm = pe.matmul(ps[:, 6 + n % 2, :], wa[hw][:, w, k, m * P:(m + 1) * P],
                                           tokens(hx, k, c * CH, CH), start=(i == 0), stop=(i == len(parts) - 1))
                    else:
                        for j in range(2):
                            parts = [(h, k) for h in EXACT for k in range(KD)]
                            for i, ((hx, hw), k) in enumerate(parts):
                                mm = pe.matmul(ps[:, 6 + n % 2, j * D:(j + 1) * D],
                                               tokens(hx, k, ((n - 8) * 2 + j) * P, P), wa[hw][:, 2, k, :],
                                               start=(i == 0), stop=(i == len(parts) - 1))
                    mm.then_inc(proj_filled, 1)

                def self_scores(j):
                    if j < 2:
                        pe.wait_ge(a_probs, b * TB)
                        pe.wait_ge(proj_done, b * PROJ + 8)
                    else:
                        pe.wait_ge(a_probs, b * TB + j - 1)
                    for c in range(S // CH):
                        parts = [(h, k) for h in EXACT for k in range(KD)]
                        for i, ((hq, hk), k) in enumerate(parts):
                            mm = pe.matmul(ps[:, j % 2 * 2 + c, :], qT[hq][:, k, j * P:(j + 1) * P],
                                           kT[hk][:, k, c * CH:(c + 1) * CH],
                                           start=(i == 0), stop=(i == len(parts) - 1))
                    mm.then_inc(a_scores, 1)
                self_scores(0)
                self_scores(1)
                for j in range(TB):
                    pe.wait_ge(a_probs, b * TB + j + 1)
                    if j == 0:
                        pe.wait_ge(a_pT_lo, b * TB)
                    else:
                        pe.wait_ge(a_pT_lo, b * TB + j)
                    for c in range(TB):
                        mm = pe.transpose(ps[:, 4 + c // 4, c % 4 * P:(c % 4 + 1) * P],
                                          p32[j % 2][:, c * P:(c + 1) * P], identf[:, :])
                    mm.then_inc(a_pT, 1)
                    if j + 2 < TB:
                        self_scores(j + 2)
                    pe.wait_ge(a_pT_lo, b * TB + j + 1)
                    if j < 2:
                        pe.wait_ge(proj_done, (b + 1) * PROJ)
                    else:
                        pe.wait_ge(a_added, b * TB + j - 1)
                    parts = [(h, c) for c in range(TB) for h in EXACT]
                    for i, ((hp, hv), c) in enumerate(parts):
                        mm = pe.matmul(ps[:, 6 + j % 2, 0:D], pT[j % 2][hp][:, c, :], va[hv][:, c, :],
                                       start=(i == 0), stop=(i == len(parts) - 1))
                    mm.then_inc(a_out, 1)

            for t in range(0, NT, 2):
                pe.wait_ge(z_norm, t + 2)
                wait(pe, z_t32, t - 2)
                for k in range(KD):
                    for u in (t, t + 1):
                        mm = pe.transpose(ps[:, t // 2 % 2, k * 2 * P + u % 2 * P:k * 2 * P + u % 2 * P + P],
                                          zn[u % 4][:, k * P:(k + 1) * P], identf[:, :])
                mm.then_inc(z_filled, 1)

            def product(dst, pairs):
                for i, (stationary, moving) in enumerate(pairs):
                    mm = pe.matmul(dst, stationary, moving, start=(i == 0), stop=(i == len(pairs) - 1))
                return mm

            def task(it_task0, t, i, units):
                b, kind = t[0], t[1]
                dst = ps[:, bank(it_task0, i), :]
                wait(pe, task_done, it_task0 + i - 1)
                if kind == "q":
                    if t[2] == 0:
                        pe.wait_ge(wx_split, (units // 2 + 1) * 2)
                    cols = slice(t[2] * CH, (t[2] + 1) * CH)
                    mm = product(dst, [(wx[hw][:, 0, k, :], lT[hx][:, k, b, cols])
                                       for hw, hx in EXACT for k in range(KD)])
                elif kind == "k":
                    cols = slice(t[2] * MW, (t[2] + 1) * MW)
                    mm = product(dst[:, 0:MW], [(wx[hw][:, 1, k, :], lT[hx][:, k, b, cols])
                                                for hw, hx in EXACT for k in range(KD)])
                elif kind == "v":
                    for j in range(4 if t[2] < 2 else 1):
                        at = (t[2] * 4 + j) * P
                        n = min(P, SK - at)
                        mm = product(dst[0:n, j * HW:(j + 1) * HW],
                                     [(lT[hx][:, k, b, at:at + n], wx[hw][:, 2, k, :])
                                      for hx, hw in EXACT for k in range(KD)])
                elif kind == "max":
                    _, _, h, j, c = t
                    if (h, j, c) == (0, 0, 0):
                        pe.wait_ge(qk_spread, (units + 1) * 192)
                    mm = pe.matmul(dst[:, 0:MW], qA[b][h][:, j * P:(j + 1) * P], kA[b][h][:, c * MW:(c + 1) * MW],
                                   start=True, stop=True)
                elif kind == "m":
                    pe.wait_ge(m_reduced, units + 1)
                    mm = pe.transpose(dst[0:2 * TB, 0:P], m16[:, :], identf[:, :])
                elif kind == "oT":
                    if t[2] == 0:
                        pe.wait_ge(o_done, (units - 1) * 4)
                    for j in range(4):
                        mm = pe.transpose(dst[:, j * P:(j + 1) * P], o32[:, t[2] * 4 + j, :], identf[:, :])
                elif kind == "wo":
                    if t[2] == 0:
                        pe.wait_ge(wo_split, units // 2 * 2)
                        pe.wait_ge(task_done, it_task0 + i)
                    for j in range(2):
                        mm = product(dst[:, j * D:(j + 1) * D], [(oT[ho][:, t[2] * 2 + j, :], wo[hw])
                                                                for ho, hw in EXACT])
                mm.then_inc(task_filled, 1)

            pe.wait_ge(z_done, NT // 2)
            pe.wait_ge(c_done, 1)
            pe.wait_ge(x_consts, 1)
            for t, i, _ in PROLOGUE:
                task(0, t, i, 0)

            def score(it, s):
                n = it.slots + s
                b, head, kt = s // A_SLOTS, s // KT % 2, s % KT
                if s % A_SLOTS == 0:
                    pe.wait_ge(m_spread, (it.units + b + 1) * 32)
                wait(pe, probs, n - 1)
                keys = slice(kt * P, min((kt + 1) * P, SK))
                rows = slice(0, keys.stop - keys.start)
                for c in range(S // CH):
                    cols = slice(c * CH, (c + 1) * CH)
                    mm = product(ps[rows, s % 2 * 2 + c, :], [(kA[b][head][:, keys], qA[b][head][:, cols]),
                                                              (kB[b][head][:, keys], qB[b][head][:, cols])])
                mm.then_inc(scores, 1)

            def mix(it, s):
                n = it.slots + s
                b, head, kt = s // A_SLOTS, s // KT, s % KT
                pe.wait_ge(probs_lo, n + 1)
                if kt == 0:
                    wait(pe, o_done, (it.units * 2 + head) * 2)
                p = pr[(head * TB + kt) % PR] if kt < TB else pc
                for j in range(TB):
                    dst = ps[:, 4 + j // 4, j % 4 * (HD + 1):(j % 4 + 1) * (HD + 1)]
                    cols = slice(j * P, (j + 1) * P)
                    last = kt == KT - 1
                    pe.matmul(dst, p[0][:, cols], vh[b][:, kt, head % 2, :], start=(kt == 0 and j % 4 == 0),
                              stop=False, skip_group_check=True)
                    pe.matmul(dst[:, 0:HD], p[0][:, cols], vl[b][:, kt, head % 2, :], start=False,
                              stop=False, skip_group_check=True)
                    mm = pe.matmul(dst, p[1][:, cols], vh[b][:, kt, head % 2, :], start=False,
                                   stop=last, skip_group_check=True)
                mm.then_inc(mixed, 1)

            def pair(it):
                for s in range(IT):
                    units = it.units + 1 + (s >= A_SLOTS)
                    score(it, s)
                    for t, i, _ in it.of(s, 1):
                        task(it.task0, t, i, units)
                    if s >= LAG:
                        mix(it, s - LAG)
                    elif not it.first:
                        mix(Iteration(it.hp - 1, False, False), s - LAG + IT)
                    for t, i, _ in it.of(s, 0):
                        task(it.task0, t, i, units)
            over_pairs(pe, pair)
            for s in range(IT - LAG, IT):
                mix(Iteration(NP - 1, False, True), s)
            for i, t in enumerate(FINISH):
                task(LAST_TASK - len(FINISH), (1, *t), i, 2 * NP + 1)

            pe.wait_ge(task_done, LAST_TASK)
            pe.wait_ge(gate_split, 2)

            def logits(g):
                pe.wait_ge(g_lo, g + 1)
                for u in range(2):
                    t = g * 2 + u
                    product(ps[:, 2, t * E:(t + 1) * E],
                            [(gT[g % 2][hx][:, k, u * P:(u + 1) * P], gate[hg][:, :, k])
                             for hx, hg in EXACT for k in range(KD)]).then_inc(g_logits, 1)
            for g in range(NT // 2):
                pe.wait_ge(g_norm, 2 * g + 2)
                wait(pe, g_lo, g - 1)
                for k in range(KD):
                    for u in range(2):
                        mm = pe.transpose(ps[:, g % 2, (k * 2 + u) * P:(k * 2 + u + 1) * P],
                                          xn3[g * 2 + u][:, k * P:(k + 1) * P], identf[:, :])
                mm.then_inc(g_filled, 1)
                if g >= 1:
                    logits(g - 1)
            logits(NT // 2 - 1)
            pe.wait_ge(mask_ready, 1)
            m2 = mask.rearrange("p t e -> p (t e)")
            pe.matmul(ps[:, 0, 0:NT * E], upper[:, :], m2, start=True, stop=True)
            pe.matmul(ps[:, 0, NT * E:2 * NT * E], ones16[:, :], m2, start=True, stop=True).then_inc(counted, 1)
            pe.wait_ge(wm_ready, 1)
            pe.wait_ge(b2_loaded, 16)

            def second_bias(t):
                pe.wait_ge(wmT_ready, t + 1)
                if t % 2 == 0:
                    wait(pe, b2_added, t // 2 - 1)
                pe.matmul(ps[:, 4 + t // 2 % 2, t % 2 * D:(t % 2 + 1) * D], wmT[0:E, t % 2 * P:(t % 2 + 1) * P], b2_sb[:, :],
                          start=True, stop=True).then_inc(b2_filled, 1)
            for t in range(NT):
                wait(pe, wmT_ready, t - 1)
                pe.transpose(ps[0:E, (3, 6)[t % 2], 0:P], wm[:, t, :], identf[:, :]).then_inc(wmT_filled, 1)
                if t >= 1:
                    second_bias(t - 1)
            second_bias(NT - 1)
            pe.wait_ge(b2_added, NT // 2)
            pe.wait_ge(eid_ready, 1)

            def turn(j, c):
                pe.wait_ge(xb_loaded[c], (j - c) * 8 + 16)
                wait(pe, e_T_lo, j - 1)
                for k in range(KD):
                    mm = pe.transpose(ps[:, c, k * P:(k + 1) * P], xb[c][:, k * P:(k + 1) * P], identf[:, :])
                mm.then_inc(e_T, 1)

            def expert_of(j):
                return pe.value_load(eid[0:1, j:j + 1] if isinstance(j, int) else eid[0:1, bass.ds(j, 1)], min_val=0, max_val=E - 1)

            def up(j, c):
                e = expert_of(j)
                pe.wait_ge(e_T_lo, j + 1)
                wait(pe, e_h32, j - 1)
                for m in range(MF):
                    mm = product(ps[:, 2 + c * 2 + m // 4, m % 4 * P:(m % 4 + 1) * P],
                                 [(w1[:, bass.ds(e * (2 * W1_F16) + (hw * KD + k) * F + m * P, P)], xbT[c][hx][:, k, :])
                                  for hw, hx in EXACT for k in range(KD)])
                mm.then_inc(e_h, 1)

            def down(j, c):
                e = expert_of(j)
                pe.wait_ge(e_hT_lo, j + 1)
                wait(pe, e_yb, j - 1)
                product(ps[:, 6 + c, 0:D],
                        [(hT[c][hh][:, m, :], w2[:, bass.ds(e * (2 * W2_F16) + (hw * MF + m) * D, D)])
                         for m in range(MF) for hh, hw in EXACT]).then_inc(e_y, 1)

            pe.wait_ge(late_split, CHUNKS - EARLY_CHUNKS)
            pe.wait_ge(raw_split, EARLY_CHUNKS)
            turn(0, 0)
            turn(1, 1)
            up(0, 0)

            def block_pe(j, c, looped):
                if looped or j + 2 < SLOTS_MAX:
                    turn(j + 2, c)
                if looped or j + 1 < SLOTS_MAX:
                    up(j + 1, 1 - c)
                down(j, c)
            over_blocks(pe, block_pe)


_INS = ["x", "ctx_1024", "L0_attn_kernel", "L0_xattn_ln1_g", "L0_xattn_ln1_b", "L0_xattn_ln2_g",
        "L0_xattn_ln2_b", "L0_xattn_Wq", "L0_xattn_Wkv", "L0_xattn_Wo", "L0_ffn_gate_w",
        "L0_ffn_w1", "L0_ffn_b1", "L0_ffn_w2", "L0_ffn_b2"]


def kernel(**inputs):
    import numpy as _np
    import concourse.bacc as _bacc
    from concourse import mybir as _mybir
    from concourse.bass_utils import run_bass_kernel_spmd as _run

    nc = _bacc.Bacc("TRN2", target_bir_lowering=False, num_devices=1)
    arrays, args = {}, []
    for name in _INS:
        a = _np.ascontiguousarray(inputs[name])
        arrays[f"in_{name}"] = a
        args.append(nc.dram_tensor(f"in_{name}", a.shape, _mybir.dt.from_np(a.dtype), kind="ExternalInput").ap())
    shape = inputs["x"].shape
    args.append(nc.dram_tensor("out_y", shape, _mybir.dt.float32, kind="ExternalOutput").ap())
    build(nc, *args)
    r = _run(nc, [arrays], core_ids=[0])
    return r.results[0]["out_y"]
```

```python
import concourse.bass as bass
from concourse import mybir
from contextlib import ExitStack

F32 = mybir.dt.float32
F16 = mybir.dt.float16
I32 = mybir.dt.int32
U32 = mybir.dt.uint32
ALU = mybir.AluOpType
ACT = mybir.ActivationFunctionType
AX = mybir.AxisListType

STAGES = 3
DEBUG = None


def build(nc, x_in, ctx_in, attn_w, ln1_g, ln1_b, ln2_g, ln2_b, wq_in, wkv_in, wo_in,
          gate_in, w1_in, b1_in, w2_in, b2_in, out):
    P = 128
    B, S, D = x_in.shape
    C = ctx_in.shape[1]
    NT = B * S // P
    TB = S // P
    KD = D // P
    SK = S + C
    EPS = 1e-5
    BANK = 512
    CH = 512
    NG = 4

    ARENA = 156 * 512

    es = ExitStack()
    with es:
        def sb(name, shape, dt):
            return es.enter_context(nc.sbuf_tensor(name, shape, dt))

        def sem(name):
            return es.enter_context(nc.semaphore(name))

        x = sb("x", [P, NT, D], F32)
        l_sb = sb("l_sb", [P, 2 * KD * B * SK], F16)
        lT = [l_sb[:, h * KD * B * SK:(h + 1) * KD * B * SK].rearrange("p (k b n) -> p k b n", k=KD, b=B)
              for h in range(2)]
        identf = sb("identf", [P, P], F32)
        stats = sb("stats", [P, NT, 6], F32)
        mv = sb("mv", [P, NT, 2], F32)
        veps = sb("veps", [P, NT], F32)
        rstd = sb("rstd", [P, NT], F32)
        half = sb("half", [P, NT], F32)
        arena = sb("arena", [P, ARENA], F16)
        ps = es.enter_context(nc.psum_tensor("ps", [P, 8, BANK], F32))

        cursor = [0]

        def room(shape, dt):
            n = 1
            for s in shape:
                n *= s
            size = n * (4 if dt is F32 else 2) // 2
            at = cursor[0]
            cursor[0] = at + -(-size // 16) * 16
            assert cursor[0] <= ARENA, cursor
            v = arena[:, at:at + size]
            if dt is F32:
                v = v.bitcast(F32)
            names = "abcd"[:len(shape)]
            if len(shape) > 1:
                v = v.rearrange(f"p ({' '.join(names)}) -> p {' '.join(names)}",
                                **{m: s for m, s in zip(names[1:], shape[1:])})
            return v

        E, F = b1_in.shape
        MF = F // P
        W1_F16 = KD * F
        W2_F16 = MF * D
        w1 = arena[:, 0:2 * E * W1_F16]
        w2 = arena[:, 2 * E * W1_F16:2 * E * (W1_F16 + W2_F16)]
        EARLY = E - 1
        ATTN = 28 * 1024
        cursor[0] = ATTN

        wraw = room([3, KD, D], F32)
        wa = [room([3, KD, D], F16) for _ in range(2)]
        xn = [room([D], F32) for _ in range(4)]
        qT = [room([KD, S], F16) for _ in range(2)]
        kT = [room([KD, S], F16) for _ in range(2)]
        va = [room([TB, D], F16) for _ in range(2)]
        p32 = [room([S], F32) for _ in range(2)]
        pT = [[room([TB, P], F16) for _ in range(2)] for _ in range(2)]
        negmax = room([TB], F32)
        nmax = room([TB], F32)
        den = room([TB], F32)
        rden = room([TB], F32)
        ctx_sb = room([B, D], F32)[0:C]
        cz = room([B, D], F32)[0:C]

        SELF_END = cursor[0]
        HD = 64
        HW = 2 * HD
        NP = wq_in.shape[1] // HW
        KT = TB + 1
        A_SLOTS = 2 * KT
        cursor[0] = ATTN
        wxraw = room([3, KD, HW], F32)
        woraw = room([D], F32)
        wx = [room([3, KD, HW], F16) for _ in range(2)]
        wo = [room([D], F16) for _ in range(2)]
        qn = [room([S], F16) for _ in range(2)]
        kn = [room([SK], F16) for _ in range(2)]
        qA = [[room([S], F16) for _ in range(2)] for _ in range(B)]
        kA = [[room([SK], F16) for _ in range(2)] for _ in range(B)]
        PX, PR = 3, 4
        px = [room([S], F32) for _ in range(PX)]
        pr = [[room([S], F16) for _ in range(2)] for _ in range(PR)]
        o32 = room([TB, HW], F32)
        oT = [room([TB, P], F16) for _ in range(2)]
        cursor[0] = max(cursor[0], SELF_END)
        qB = [[room([S], F16) for _ in range(2)] for _ in range(B)]
        kB = [[room([SK], F16) for _ in range(2)] for _ in range(B)]
        vh = [room([KT, 2, HD + 1], F16) for _ in range(B)]
        vl = [room([KT, 2, HD], F16) for _ in range(B)]
        pc = [room([S], F16) for _ in range(2)]
        mx3 = sb("mx3", [P, 2 * TB, 3], F32)
        m16 = sb("m16", [P, 2 * TB], F32)
        mT = sb("mT", [2 * TB, P], F16)
        rden8 = sb("rden8", [P, TB], F32)
        ROW_B1 = 4 * KD
        ROW_GATE = ROW_B1 + E * MF
        ROWS = ROW_GATE + E * KD
        rows_sb = sb("rows_sb", [ROWS, P], F32)
        cols_sb = sb("cols_sb", [P, ROWS], F32)

        def gain_shift(which, k):
            at = which * 2 * KD + k
            return dict(scale=cols_sb[:, at:at + 1], bias=cols_sb[:, at + KD:at + KD + 1])

        zn = [px[0][:, i * D:(i + 1) * D] for i in range(4)]
        t32 = [pr[i][0].rearrange("p (n) -> p n", n=S).bitcast(F32) for i in range(2)]
        cstats = sb("cstats", [C, B, 6], F32)
        cmv = sb("cmv", [C, B, 2], F32)
        cveps = sb("cveps", [C, B], F32)
        crstd = sb("crstd", [C, B], F32)
        ct32 = sb("ct32", [P, KD, B, C], F32)

        raw = [sb(f"raw{i}", [P, 2 * CH], F32) for i in range(2)]
        cursor[0] = 2 * E * (W1_F16 + W2_F16)
        xb = [room([D], F32) for _ in range(2)]
        xbT = [[room([KD, P], F16) for _ in range(2)] for _ in range(2)]
        h32 = [room([MF, P], F32) for _ in range(2)]
        hT = [[room([MF, P], F16) for _ in range(2)] for _ in range(2)]
        yb = [room([D], F32) for _ in range(2)]
        cursor[0] = 2 * E * (W1_F16 + W2_F16)
        gT = [room([KD, 2 * P], F32) for _ in range(2)]
        probs8 = room([NT, E], F32)
        ex8 = room([NT, E], F32)
        mx8 = room([NT], F32)
        sum8 = room([NT], F32)
        rec8 = room([NT], F32)
        top8 = sb("top8", [P, NT, 8], F32)
        idx8 = sb("idx8", [P, NT, 8], U32)
        idxf = room([NT, 2], F32)
        oh = [room([NT, E], F32) for _ in range(2)]
        wm = room([NT, E], F32)
        wm1 = room([NT, E], F32)
        mask = room([NT, E], F16)
        tot = room([E, NT], F32)
        inc = room([E, NT], F32)
        slotf = room([NT, E], F32)
        sl = [room([NT, E], F32) for _ in range(2)]
        sfl = room([2, NT], F32)
        nblk = room([3, E], F32)
        wmT = room([2 * P], F32)
        late_raw = raw + [room([2 * CH], F32) for _ in range(4)]
        LATE = len(late_raw)
        slot_u = sb("slot_u", [P, 2, NT], U32)
        nblk_i = sb("nblk_i", [P, 2, E], I32)
        SLOTS_MAX = NT * P * 2 // P + E - 1
        eid_f = sb("eid_f", [1, SLOTS_MAX, E], F32)
        eid_s = sb("eid_s", [1, 2, SLOTS_MAX], F32)
        eid = sb("eid", [1, SLOTS_MAX], I32)
        iota8 = sb("iota8", [P, E], F32)
        jot = sb("jot", [1, SLOTS_MAX], F32)
        upper = sb("upper", [P, P], F16)
        ones16 = sb("ones16", [P, P], F16)
        noreset = sb("noreset", [P, E, NT], F32)
        b2_sb = sb("b2_sb", [E, D], F32)
        b1cur = sb("b1cur", [P, 2, MF], F32)
        zero = sb("zero", [P, D], F32)
        xn3 = [l_sb[:, t * 2 * D:(t + 1) * 2 * D].bitcast(F32) for t in range(NT)]
        yt = [h32[i // 2].rearrange("p m n -> p (m n)")[:, i % 2 * 2 * D:(i % 2 + 1) * 2 * D].rearrange("p (a d) -> p a d", a=2) for i in range(4)]
        xg = nc.dram_tensor("xg", (SLOTS_MAX * P, D), F32, kind="Internal").ap()
        yg = nc.dram_tensor("yg", (SLOTS_MAX * P, D), F32, kind="Internal").ap()

        x_loaded = [sem(f"x_loaded_{g}") for g in range(NT // NG)]
        wa_loaded = sem("wa_loaded")
        wa_split = sem("wa_split")
        consts = sem("consts")
        consts0 = sem("consts0")
        stat_a = sem("stat_a")
        var_ready = sem("var_ready")
        rstd_ready = sem("rstd_ready")
        xn_ready = sem("xn_ready")
        xnT_filled = sem("xnT_filled")
        xnT_hi = sem("xnT_hi")
        xnT_done = sem("xnT_done")
        proj_filled = sem("proj_filled")
        proj_hi = sem("proj_hi")
        proj_done = sem("proj_done")
        a_scores = sem("a_scores")
        a_negmax = sem("a_negmax")
        a_max = sem("a_max")
        a_probs = sem("a_probs")
        a_pT = sem("a_pT")
        a_pT_hi = sem("a_pT_hi")
        a_pT_lo = sem("a_pT_lo")
        a_out = sem("a_out")
        a_rden = sem("a_rden")
        a_added = sem("a_added")
        out_done = sem("out_done")
        rows_loaded = sem("rows_loaded")
        cols_filled = sem("cols_filled")
        cols_ready = sem("cols_ready")
        ctx_loaded = sem("ctx_loaded")
        c_stat = sem("c_stat")
        c_rstd = sem("c_rstd")
        c_norm = sem("c_norm")
        c_filled = sem("c_filled")
        c_t32 = sem("c_t32")
        c_hi = sem("c_hi")
        c_done = sem("c_done")
        z_stat = sem("z_stat")
        z_var = sem("z_var")
        z_rstd = sem("z_rstd")
        z_norm = sem("z_norm")
        z_filled = sem("z_filled")
        z_t32 = sem("z_t32")
        z_hi = sem("z_hi")
        z_done = sem("z_done")
        x_consts = sem("x_consts")
        wx_loaded = sem("wx_loaded")
        wo_loaded = sem("wo_loaded")
        wx_split = sem("wx_split")
        wo_split = sem("wo_split")
        task_filled = sem("task_filled")
        task_hi = sem("task_hi")
        task_done = sem("task_done")
        m_reduced = sem("m_reduced")
        qk_spread = [sem(f"qk_spread_{i}") for i in range(3)]
        m_spread = sem("m_spread")
        scores = sem("scores")
        probs = sem("probs")
        raw_loaded = [sem(f"raw_loaded{i}") for i in range(2)]
        late_loaded = [sem(f"late_loaded{i}") for i in range(LATE)]
        raw_hi = sem("raw_hi")
        raw_split = sem("raw_split")
        late_hi = sem("late_hi")
        late_split = [sem("late_split_pool"), sem("late_split_dve")]
        f_consts0 = sem("f_consts0")
        f_consts = sem("f_consts")
        zero_set = sem("zero_set")
        xg_zeroed = sem("xg_zeroed")
        b2_loaded = sem("b2_loaded")
        g_stat = sem("g_stat")
        g_var = sem("g_var")
        g_rstd = sem("g_rstd")
        g_norm = sem("g_norm")
        g_filled = sem("g_filled")
        g_turned = sem("g_turned")
        g_logits = sem("g_logits")
        ex_ready = sem("ex_ready")
        ex_done = sem("ex_done")
        route = sem("route")
        mask_ready = sem("mask_ready")
        counted = sem("counted")
        slots_ready = sem("slots_ready")
        eid_ready = sem("eid_ready")
        wm_ready = sem("wm_ready")
        wmT_filled = sem("wmT_filled")
        wmT_ready = sem("wmT_ready")
        b2_filled = sem("b2_filled")
        b2_added = sem("b2_added")
        scattered = sem("scattered")
        xb_loaded = [sem(f"xb_loaded{i}") for i in range(2)]
        e_T = sem("e_T")
        e_T_hi = sem("e_T_hi")
        e_T_lo = sem("e_T_lo")
        e_h = sem("e_h")
        e_h32 = sem("e_h32")
        e_hT_hi = sem("e_hT_hi")
        e_hT_lo = sem("e_hT_lo")
        e_y = sem("e_y")
        e_yb = sem("e_yb")
        e_bias = sem("e_bias")
        y_stored = [sem(f"y_stored{i}") for i in range(2)]
        gathered = [sem(f"gathered{i}") for i in range(4)]
        combined = sem("combined")
        probs_hi = sem("probs_hi")
        probs_lo = sem("probs_lo")
        mixed = sem("mixed")
        o_rden = sem("o_rden")
        o_done = sem("o_done")

        LAG = 3
        AT_QKV, MAX0, AT_M, AT_FINISH = [0, 2, 3, 5, 6, 11, 12, 13], 15, 65, [15, 18, 21, 24, 27, 30]
        IT = 2 * A_SLOTS
        MC = 3
        MW = SK // MC
        PREP = ([("q", c) for c in range(2)] + [("k", c) for c in range(MC)] + [("v", i) for i in range(3)]
                + [("max", h, j, c) for h in range(2) for j in range(TB) for c in range(MC)] + [("m",)])
        FINISH = [("oT", i) for i in range(2)] + [("wo", i) for i in range(TB // 2)]
        HI_TASKS = ("q", "k", "v", "oT")

        def unit_tasks(finish, prep):
            out = []
            if prep is not None:
                at = AT_QKV + [MAX0 + n for n in range(48)] + [AT_M]
                out += [(q, (prep, *t)) for q, t in zip(at, PREP)]
            if finish is not None:
                out += [(q, (finish, *t)) for q, t in zip(AT_FINISH, FINISH)]
            return sorted(out, key=lambda w: w[0])

        def iteration_tasks(first, last):
            a = unit_tasks(None if first else 1, 1)
            b = unit_tasks(0, None if last else 0)
            return a + [(q + 4 * A_SLOTS, t) for q, t in b]

        LAST_TASK = 2 * NP * (len(PREP) + len(FINISH))

        class Iteration:

            def __init__(self, hp, first, last):
                self.hp, self.first, self.last = hp, first, last
                self.slots = hp * IT
                self.units = hp * 2
                n, f = len(PREP), len(FINISH)
                self.task0 = n if first else hp * 2 * (n + f) + n - f
                self.hi0 = 8 if first else hp * 20 + 6
                self.tasks, hi = [], 0
                for i, (q, t) in enumerate(iteration_tasks(first, last)):
                    self.tasks.append((q, t, i, hi))
                    hi += t[1] in HI_TASKS

            def of(self, slot, *quarters):
                return [w[1:] for w in self.tasks if w[0] // 4 == slot and w[0] % 4 in quarters]

            def number(self, b, *task):
                return next(i for _, t, i, _ in self.tasks if t == (b, *task)) + self.task0 + 1

            def turned(self, t):
                return self.number(t[0], "oT", 1) if t[1:] == ("wo", 0) else 0

        PROLOGUE = [((0, *t), i, min(i, 8)) for i, t in enumerate(PREP)]

        Z_BATCH = TB // 2
        Z_TASKS = 2 * Z_BATCH

        def beside_z(p):
            return PROLOGUE[2 * (p - Z_BATCH):2 * (p - Z_BATCH) + 2] if p >= Z_BATCH else []

        CONSTANTS = 11 * B

        def bank(task0, i):
            return 6 + (i + (task0 if isinstance(task0, int) else 1)) % 2

        def wait(eng, sem, value):
            if not isinstance(value, int) or value > 0:
                eng.wait_ge(sem, value)

        def lat_slot(n):
            return n // TB * KT + n % TB

        def over_pairs(eng, body):
            body(Iteration(0, True, False))
            with eng.Fori(1, NP - 1) as hp:
                body(Iteration(hp, False, False))
            body(Iteration(NP - 1, False, True))

        LEAD, STEP = 2, 4
        TURNS = (SLOTS_MAX - 2 - LEAD) // STEP

        def over_blocks(eng, body, ahead=None):
            def stretch(j, n, looped):
                extra = () if ahead is None else (ahead(j, n + 1 if looped else min(n + 1, SLOTS_MAX - j)),)
                for c in range(n):
                    body(j + c, c % 2, looped, *(() if ahead is None else (c, *extra)))
            stretch(0, LEAD, False)
            with eng.Fori(0, TURNS) as i:
                stretch(i * STEP + LEAD, STEP, True)
            stretch(LEAD + TURNS * STEP, SLOTS_MAX - LEAD - TURNS * STEP, False)

        def chunk(n):
            if n < 2 * E:
                e, k = n // 2, n % 2
                src = w1_in[e, k * P:(k + 1) * P, :]
                at = [((e * 2 + h) * KD + k) * F for h in range(2)]
                return src, [w1[:, a:a + F] for a in at]
            e, g = (n - 2 * E) // 2, n % 2
            src = w2_in[e, g * 4 * P:(g + 1) * 4 * P, :].rearrange("(m p) d -> p m d", p=P)
            at = [((e * 2 + h) * MF + g * 4) * D for h in range(2)]
            return src, [w2[:, a:a + 4 * D] for a in at]

        EARLY_CHUNKS = 2 * EARLY
        CHUNKS = 4 * E

        LATE_CHUNKS = CHUNKS - EARLY_CHUNKS
        BY_POOL = 7

        def late_done(m):
            return (late_split[0], m + 1) if m < BY_POOL else (late_split[1], m - BY_POOL + 1)

        def raw_as(n):
            r = (raw[n % 2] if n < EARLY_CHUNKS else late_raw[(n - EARLY_CHUNKS) % LATE])[:, :]
            return r if n < 2 * E else r.rearrange("p (m d) -> p m d", d=D)

        block = es.enter_context(nc.Block())
        x_v = x_in.rearrange("b (t p) d -> p (b t) d", p=P)
        out_v = out.rearrange("b (t p) d -> p (b t) d", p=P)

        @block.sync
        def _(sp):
            for g in range(NT // NG):
                sp.dma_start(x[:, g * NG:(g + 1) * NG, :], x_v[:, g * NG:(g + 1) * NG, :]).then_inc(x_loaded[g], 16)
            sp.dma_start(wraw, attn_w.rearrange("w (k p) e -> p w k e", p=P)).then_inc(wa_loaded, 16)
            for i, row in enumerate((ln1_g, ln1_b, ln2_g, ln2_b)):
                sp.dma_start(rows_sb[i * KD:(i + 1) * KD, :], row.rearrange("(k p) -> k p", p=P)).then_inc(rows_loaded, 16)
            sp.dma_start(rows_sb[ROW_B1:ROW_GATE, :], b1_in.rearrange("e (m p) -> (e m) p", p=P)).then_inc(rows_loaded, 16)
            sp.dma_start(rows_sb[ROW_GATE:ROWS, :], gate_in.rearrange("e (k p) -> (e k) p", p=P)).then_inc(rows_loaded, 16)
            sp.dma_start(ctx_sb[:, :, :], ctx_in.rearrange("b c d -> c b d")).then_inc(ctx_loaded, 16)

            wq_v = wq_in.rearrange("(k p) n -> p k n", p=P)
            wkv_v = wkv_in.rearrange("(k p) n -> p k n", p=P)

            def at_pair(hp, start=0):
                at = hp * HW + start
                return slice(at, at + HW) if isinstance(hp, int) else bass.ds(sp.snap(at), HW)

            def load_wx(hp, free):
                where = [at_pair(hp), at_pair(hp), at_pair(hp, NP * HW)]
                wait(sp, wx_split, free)
                for i, (src, cols) in enumerate(zip((wq_v, wkv_v, wkv_v), where)):
                    sp.dma_start(wxraw[:, i, :, :], src[:, :, cols]).then_inc(wx_loaded, 16)

            def load_wo(hp):
                rows = at_pair(hp)
                wait(sp, wo_split, hp * 2)
                sp.dma_start(woraw, wo_in[rows, :]).then_inc(wo_loaded, 16)

            def spread_qk(b, q_task, k_task):
                lo, hi = slice(0, HD), slice(HD, P)
                sp.wait_ge(task_done, q_task)
                for dst, src in ((qA[b][0][lo], qn[0][lo]), (qA[b][0][hi], qn[1][lo])):
                    sp.dma_start(dst, src).then_inc(qk_spread[0], 16)
                sp.wait_ge(task_done, k_task)
                for dst, src in ((kA[b][0][lo], kn[0][lo]), (kA[b][0][hi], kn[0][lo])):
                    sp.dma_start(dst, src).then_inc(qk_spread[0], 16)
                for dst, src in ((qA[b][1][lo], qn[1][hi]), (qA[b][1][hi], qn[0][hi]),
                                 (kA[b][1][lo], kn[0][hi]), (kA[b][1][hi], kn[0][hi])):
                    sp.dma_start(dst, src).then_inc(qk_spread[1], 16)
                for dst, src in ((qB[b][0][lo], qn[0][lo]), (qB[b][1][hi], qn[0][hi]),
                                 (kB[b][0][lo], kn[1][lo]), (kB[b][1][hi], kn[1][hi])):
                    sp.dma_start(dst, src).then_inc(qk_spread[2], 16)

            def spread_m(b, m_task):
                sp.wait_ge(task_done, m_task)
                for h, row in ((0, HD), (1, 0)):
                    sp.dma_start(qB[b][h][row:row + 1, :].rearrange("a (j n) -> a j n", n=P),
                                 mT[h * TB:(h + 1) * TB, :]).then_inc(m_spread, 16)

            sp.dma_start(b2_sb[:, :], b2_in).then_inc(b2_loaded, 16)
            sp.wait_ge(a_added, NT)
            load_wx(0, 0)
            sp.wait_ge(x_consts, CONSTANTS)
            spread_qk(0, 2, 5)
            spread_m(0, len(PREP))

            def pair(it):
                if not it.last:
                    load_wx(it.hp + 1, (it.hp + 1) * 2)
                load_wo(it.hp)
                spread_qk(1, it.number(1, "q", 1), it.number(1, "k", MC - 1))
                spread_m(1, it.number(1, "m"))
                if not it.last:
                    spread_qk(0, it.number(0, "q", 1), it.number(0, "k", MC - 1))
                    spread_m(0, it.number(0, "m"))

            def load_late(m):
                n = m + EARLY_CHUNKS
                if m >= LATE:
                    sp.wait_ge(*late_done(m - LATE))
                sp.dma_start(raw_as(n), chunk(n)[0]).then_inc(late_loaded[m % LATE], 16)
            sp.wait_ge(raw_split, EARLY_CHUNKS)
            for m in range(2):
                load_late(m)
            over_pairs(sp, pair)
            sp.wait_ge(task_done, LAST_TASK)
            for m in range(2, LATE_CHUNKS):
                load_late(m)
            sp.wait_ge(scattered, 2 * NT * 16)

            def rows_of(j):
                return slice(j * P, (j + 1) * P) if isinstance(j, int) else bass.ds(sp.snap(j * P), P)

            for j in range(2):
                sp.dma_start(xb[j], xg[rows_of(j), :]).then_inc(xb_loaded[j], 16)

            def load_block(j, c, looped):
                if looped or j + 2 < SLOTS_MAX:
                    rows = rows_of(j + 2)
                    sp.wait_ge(e_T, j + 1)
                    sp.dma_start(xb[c], xg[rows, :]).then_inc(xb_loaded[c], 16)
            over_blocks(sp, load_block)
            for g in range(NT // 2):
                sp.wait_ge(combined, 2 * (g * 2 + 2))
                sp.dma_start(out_v[:, g * 2:g * 2 + 2, :], x[:, g * 2:g * 2 + 2, :]).then_inc(out_done, 16)
            sp.wait_ge(out_done, NT // 2 * 16)

        def split_early(pool, n):
            pool.wait_ge(raw_loaded[n % 2], (n // 2 + 1) * 16)
            dst = [d.rearrange("p (m d) -> p m d", d=D) if n >= 2 * E else d for d in chunk(n)[1]]
            pool.tensor_copy(dst[0], raw_as(n)).then_inc(raw_hi, 1)
            pool.wait_ge(raw_hi, n + 1)
            pool.tensor_tensor(dst[1], raw_as(n), dst[0], ALU.subtract).then_inc(raw_split, 1)

        def split_late(eng, m):
            n = m + EARLY_CHUNKS
            dst = [d if n < 2 * E else d.rearrange("p (m d) -> p m d", d=D) for d in chunk(n)[1]]
            eng.wait_ge(late_hi, m + 1)
            eng.tensor_tensor(dst[1], raw_as(n), dst[0], ALU.subtract).then_inc(late_done(m)[0], 1)

        @block.gpsimd
        def _(pool):
            pool.memset(identf[:, :], 0.0).then_inc(consts0, 1)
            pool.memset(half[:, :], -0.5).then_inc(consts0, 1)
            pool.wait_ge(consts0, 2)
            pool.affine_select(out=identf[:, :], in_=identf[:, :], compare_op=ALU.not_equal, fill=1.0,
                               base=0, pattern=[[-1, P]], channel_multiplier=1).then_inc(consts, 1)
            pool.memset(zero[:, :], 0.0).then_inc(zero_set, 1)
            pool.wait_ge(zero_set, 1)
            pool.dma_start(xg.rearrange("(j p) d -> p j d", p=P), zero[:, None, :].to_broadcast([P, SLOTS_MAX, D])).then_inc(xg_zeroed, 16)
            pool.iota(iota8[:, :], pattern=[[1, E]], base=0, channel_multiplier=0,
                      allow_small_or_imprecise_dtypes=True).then_inc(f_consts, 1)
            pool.iota(jot[:, :], pattern=[[1, SLOTS_MAX]], base=0, channel_multiplier=0,
                      allow_small_or_imprecise_dtypes=True).then_inc(f_consts, 1)
            pool.memset(ones16[:, :], 1.0).then_inc(f_consts0, 1)
            pool.memset(noreset[:, :, :], 1.0).then_inc(f_consts0, 1)
            pool.wait_ge(f_consts0, 2)
            pool.memset(noreset[:, :, 0:1], 0.0).then_inc(f_consts, 1)
            pool.affine_select(out=upper[:, :], in_=ones16[:, :], compare_op=ALU.is_gt, fill=0.0,
                               base=0, pattern=[[1, P]], channel_multiplier=-1).then_inc(f_consts, 1)
            for g in range(NT // NG):
                pool.wait_ge(var_ready, g + 1)
                pool.tensor_tensor(rstd[:, g * NG:(g + 1) * NG], veps[:, g * NG:(g + 1) * NG],
                                   half[:, g * NG:(g + 1) * NG], ALU.pow).then_inc(rstd_ready, 1)

            pool.wait_ge(c_stat, 2 * B + 1)
            pool.tensor_tensor(crstd[:, :], cveps[:, :], half[0:C, 0:B], ALU.pow).then_inc(c_rstd, 1)
            for n in range(EARLY_CHUNKS):
                if n >= 2:
                    pool.wait_ge(raw_split, n - 1)
                pool.dma_start(raw_as(n), chunk(n)[0]).then_inc(raw_loaded[n % 2], 16)
                if n >= 1:
                    split_early(pool, n - 1)
            split_early(pool, EARLY_CHUNKS - 1)

            constants = []
            for b in range(B):
                for h, rows in ((0, slice(HD, P)), (1, slice(0, HD))):
                    constants += [(kB[b][h][rows], 0.0), (qB[b][h][rows], 0.0)]
                constants += [(v[HD:P, TB, :, :], 0.0) for v in (vh[b], vl[b])]
                constants.append((pc[b][HD:P], 0.0))
            for b in range(B):
                constants += [(kB[b][h][row:row + 1], -8.0) for h, row in ((0, HD), (1, 0))]
                constants.append((vh[b][:, 0:TB, :, HD:HD + 1], 1.0))
                constants.append((vh[b][0:C, TB, :, HD:HD + 1], 1.0))
            pool.wait_ge(raw_split, EARLY_CHUNKS)
            for i, (buf, value) in enumerate(constants):
                if i > 0:
                    pool.wait_ge(x_consts, i)
                pool.memset(buf, value).then_inc(x_consts, 1)

            for g in range(NT // NG):
                pool.wait_ge(z_var, g + 1)
                pool.tensor_tensor(rstd[:, g * NG:(g + 1) * NG], veps[:, g * NG:(g + 1) * NG],
                                   half[:, g * NG:(g + 1) * NG], ALU.pow).then_inc(z_rstd, 1)


            def split_low(sem, n, dst, src):
                pool.wait_ge(sem, n * 2 + 1)
                pool.tensor_tensor(dst[1], src, dst[0], ALU.subtract).then_inc(sem, 1)

            split_low(wx_split, 0, wx, wxraw)

            def low_half(it, s):
                n = it.slots + s
                head, kt = s // KT, s % KT
                rows = slice(0, P if kt < TB else C)
                if kt < TB:
                    dst = pr[(head * TB + kt) % PR]
                    wait(pool, mixed, it.slots + lat_slot(head * TB + kt - PR) + 1)
                else:
                    dst = pc
                    wait(pool, mixed, n - KT + 1)
                pool.wait_ge(probs_hi, n + 1)
                pool.tensor_tensor(dst[1][rows], px[s % PX][rows], dst[0][rows], ALU.subtract).then_inc(probs_lo, 1)

            def rstd_of(g):
                pool.wait_ge(g_var, g + 1)
                pool.tensor_tensor(rstd[:, g * NG:(g + 1) * NG], veps[:, g * NG:(g + 1) * NG],
                                   half[:, g * NG:(g + 1) * NG], ALU.pow).then_inc(g_rstd, 1)

            def pair(it):
                for s in range(IT):
                    low_half(it, s)
                    if it.last and s == A_SLOTS + 12:
                        for g in range(2):
                            rstd_of(g)
                    if s == 9 and not it.last:
                        split_low(wx_split, it.hp + 1, wx, wxraw)
                    if s == 12:
                        split_low(wo_split, it.hp, wo, woraw)
            over_pairs(pool, pair)
            for g in range(2, NT // NG):
                rstd_of(g)
            for m in range(BY_POOL):
                split_late(pool, m)
            pool.wait_ge(slots_ready, 1)
            pool.wait_ge(xg_zeroed, 16)
            for t in range(NT):
                for a in range(2):
                    pool.indirect_dma_start(out=xg[:, :], out_offset=bass.IndirectOffsetOnAxis(ap=slot_u[:, a, t:t + 1], axis=0),
                                            in_=xn3[t], in_offset=None).then_inc(scattered, 16)

            def store_block(j, c, looped):
                rows = slice(j * P, (j + 1) * P) if isinstance(j, int) else bass.ds(pool.snap(j * P), P)
                pool.wait_ge(e_yb, j + 1)
                pool.dma_start(yg[rows, :], yb[c]).then_inc(y_stored[c], 16)
            over_blocks(pool, store_block)
            pool.wait_ge(y_stored[0], (SLOTS_MAX + 1) // 2 * 16)
            pool.wait_ge(y_stored[1], SLOTS_MAX // 2 * 16)
            for t in range(NT):
                if t >= 4:
                    pool.wait_ge(combined, 2 * (t - 3))
                for a in range(2):
                    pool.indirect_dma_start(out=yt[t % 4][:, a, :], out_offset=None, in_=yg[:, :],
                                            in_offset=bass.IndirectOffsetOnAxis(ap=slot_u[:, a, t:t + 1], axis=0)).then_inc(gathered[t % 4], 16)

        PROJ = 12

        @block.scalar
        def _(act):
            def hi_of_xnT():
                for t in range(0, NT, 2):
                    act.wait_ge(xnT_filled, t // 2 + 1)
                    b, j = t // TB, t % TB
                    act.activation(lT[0][:, :, b, j * P:(j + 2) * P],
                                   ps[:, t // 2 % 2, :].rearrange("p (k n) -> p k n", k=KD),
                                   ACT.Copy).then_inc(xnT_hi, 1)
            hi_of_xnT()
            act.wait_ge(cols_filled, 1)
            act.activation(cols_sb[:, :], ps[:, 3, 0:ROWS], ACT.Copy).then_inc(cols_ready, 1)
            act.wait_ge(cols_ready, 1)
            act.wait_ge(c_filled, 1)
            for b in range(B):
                for k in range(KD):
                    act.activation(ct32[:, k, b, :], ps[:, 2, :].rearrange("p (k b n) -> p k b n", k=KD, b=B)[:, k, b, 0:C],
                                   ACT.Identity, **gain_shift(0, k)).then_inc(c_t32, 1)
            with act.Fori(0, B) as b:
                for n in range(PROJ):
                    act.wait_ge(proj_filled, b * PROJ + n + 1)
                    if n < 8:
                        dst = (qT, kT)[n // 4][0][:, n % 4 // 2, n % 2 * CH:(n % 2 + 1) * CH]
                        src = ps[:, 6 + n % 2, :]
                    else:
                        dst = va[0][:, (n - 8) * 2:(n - 8) * 2 + 2, :]
                        src = ps[:, 6 + n % 2, :].rearrange("p (j d) -> p j d", j=2)
                    act.activation(dst, src, ACT.Copy).then_inc(proj_hi, 1)

                def exp(j):
                    act.wait_ge(a_max, b * TB + j + 1)
                    if j >= 2:
                        act.wait_ge(a_pT, b * TB + j - 1)
                    act.activation(p32[j % 2], ps[:, j % 2 * 2:j % 2 * 2 + 2, :], ACT.Exp, scale=1.0 / 16,
                                   bias=nmax[:, j:j + 1], accum_out=den[:, j:j + 1]).then_inc(a_probs, 1)
                exp(0)
                exp(1)
                for j in range(TB):
                    act.wait_ge(a_pT, b * TB + j + 1)
                    if j >= 2:
                        act.wait_ge(a_out, b * TB + j - 1)
                    act.activation(pT[j % 2][0], ps[:, 4:6, :].rearrange("p a (c n) -> p (a c) n", n=P),
                                   ACT.Copy).then_inc(a_pT_hi, 1)
                    if j + 2 < TB:
                        exp(j + 2)

            def z_affine(p):
                act.wait_ge(z_filled, p + 1)
                wait(act, z_done, p - 1)
                for k in range(KD):
                    act.activation(t32[p % 2][:, k * 2 * P:(k + 1) * 2 * P], ps[:, p % 2, k * 2 * P:(k + 1) * 2 * P],
                                   ACT.Identity, **gain_shift(1, k)).then_inc(z_t32, 1)

            def task(it_task0, it_hi0, t, i, hi, units):
                b, kind = t[0], t[1]
                src = ps[:, bank(it_task0, i), :]
                if kind in HI_TASKS:
                    act.wait_ge(task_filled, it_task0 + i + 1)
                if kind == "q":
                    if t[2] == 0:
                        for spread in qk_spread:
                            wait(act, spread, units * 64)
                    act.activation(qn[0][:, t[2] * CH:(t[2] + 1) * CH], src, ACT.Copy).then_inc(task_hi, 1)
                elif kind == "k":
                    act.activation(kn[0][:, t[2] * MW:(t[2] + 1) * MW], src[:, 0:MW], ACT.Copy).then_inc(task_hi, 1)
                elif kind == "v":
                    if t[2] == 0:
                        wait(act, mixed, (units - 1) * A_SLOTS)
                    if t[2] < 2:
                        act.activation(vh[b][:, t[2] * 4:t[2] * 4 + 4, :, 0:HD],
                                       src.rearrange("p (j h d) -> p j h d", j=4, h=2), ACT.Copy).then_inc(task_hi, 1)
                    else:
                        act.activation(vh[b][0:C, TB, :, 0:HD], src[0:C, 0:HW].rearrange("p (h d) -> p h d", h=2),
                                       ACT.Copy).then_inc(task_hi, 1)
                elif kind == "oT":
                    act.activation(oT[0][:, t[2] * 4:t[2] * 4 + 4, :], src.rearrange("p (j n) -> p j n", n=P),
                                   ACT.Copy).then_inc(task_hi, 1)

            for p in range(NT // 2):
                z_affine(p)
                if p == Z_BATCH - 1:
                    act.wait_ge(wx_loaded, 48)
                    act.activation(wx[0], wxraw, ACT.Copy).then_inc(wx_split, 1)
                    act.wait_ge(x_consts, CONSTANTS)
                for t, i, hi in beside_z(p):
                    task(0, 0, t, i, hi, 0)
            for t, i, hi in PROLOGUE[Z_TASKS:]:
                task(0, 0, t, i, hi, 0)

            def probs_of(it, s):
                n = it.slots + s
                head, kt = s // KT, s % KT
                rows = slice(0, P if kt < TB else C)
                act.wait_ge(scores, n + 1)
                wait(act, probs_lo, n - PX + 1)
                act.activation(px[s % PX][rows], ps[rows, s % 2 * 2:s % 2 * 2 + 2, :], ACT.Exp,
                               scale=0.125).then_inc(probs, 1)

            def high_half(it, s):
                n = it.slots + s
                head, kt = s // KT, s % KT
                rows = slice(0, P if kt < TB else C)
                if kt < TB:
                    dst = pr[(head * TB + kt) % PR][0]
                    wait(act, mixed, it.slots + lat_slot(head * TB + kt - PR) + 1)
                else:
                    dst = pc[0]
                    wait(act, mixed, n - KT + 1)
                act.wait_ge(probs, n + 1)
                act.activation(dst[rows], px[s % PX][rows], ACT.Copy).then_inc(probs_hi, 1)

            def pair(it):
                for s in range(IT):
                    units = it.units + 1 + (s >= A_SLOTS)
                    for step, quarters in ((None, (0,)), (probs_of, (1,)), (high_half, (2, 3))):
                        if step is not None:
                            step(it, s)
                        for t, i, hi in it.of(s, *quarters):
                            task(it.task0, it.hi0, t, i, hi, units)
                    if s == 8 and not it.last:
                        act.wait_ge(wx_loaded, (it.hp + 2) * 48)
                        act.wait_ge(task_done, it.number(1, "v", 2))
                        act.activation(wx[0], wxraw, ACT.Copy).then_inc(wx_split, 1)
                    if s == 11:
                        act.wait_ge(wo_loaded, (it.hp + 1) * 16)
                        if not it.first:
                            act.wait_ge(task_done, it.number(1, "wo", TB // 2 - 1))
                        act.activation(wo[0], woraw, ACT.Copy).then_inc(wo_split, 1)
            over_pairs(act, pair)
            for i, t in enumerate(FINISH):
                task(LAST_TASK - len(FINISH), 0, (1, *t), i, 0, 2 * NP)

            act.wait_ge(task_done, LAST_TASK)

            def late_high(m):
                n = m + EARLY_CHUNKS
                act.wait_ge(late_loaded[m % LATE], (m // LATE + 1) * 16)
                dst = chunk(n)[1][0]
                act.activation(dst if n < 2 * E else dst.rearrange("p (m d) -> p m d", d=D), raw_as(n), ACT.Copy).then_inc(late_hi, 1)

            for g in range(NT // 2):
                act.wait_ge(g_filled, g + 1)
                wait(act, g_logits, 2 * (g - 1))
                act.activation(gT[g % 2], ps[:, g % 2, :].rearrange("p (k n) -> p k n", k=KD),
                               ACT.Copy).then_inc(g_turned, 1)
                if g in (3, 4):
                    late_high(g - 3)
            late_high(2)
            act.wait_ge(ex_ready, 1)
            act.activation(probs8, ex8, ACT.Exp).then_inc(ex_done, 1)
            for m in range(3, BY_POOL + LATE):
                late_high(m)
            for t in range(NT):
                act.wait_ge(wmT_filled, t + 1)
                wait(act, b2_filled, t - 1)
                act.activation(wmT[0:E, t % 2 * P:(t % 2 + 1) * P], ps[0:E, (3, 6)[t % 2], 0:P], ACT.Copy).then_inc(wmT_ready, 1)
            for m in range(BY_POOL + LATE, LATE_CHUNKS):
                late_high(m)

            def turn_hi(j, c, looped):
                act.wait_ge(e_T, j + 1)
                wait(act, e_h, j - 1)
                act.activation(xbT[c][0], ps[:, c, 0:2 * P].rearrange("p (k n) -> p k n", k=KD), ACT.Copy).then_inc(e_T_hi, 1)

            def hidden(j, c):
                act.wait_ge(e_h, j + 1)
                act.wait_ge(e_bias, j + 1)
                wait(act, e_hT_lo, j - 1)
                for m in range(MF):
                    op = act.activation(h32[c][:, m, :], ps[:, 2 + c * 2 + m // 4, m % 4 * P:(m % 4 + 1) * P], ACT.Relu,
                                        bias=b1cur[:, c, m:m + 1])
                op.then_inc(e_h32, 1)

            turn_hi(0, 0, False)
            turn_hi(1, 1, False)
            hidden(0, 0)

            def block_act(j, c, looped):
                if looped or j + 2 < SLOTS_MAX:
                    turn_hi(j + 2, c, looped)
                if looped or j + 1 < SLOTS_MAX:
                    hidden(j + 1, 1 - c)
                act.wait_ge(e_y, j + 1)
                wait(act, y_stored[c], (j - c) * 8)
                act.activation(yb[c], ps[:, 6 + c, 0:D], ACT.Copy).then_inc(e_yb, 1)
            over_blocks(act, block_act)

        @block.vector
        def _(dve):
            def ln_stats():
                for g in range(NT // NG):
                    dve.wait_ge(x_loaded[g], 16)
                    for t in range(g * NG, (g + 1) * NG):
                        dve.bn_stats(stats[:, t, :], x[:, t, :]).then_inc(stat_a, 1)
                    for t in range(g * NG, (g + 1) * NG):
                        dve.wait_ge(stat_a, g * NG * 2 + t - g * NG + 1)
                        dve.bn_aggr(mv[:, t, :], stats[:, t, :]).then_inc(stat_a, 1)
                    dve.wait_ge(stat_a, (g + 1) * NG * 2)
                    dve.tensor_scalar(veps[:, g * NG:(g + 1) * NG], mv[:, g * NG:(g + 1) * NG, 1], EPS, None,
                                      ALU.add).then_inc(var_ready, 1)
            ln_stats()
            dve.wait_ge(wa_loaded, 16)
            dve.tensor_copy(wa[0], wraw).then_inc(wa_split, 1)
            dve.wait_ge(wa_split, 1)
            dve.tensor_tensor(wa[1], wraw, wa[0], ALU.subtract).then_inc(wa_split, 1)

            def lo_of_xnT(t):
                dve.wait_ge(xnT_hi, t // 2 + 1)
                b, j = t // TB, t % TB
                dve.tensor_tensor(lT[1][:, :, b, j * P:(j + 2) * P],
                                  ps[:, t // 2 % 2, :].rearrange("p (k n) -> p k n", k=KD),
                                  lT[0][:, :, b, j * P:(j + 2) * P], ALU.subtract).then_inc(xnT_done, 1)
            for t in range(0, NT, 2):
                dve.wait_ge(rstd_ready, t // NG + 1)
                if t >= 4:
                    dve.wait_ge(xnT_filled, (t - 4) // 2 + 1)
                for u in (t, t + 1):
                    dve.tensor_scalar(xn[u % 4], x[:, u, :], mv[:, u, 0:1], rstd[:, u:u + 1],
                                      ALU.subtract, ALU.mult).then_inc(xn_ready, 1)
                if t >= 2:
                    lo_of_xnT(t - 2)
            lo_of_xnT(NT - 2)
            dve.wait_ge(ctx_loaded, 16)
            for b in range(B):
                dve.bn_stats(cstats[:, b, :], ctx_sb[:, b, :]).then_inc(c_stat, 1)
            for b in range(B):
                dve.wait_ge(c_stat, b + 1)
                dve.bn_aggr(cmv[:, b, :], cstats[:, b, :]).then_inc(c_stat, 1)
            dve.wait_ge(c_stat, 2 * B)
            dve.tensor_scalar(cveps[:, :], cmv[:, :, 1], EPS, None, ALU.add).then_inc(c_stat, 1)
            dve.wait_ge(c_rstd, 1)
            for b in range(B):
                dve.tensor_scalar(cz[:, b, :], ctx_sb[:, b, :], cmv[:, b, 0:1], crstd[:, b:b + 1],
                                  ALU.subtract, ALU.mult).then_inc(c_norm, 1)
            dve.wait_ge(c_t32, KD * B)
            dve.tensor_copy(lT[0][:, :, :, S:SK], ct32[:, :, :, :]).then_inc(c_hi, 1)
            dve.wait_ge(c_hi, 1)
            dve.tensor_tensor(lT[1][:, :, :, S:SK], ct32[:, :, :, :], lT[0][:, :, :, S:SK], ALU.subtract).then_inc(c_done, 1)
            with dve.Fori(0, B) as b:
                for n in range(PROJ):
                    dve.wait_ge(proj_hi, b * PROJ + n + 1)
                    if n < 8:
                        dst = [h[:, n % 4 // 2, n % 2 * CH:(n % 2 + 1) * CH] for h in (qT, kT)[n // 4]]
                        src = ps[:, 6 + n % 2, :]
                    else:
                        dst = [h[:, (n - 8) * 2:(n - 8) * 2 + 2, :] for h in va]
                        src = ps[:, 6 + n % 2, :].rearrange("p (j d) -> p j d", j=2)
                    dve.tensor_tensor(dst[1], src, dst[0], ALU.subtract).then_inc(proj_done, 1)

                def rowmax(j):
                    dve.wait_ge(a_scores, b * TB + j + 1)
                    dve.tensor_reduce(negmax[:, j:j + 1], ps[:, j % 2 * 2:j % 2 * 2 + 2, :], AX.XY, ALU.max,
                                      negate=True).then_inc(a_negmax, 1)
                    dve.wait_ge(a_negmax, b * TB + j + 1)
                    dve.tensor_scalar(nmax[:, j:j + 1], negmax[:, j:j + 1], 1.0 / 16, None,
                                      ALU.mult).then_inc(a_max, 1)
                rowmax(0)
                rowmax(1)
                for j in range(TB):
                    dve.wait_ge(a_pT_hi, b * TB + j + 1)
                    dve.tensor_tensor(pT[j % 2][1], ps[:, 4:6, :].rearrange("p a (c n) -> p (a c) n", n=P),
                                      pT[j % 2][0], ALU.subtract).then_inc(a_pT_lo, 1)
                    if j + 2 < TB:
                        rowmax(j + 2)
                    dve.reciprocal(rden[:, j:j + 1], den[:, j:j + 1]).then_inc(a_rden, 1)
                    dve.wait_ge(a_rden, b * TB + j + 1)
                    dve.wait_ge(a_out, b * TB + j + 1)
                    xt = x[:, bass.ds(b * TB + j, 1), :].rearrange("p a d -> p (a d)")
                    dve.scalar_tensor_tensor(out=xt, in0=ps[:, 6 + j % 2, 0:D], scalar=rden[:, j:j + 1],
                                             in1=xt, op0=ALU.mult, op1=ALU.add).then_inc(a_added, 1)

            dve.wait_ge(a_added, NT)

            def z_stats(g):
                gs = slice(g * NG, (g + 1) * NG)
                for t in range(g * NG, (g + 1) * NG):
                    dve.bn_stats(stats[:, t, :], x[:, t, :]).then_inc(z_stat, 1)
                for t in range(g * NG, (g + 1) * NG):
                    dve.wait_ge(z_stat, g * NG * 2 + t - g * NG + 1)
                    dve.bn_aggr(mv[:, t, :], stats[:, t, :]).then_inc(z_stat, 1)
                dve.wait_ge(z_stat, (g + 1) * NG * 2)
                dve.tensor_scalar(veps[:, gs], mv[:, gs, 1], 1 + EPS, EPS * EPS, ALU.mult, ALU.add).then_inc(z_var, 1)

            def z_normal(p):
                for t in (2 * p, 2 * p + 1):
                    dve.wait_ge(z_rstd, t // NG + 1)
                    wait(dve, z_filled, (t - 4) // 2 + 1)
                    dve.tensor_scalar(zn[t % 4], x[:, t, :], mv[:, t, 0:1], rstd[:, t:t + 1],
                                      ALU.subtract, ALU.mult).then_inc(z_norm, 1)

            def z_halves(p):
                b, j = 2 * p // TB, 2 * p % TB
                src = t32[p % 2].rearrange("p (k n) -> p k n", k=KD)
                dst = [lT[h][:, :, b, j * P:(j + 2) * P] for h in range(2)]
                dve.wait_ge(z_t32, 2 * p + 2)
                dve.tensor_copy(dst[0], src).then_inc(z_hi, 1)
                dve.wait_ge(z_hi, p + 1)
                dve.tensor_tensor(dst[1], src, dst[0], ALU.subtract).then_inc(z_done, 1)

            def task(it_task0, it_hi0, t, i, hi, units):
                b, kind = t[0], t[1]
                src = ps[:, bank(it_task0, i), :]
                if kind in HI_TASKS:
                    dve.wait_ge(task_hi, it_hi0 + hi + 1)
                else:
                    dve.wait_ge(task_filled, it_task0 + i + 1)
                if kind == "q":
                    cols = slice(t[2] * CH, (t[2] + 1) * CH)
                    op = dve.tensor_tensor(qn[1][:, cols], src, qn[0][:, cols], ALU.subtract)
                elif kind == "k":
                    cols = slice(t[2] * MW, (t[2] + 1) * MW)
                    op = dve.tensor_tensor(kn[1][:, cols], src[:, 0:MW], kn[0][:, cols], ALU.subtract)
                elif kind == "v" and t[2] < 2:
                    js = slice(t[2] * 4, t[2] * 4 + 4)
                    op = dve.tensor_tensor(vl[b][:, js, :, :], src.rearrange("p (j h d) -> p j h d", j=4, h=2),
                                           vh[b][:, js, :, 0:HD], ALU.subtract)
                elif kind == "v":
                    op = dve.tensor_tensor(vl[b][0:C, TB, :, :], src[0:C, 0:HW].rearrange("p (h d) -> p h d", h=2),
                                           vh[b][0:C, TB, :, 0:HD], ALU.subtract)
                elif kind == "oT":
                    js = slice(t[2] * 4, t[2] * 4 + 4)
                    op = dve.tensor_tensor(oT[1][:, js, :], src.rearrange("p (j n) -> p j n", n=P),
                                           oT[0][:, js, :], ALU.subtract)
                elif kind == "max":
                    _, _, h, j, c = t
                    op = dve.tensor_reduce(mx3[:, h * TB + j, c:c + 1], src[:, 0:MW], AX.X, ALU.max)
                elif kind == "m":
                    wait(dve, m_spread, units * 32)
                    op = dve.tensor_scalar(mT[:, :], src[0:2 * TB, 0:P], 0.125, None, ALU.mult)
                elif kind == "wo":
                    xt = x[:, b * TB + t[2] * 2:b * TB + t[2] * 2 + 2, :]
                    op = dve.tensor_tensor(xt, src.rearrange("p (a d) -> p a d", a=2), xt, ALU.add)
                op.then_inc(task_done, 1)
                if kind == "max" and t[2:] == (1, TB - 1, MC - 1):
                    dve.wait_ge(task_done, it_task0 + i + 1)
                    dve.tensor_reduce(m16[:, :], mx3[:, :, :], AX.X, ALU.max).then_inc(m_reduced, 1)

            def head_out(it, head):
                n = it.units * 2 + head
                dve.wait_ge(mixed, it.slots + (head + 1) * KT)
                acc = ps[:, 4:6, 0:4 * (HD + 1)].rearrange("p a (j d) -> p a j d", d=HD + 1)
                dve.reciprocal(rden8[:, :].rearrange("p (a j) -> p a j", a=2), acc[:, :, :, HD]).then_inc(o_rden, 1)
                dve.wait_ge(o_rden, n + 1)
                for a in range(2):
                    dve.tensor_tensor(o32[:, a * 4:a * 4 + 4, head % 2 * HD:(head % 2 + 1) * HD], acc[:, a, :, 0:HD],
                                      rden8[:, a * 4:a * 4 + 4, None].to_broadcast([P, 4, HD]), ALU.mult).then_inc(o_done, 1)

            z_stats(0)
            z_stats(1)
            for p in range(NT // 2):
                z_normal(p)
                if p >= 1:
                    z_halves(p - 1)
                if p in (1, 2):
                    z_stats(p + 1)
                for t, i, hi in beside_z(p):
                    task(0, 0, t, i, hi, 0)
            z_halves(NT // 2 - 1)
            for t, i, hi in PROLOGUE[Z_TASKS:]:
                task(0, 0, t, i, hi, 0)

            def g_stats(g):
                tiles = range(g * NG, (g + 1) * NG)
                gs = slice(g * NG, (g + 1) * NG)
                for t in tiles:
                    dve.bn_stats(stats[:, t, :], x[:, t, :]).then_inc(g_stat, 1)
                for t in tiles:
                    dve.wait_ge(g_stat, g * NG * 2 + t - g * NG + 1)
                    dve.bn_aggr(mv[:, t, :], stats[:, t, :]).then_inc(g_stat, 1)
                dve.wait_ge(g_stat, (g + 1) * NG * 2)
                dve.tensor_scalar(veps[:, gs], mv[:, gs, 1], EPS, None, ALU.add).then_inc(g_var, 1)

            def g_normal(t):
                dve.wait_ge(g_rstd, t // NG + 1)
                dve.tensor_scalar(xn3[t], x[:, t, :], mv[:, t, 0:1], rstd[:, t:t + 1],
                                  ALU.subtract, ALU.mult).then_inc(g_norm, 1)

            def pair(it):
                for s in range(IT):
                    if it.last and s == A_SLOTS + 10:
                        dve.wait_ge(task_done, it.number(0, "wo", TB // 2 - 1))
                        for g in range(2):
                            g_stats(g)
                    if it.last and s == A_SLOTS + 14:
                        for t in range(NT // 2):
                            g_normal(t)
                    units = it.units + 1 + (s >= A_SLOTS)
                    for quarter in range(4):
                        if quarter == 3:
                            for head in range(4):
                                if s == head * KT + KT + LAG - 1:
                                    head_out(it, head)
                            if s == LAG - 1 and not it.first:
                                head_out(Iteration(it.hp - 1, False, False), 3)
                        for t, i, hi in it.of(s, quarter):
                            task(it.task0, it.hi0, t, i, hi, units)
            over_pairs(dve, pair)
            head_out(Iteration(NP - 1, False, True), 3)
            for i, t in enumerate(FINISH):
                task(LAST_TASK - len(FINISH), 20 * NP - 2, (1, *t), i, i, 2 * NP)

            dve.wait_ge(task_done, LAST_TASK)
            for g in range(2, NT // NG):
                g_stats(g)
            for t in range(NT // 2, NT):
                g_normal(t)

            step = [0]

            def then(ins):
                step[0] += 1
                ins.then_inc(route, 1)
                dve.wait_ge(route, step[0])

            dve.wait_ge(g_logits, NT)
            lg = ps[:, 2, 0:NT * E].rearrange("p (t e) -> p t e", e=E)
            along_e = lambda v: v[:, :, None].to_broadcast([P, NT, E])
            then(dve.tensor_reduce(mx8, lg, AX.X, ALU.max))
            dve.tensor_tensor(ex8, lg, along_e(mx8), ALU.subtract).then_inc(ex_ready, 1)
            dve.wait_ge(ex_done, 1)
            then(dve.tensor_reduce(sum8, probs8, AX.X, ALU.add))
            then(dve.reciprocal(rec8, sum8))
            then(dve.tensor_tensor(ex8, probs8, along_e(rec8), ALU.mult))
            for t in range(NT):
                ins = dve.max(top8[:, t, :], ex8[:, t, :])
            then(ins)
            for t in range(NT):
                ins = dve.max_index(out=idx8[:, t, :], in_max=top8[:, t, :], in_values=ex8[:, t, :])
            then(ins)
            then(dve.tensor_copy(idxf, idx8[:, :, 0:2]))
            dve.wait_ge(f_consts, 4)
            for a in range(2):
                then(dve.tensor_tensor(oh[a], iota8[:, None, :].to_broadcast([P, NT, E]), along_e(idxf[:, :, a]), ALU.is_equal))
            dve.tensor_tensor(mask, oh[0], oh[1], ALU.add).then_inc(mask_ready, 1)
            then(dve.tensor_tensor(wm, oh[0], along_e(top8[:, :, 0]), ALU.mult))
            then(dve.tensor_tensor(wm1, oh[1], along_e(top8[:, :, 1]), ALU.mult))
            dve.tensor_tensor(wm, wm, wm1, ALU.add).then_inc(wm_ready, 1)
            dve.wait_ge(counted, 1)
            before = ps[:, 0, 0:NT * E].rearrange("p (t e) -> p t e", e=E)
            total = ps[:, 0, NT * E:2 * NT * E].rearrange("p (t e) -> p e t", e=E)
            then(dve.tensor_copy(tot, total))
            flat = lambda v: v.rearrange("p e t -> p (e t)")
            then(dve.tensor_tensor_scan(flat(inc), flat(noreset[:, :, :]), flat(tot), 0.0, ALU.mult, ALU.add))
            then(dve.tensor_scalar(nblk_i[:, 0, :], inc[:, :, NT - 1], float(P - 1), None, ALU.add))
            then(dve.tensor_scalar(nblk_i[:, 1, :], nblk_i[:, 0, :], 7, None, ALU.arith_shift_right))
            then(dve.tensor_copy(nblk[:, 0, :], nblk_i[:, 1, :]))
            then(dve.tensor_tensor_scan(nblk[:, 1, :], noreset[:, 0:1, 1:1 + E].rearrange("p a e -> p (a e)"), nblk[:, 0, :], 0.0, ALU.mult, ALU.add))
            then(dve.tensor_tensor(nblk[:, 2, :], nblk[:, 1, :], nblk[:, 0, :], ALU.subtract))
            then(dve.tensor_scalar(nblk[:, 2, :], nblk[:, 2, :], float(P), None, ALU.mult))
            then(dve.tensor_tensor(inc, inc, tot, ALU.subtract))
            then(dve.tensor_tensor(inc, inc, nblk[:, 2, :][:, :, None].to_broadcast([P, E, NT]), ALU.add))
            then(dve.tensor_tensor(slotf, before, inc.rearrange("p e t -> p t e"), ALU.add))
            for a in range(2):
                then(dve.tensor_tensor(sl[a], oh[a], slotf, ALU.mult))
                then(dve.tensor_reduce(sfl[:, a, :], sl[a], AX.X, ALU.add))
            dve.tensor_copy(slot_u[:, :, :], sfl).then_inc(slots_ready, 1)
            then(dve.tensor_tensor(eid_f[:, :, :], jot[:, :, None].to_broadcast([1, SLOTS_MAX, E]),
                                   nblk[0:1, 1, :][:, None, :].to_broadcast([1, SLOTS_MAX, E]), ALU.is_ge))
            then(dve.tensor_reduce(eid_s[:, 0, :], eid_f[:, :, :], AX.X, ALU.add))
            then(dve.tensor_scalar(eid[:, :], eid_s[:, 0, :], float(E - 1), None, ALU.min))
            dve.memset(eid_s[:, 1, :], 0.0).then_inc(eid_ready, 1)
            for m in range(BY_POOL, BY_POOL + LATE):
                split_late(dve, m)
            for t in range(0, NT, 2):
                dve.wait_ge(b2_filled, t + 2)
                dve.tensor_tensor(x[:, t:t + 2, :], ps[:, 4 + t // 2 % 2, :].rearrange("p (a d) -> p a d", a=2),
                                  x[:, t:t + 2, :], ALU.add).then_inc(b2_added, 1)
            for m in range(BY_POOL + LATE, LATE_CHUNKS):
                split_late(dve, m)

            def turn_lo(j, c):
                dve.wait_ge(e_T_hi, j + 1)
                dve.tensor_tensor(xbT[c][1], ps[:, c, 0:2 * P].rearrange("p (k n) -> p k n", k=KD), xbT[c][0],
                                  ALU.subtract).then_inc(e_T_lo, 1)

            def bias(j, c):
                wait(dve, e_h32, j - 1)
                e = dve.value_load(eid[0:1, j:j + 1] if isinstance(j, int) else eid[0:1, bass.ds(j, 1)], min_val=0, max_val=E - 1)
                dve.tensor_copy(b1cur[:, c, :], cols_sb[:, bass.ds(e * MF + ROW_B1, MF)]).then_inc(e_bias, 1)

            def split_hidden(j, c):
                dve.wait_ge(e_h32, j + 1)
                wait(dve, e_y, j - 1)
                dve.tensor_copy(hT[c][0], h32[c]).then_inc(e_hT_hi, 1)
                dve.wait_ge(e_hT_hi, j + 1)
                dve.tensor_tensor(hT[c][1], h32[c], hT[c][0], ALU.subtract).then_inc(e_hT_lo, 1)

            turn_lo(0, 0)
            bias(0, 0)
            turn_lo(1, 1)
            split_hidden(0, 0)

            def block_dve(j, c, looped):
                if looped or j + 1 < SLOTS_MAX:
                    bias(j + 1, 1 - c)
                if looped or j + 2 < SLOTS_MAX:
                    turn_lo(j + 2, c)
                if looped or j + 1 < SLOTS_MAX:
                    split_hidden(j + 1, 1 - c)
            over_blocks(dve, block_dve)
            for t in range(NT):
                dve.wait_ge(gathered[t % 4], (t // 4 + 1) * 32)
                for a in range(2):
                    if a == 1:
                        dve.wait_ge(combined, 2 * t + 1)
                    dve.scalar_tensor_tensor(out=x[:, t, :], in0=yt[t % 4][:, a, :], scalar=top8[:, t, a:a + 1],
                                             in1=x[:, t, :], op0=ALU.mult, op1=ALU.add).then_inc(combined, 1)

        @block.tensor
        def _(pe):
            pe.wait_ge(consts, 1)
            for t in range(0, NT, 2):
                pe.wait_ge(xn_ready, t + 2)
                if t >= 4:
                    pe.wait_ge(xnT_done, (t - 4) // 2 + 1)
                for k in range(KD):
                    for u in (t, t + 1):
                        mm = pe.transpose(ps[:, t // 2 % 2, k * 2 * P + u % 2 * P:k * 2 * P + u % 2 * P + P],
                                          xn[u % 4][:, k * P:(k + 1) * P], identf[:, :])
                mm.then_inc(xnT_filled, 1)
            pe.wait_ge(xnT_done, NT // 2)
            pe.wait_ge(rows_loaded, 6 * 16)
            pe.transpose(ps[:, 3, 0:ROWS], rows_sb[:, :], identf[0:ROWS, 0:ROWS]).then_inc(cols_filled, 1)
            pe.wait_ge(c_norm, B)
            for b in range(B):
                for k in range(KD):
                    mm = pe.transpose(ps[:, 2, :].rearrange("p (k b n) -> p k b n", k=KD, b=B)[:, k, b, 0:C],
                                      cz[:, b, k * P:(k + 1) * P], identf[0:C, 0:C])
            mm.then_inc(c_filled, 1)
            pe.wait_ge(wa_split, 2)
            EXACT = ((0, 0), (1, 0), (0, 1))

            with pe.Fori(0, B) as b:
                def tokens(half, k, at, n):
                    return lT[half][:, k, bass.ds(b, 1), at:at + n].rearrange("p a n -> p (a n)")
                for n in range(PROJ):
                    if n >= 2:
                        pe.wait_ge(proj_done, b * PROJ + n - 1)
                    if n < 8:
                        w, m, c = (1, 0)[n // 4], n % 4 // 2, n % 2
                        parts = [(h, k) for h in EXACT for k in range(KD)]
                        for i, ((hw, hx), k) in enumerate(parts):
                            mm = pe.matmul(ps[:, 6 + n % 2, :], wa[hw][:, w, k, m * P:(m + 1) * P],
                                           tokens(hx, k, c * CH, CH), start=(i == 0), stop=(i == len(parts) - 1))
                    else:
                        for j in range(2):
                            parts = [(h, k) for h in EXACT for k in range(KD)]
                            for i, ((hx, hw), k) in enumerate(parts):
                                mm = pe.matmul(ps[:, 6 + n % 2, j * D:(j + 1) * D],
                                               tokens(hx, k, ((n - 8) * 2 + j) * P, P), wa[hw][:, 2, k, :],
                                               start=(i == 0), stop=(i == len(parts) - 1))
                    mm.then_inc(proj_filled, 1)

                def self_scores(j):
                    if j < 2:
                        pe.wait_ge(proj_done, b * PROJ + 8)
                    else:
                        pe.wait_ge(a_probs, b * TB + j - 1)
                    for c in range(S // CH):
                        parts = [(h, k) for h in EXACT for k in range(KD)]
                        for i, ((hq, hk), k) in enumerate(parts):
                            mm = pe.matmul(ps[:, j % 2 * 2 + c, :], qT[hq][:, k, j * P:(j + 1) * P],
                                           kT[hk][:, k, c * CH:(c + 1) * CH],
                                           start=(i == 0), stop=(i == len(parts) - 1))
                    mm.then_inc(a_scores, 1)
                self_scores(0)
                self_scores(1)
                for j in range(TB):
                    pe.wait_ge(a_probs, b * TB + j + 1)
                    if j > 0:
                        pe.wait_ge(a_pT_lo, b * TB + j)
                    for c in range(TB):
                        mm = pe.transpose(ps[:, 4 + c // 4, c % 4 * P:(c % 4 + 1) * P],
                                          p32[j % 2][:, c * P:(c + 1) * P], identf[:, :])
                    mm.then_inc(a_pT, 1)
                    if j + 2 < TB:
                        self_scores(j + 2)
                    pe.wait_ge(a_pT_lo, b * TB + j + 1)
                    if j < 2:
                        pe.wait_ge(proj_done, (b + 1) * PROJ)
                    else:
                        pe.wait_ge(a_added, b * TB + j - 1)
                    parts = [(h, c) for c in range(TB) for h in EXACT]
                    for i, ((hp, hv), c) in enumerate(parts):
                        mm = pe.matmul(ps[:, 6 + j % 2, 0:D], pT[j % 2][hp][:, c, :], va[hv][:, c, :],
                                       start=(i == 0), stop=(i == len(parts) - 1))
                    mm.then_inc(a_out, 1)
                pe.wait_ge(a_added, (b + 1) * TB)

            def product(dst, pairs):
                for i, (stationary, moving) in enumerate(pairs):
                    mm = pe.matmul(dst, stationary, moving, start=(i == 0), stop=(i == len(pairs) - 1))
                return mm

            def task(it_task0, t, i, units, turned=0):
                b, kind = t[0], t[1]
                dst = ps[:, bank(it_task0, i), :]
                wait(pe, task_done, it_task0 + i - 1)
                if kind == "q":
                    if t[2] == 0:
                        pe.wait_ge(wx_split, (units // 2 + 1) * 2)
                    cols = slice(t[2] * CH, (t[2] + 1) * CH)
                    mm = product(dst, [(wx[hw][:, 0, k, :], lT[hx][:, k, b, cols])
                                       for hw, hx in EXACT for k in range(KD)])
                elif kind == "k":
                    cols = slice(t[2] * MW, (t[2] + 1) * MW)
                    mm = product(dst[:, 0:MW], [(wx[hw][:, 1, k, :], lT[hx][:, k, b, cols])
                                                for hw, hx in EXACT for k in range(KD)])
                elif kind == "v":
                    for j in range(4 if t[2] < 2 else 1):
                        at = (t[2] * 4 + j) * P
                        n = min(P, SK - at)
                        mm = product(dst[0:n, j * HW:(j + 1) * HW],
                                     [(lT[hx][:, k, b, at:at + n], wx[hw][:, 2, k, :])
                                      for hx, hw in EXACT for k in range(KD)])
                elif kind == "max":
                    _, _, h, j, c = t
                    if (j, c) == (0, 0):
                        pe.wait_ge(qk_spread[h], (units + 1) * 64)
                    mm = pe.matmul(dst[:, 0:MW], qA[b][h][:, j * P:(j + 1) * P], kA[b][h][:, c * MW:(c + 1) * MW],
                                   start=True, stop=True)
                elif kind == "m":
                    pe.wait_ge(m_reduced, units + 1)
                    mm = pe.transpose(dst[0:2 * TB, 0:P], m16[:, :], identf[:, :])
                elif kind == "oT":
                    if t[2] == 0:
                        pe.wait_ge(o_done, (units - 1) * 4)
                    for j in range(4):
                        mm = pe.transpose(dst[:, j * P:(j + 1) * P], o32[:, t[2] * 4 + j, :], identf[:, :])
                elif kind == "wo":
                    if t[2] == 0:
                        pe.wait_ge(wo_split, units // 2 * 2)
                        pe.wait_ge(task_done, turned)
                    for j in range(2):
                        mm = product(dst[:, j * D:(j + 1) * D], [(oT[ho][:, t[2] * 2 + j, :], wo[hw])
                                                                for ho, hw in EXACT])
                mm.then_inc(task_filled, 1)

            for p in range(NT // 2):
                pe.wait_ge(z_norm, 2 * p + 2)
                wait(pe, z_t32, 2 * p - 2)
                for k in range(KD):
                    for u in (2 * p, 2 * p + 1):
                        mm = pe.transpose(ps[:, p % 2, k * 2 * P + u % 2 * P:k * 2 * P + u % 2 * P + P],
                                          zn[u % 4][:, k * P:(k + 1) * P], identf[:, :])
                mm.then_inc(z_filled, 1)
                if p == Z_BATCH:
                    pe.wait_ge(z_done, Z_BATCH)
                    pe.wait_ge(c_done, 1)
                for t, i, _ in beside_z(p):
                    task(0, t, i, 0)
            pe.wait_ge(z_done, NT // 2)
            for t, i, _ in PROLOGUE[Z_TASKS:]:
                task(0, t, i, 0)

            def score(it, s, c):
                n = it.slots + s
                b, head, kt = s // A_SLOTS, s // KT % 2, s % KT
                if s % A_SLOTS == 0 and c == 0:
                    pe.wait_ge(qk_spread[2], (it.units + b + 1) * 64)
                    pe.wait_ge(m_spread, (it.units + b + 1) * 32)
                if c == 0:
                    wait(pe, probs, n - 1)
                keys = slice(kt * P, min((kt + 1) * P, SK))
                rows = slice(0, keys.stop - keys.start)
                cols = slice(c * CH, (c + 1) * CH)
                mm = product(ps[rows, s % 2 * 2 + c, :], [(kA[b][head][:, keys], qA[b][head][:, cols]),
                                                          (kB[b][head][:, keys], qB[b][head][:, cols])])
                if c == S // CH - 1:
                    mm.then_inc(scores, 1)

            def mix(it, s, a):
                n = it.slots + s
                b, head, kt = s // A_SLOTS, s // KT, s % KT
                if a == 0:
                    pe.wait_ge(probs_lo, n + 1)
                if kt == 0 and a == 0:
                    wait(pe, o_done, (it.units * 2 + head) * 2)
                p = pr[(head * TB + kt) % PR] if kt < TB else pc
                for j in range(a * 4, a * 4 + 4):
                    dst = ps[:, 4 + j // 4, j % 4 * (HD + 1):(j % 4 + 1) * (HD + 1)]
                    cols = slice(j * P, (j + 1) * P)
                    last = kt == KT - 1
                    pe.matmul(dst, p[0][:, cols], vh[b][:, kt, head % 2, :], start=(kt == 0 and j % 4 == 0),
                              stop=False, skip_group_check=True)
                    pe.matmul(dst[:, 0:HD], p[0][:, cols], vl[b][:, kt, head % 2, :], start=False,
                              stop=False, skip_group_check=True)
                    mm = pe.matmul(dst, p[1][:, cols], vh[b][:, kt, head % 2, :], start=False,
                                   stop=last, skip_group_check=True)
                if a == 1:
                    mm.then_inc(mixed, 1)

            def pair(it):
                for s in range(IT):
                    units = it.units + 1 + (s >= A_SLOTS)
                    for quarter in range(4):
                        if quarter < 2:
                            score(it, s, quarter)
                        elif s >= LAG:
                            mix(it, s - LAG, quarter - 2)
                        elif not it.first:
                            mix(Iteration(it.hp - 1, False, False), s - LAG + IT, quarter - 2)
                        for t, i, _ in it.of(s, quarter):
                            task(it.task0, t, i, units, it.turned(t))
            over_pairs(pe, pair)
            for s in range(IT - LAG, IT):
                for a in range(2):
                    mix(Iteration(NP - 1, False, True), s, a)
            for i, t in enumerate(FINISH):
                task(LAST_TASK - len(FINISH), (1, *t), i, 2 * NP + 1, LAST_TASK - len(FINISH) + 2)

            pe.wait_ge(task_done, LAST_TASK)

            def logits(g):
                pe.wait_ge(g_turned, g + 1)
                for u in range(2):
                    t = g * 2 + u
                    product(ps[:, 2, t * E:(t + 1) * E],
                            [(gT[g % 2][:, k, u * P:(u + 1) * P],
                              cols_sb[:, ROW_GATE:ROWS].rearrange("p (e k) -> p k e", k=KD)[:, k, :])
                             for k in range(KD)]).then_inc(g_logits, 1)
            for g in range(NT // 2):
                pe.wait_ge(g_norm, 2 * g + 2)
                wait(pe, g_turned, g - 1)
                for k in range(KD):
                    for u in range(2):
                        mm = pe.transpose(ps[:, g % 2, (k * 2 + u) * P:(k * 2 + u + 1) * P],
                                          xn3[g * 2 + u][:, k * P:(k + 1) * P], identf[:, :])
                mm.then_inc(g_filled, 1)
                if g >= 1:
                    logits(g - 1)
            logits(NT // 2 - 1)
            pe.wait_ge(mask_ready, 1)
            m2 = mask.rearrange("p t e -> p (t e)")
            pe.matmul(ps[:, 0, 0:NT * E], upper[:, :], m2, start=True, stop=True)
            pe.matmul(ps[:, 0, NT * E:2 * NT * E], ones16[:, :], m2, start=True, stop=True).then_inc(counted, 1)
            pe.wait_ge(wm_ready, 1)
            pe.wait_ge(b2_loaded, 16)

            def second_bias(t):
                pe.wait_ge(wmT_ready, t + 1)
                if t % 2 == 0:
                    wait(pe, b2_added, t // 2 - 1)
                pe.matmul(ps[:, 4 + t // 2 % 2, t % 2 * D:(t % 2 + 1) * D], wmT[0:E, t % 2 * P:(t % 2 + 1) * P], b2_sb[:, :],
                          start=True, stop=True).then_inc(b2_filled, 1)
            for t in range(NT):
                wait(pe, wmT_ready, t - 1)
                pe.transpose(ps[0:E, (3, 6)[t % 2], 0:P], wm[:, t, :], identf[:, :]).then_inc(wmT_filled, 1)
                if t >= 1:
                    second_bias(t - 1)
            second_bias(NT - 1)
            pe.wait_ge(b2_added, NT // 2)
            pe.wait_ge(eid_ready, 1)

            def turn(j, c):
                pe.wait_ge(xb_loaded[c], (j - c) * 8 + 16)
                wait(pe, e_T_lo, j - 1)
                for k in range(KD):
                    mm = pe.transpose(ps[:, c, k * P:(k + 1) * P], xb[c][:, k * P:(k + 1) * P], identf[:, :])
                mm.then_inc(e_T, 1)

            def expert_of(j):
                return pe.value_load(eid[0:1, j:j + 1] if isinstance(j, int) else eid[0:1, bass.ds(j, 1)], min_val=0, max_val=E - 1)

            def up(j, c, e):
                mine = w1[:, bass.ds(e * (2 * W1_F16), 2 * W1_F16)]
                pe.wait_ge(e_T_lo, j + 1)
                wait(pe, e_h32, j - 1)
                for m in range(MF):
                    mm = product(ps[:, 2 + c * 2 + m // 4, m % 4 * P:(m % 4 + 1) * P],
                                 [(mine[:, (hw * KD + k) * F + m * P:(hw * KD + k) * F + (m + 1) * P], xbT[c][hx][:, k, :])
                                  for hw, hx in EXACT for k in range(KD)])
                mm.then_inc(e_h, 1)

            def down(j, c, e):
                mine = w2[:, bass.ds(e * (2 * W2_F16), 2 * W2_F16)]
                pe.wait_ge(e_hT_lo, j + 1)
                wait(pe, e_yb, j - 1)
                product(ps[:, 6 + c, 0:D],
                        [(hT[c][hh][:, m, :], mine[:, (hw * MF + m) * D:(hw * MF + m + 1) * D])
                         for m in range(MF) for hh, hw in EXACT]).then_inc(e_y, 1)

            for m in (BY_POOL - 1, LATE_CHUNKS - 1):
                pe.wait_ge(*late_done(m))
            pe.wait_ge(raw_split, EARLY_CHUNKS)
            turn(0, 0)
            turn(1, 1)
            up(0, 0, expert_of(0))

            def block_pe(j, c, looped, n, experts):
                if looped or j + 2 < SLOTS_MAX:
                    turn(j + 2, c)
                if looped or j + 1 < SLOTS_MAX:
                    up(j + 1, 1 - c, experts[n + 1])
                down(j, c, experts[n])
            over_blocks(pe, block_pe, lambda j, n: [expert_of(j + i) for i in range(n)])


_INS = ["x", "ctx_1024", "L0_attn_kernel", "L0_xattn_ln1_g", "L0_xattn_ln1_b", "L0_xattn_ln2_g",
        "L0_xattn_ln2_b", "L0_xattn_Wq", "L0_xattn_Wkv", "L0_xattn_Wo", "L0_ffn_gate_w",
        "L0_ffn_w1", "L0_ffn_b1", "L0_ffn_w2", "L0_ffn_b2"]


def kernel(**inputs):
    import numpy as _np
    import concourse.bacc as _bacc
    from concourse import mybir as _mybir
    from concourse.bass_utils import run_bass_kernel_spmd as _run

    nc = _bacc.Bacc("TRN2", target_bir_lowering=False, num_devices=1)
    arrays, args = {}, []
    for name in _INS:
        a = _np.ascontiguousarray(inputs[name])
        arrays[f"in_{name}"] = a
        args.append(nc.dram_tensor(f"in_{name}", a.shape, _mybir.dt.from_np(a.dtype), kind="ExternalInput").ap())
    shape = inputs["x"].shape
    args.append(nc.dram_tensor("out_y", shape, _mybir.dt.float32, kind="ExternalOutput").ap())
    build(nc, *args)
    r = _run(nc, [arrays], core_ids=[0])
    return r.results[0]["out_y"]
```

```python
import concourse.bass as bass
from concourse import mybir
from contextlib import ExitStack

F32 = mybir.dt.float32
F16 = mybir.dt.float16
I32 = mybir.dt.int32
U32 = mybir.dt.uint32
ALU = mybir.AluOpType
ACT = mybir.ActivationFunctionType
AX = mybir.AxisListType


def build(nc, x_in, ctx_in, attn_w, ln1_g, ln1_b, ln2_g, ln2_b, wq_in, wkv_in, wo_in,
          gate_in, w1_in, b1_in, w2_in, b2_in, out):
    P = 128
    B, S, D = x_in.shape
    C = ctx_in.shape[1]
    NT = B * S // P
    TB = S // P
    KD = D // P
    SK = S + C
    EPS = 1e-5
    BANK = 512
    CH = 512
    NG = 4
    NR = 4

    ARENA = 156 * 512

    es = ExitStack()
    with es:
        def sb(name, shape, dt):
            return es.enter_context(nc.sbuf_tensor(name, shape, dt))

        def sem(name):
            return es.enter_context(nc.semaphore(name))

        x = sb("x", [P, NT, D], F32)
        l_sb = sb("l_sb", [P, 2 * KD * B * SK], F16)
        lT = [l_sb[:, h * KD * B * SK:(h + 1) * KD * B * SK].rearrange("p (k b n) -> p k b n", k=KD, b=B)
              for h in range(2)]
        identf = sb("identf", [P, P], F32)
        stats = sb("stats", [P, NT, 6], F32)
        mv = sb("mv", [P, NT, 2], F32)
        veps = sb("veps", [P, NT], F32)
        rstd = sb("rstd", [P, NT], F32)
        half = sb("half", [P, NT], F32)
        arena = sb("arena", [P, ARENA], F16)
        ps = es.enter_context(nc.psum_tensor("ps", [P, 8, BANK], F32))

        cursor = [0]

        def room(shape, dt):
            n = 1
            for s in shape:
                n *= s
            size = n * (4 if dt is F32 else 2) // 2
            at = cursor[0]
            cursor[0] = at + -(-size // 16) * 16
            assert cursor[0] <= ARENA, cursor
            v = arena[:, at:at + size]
            if dt is F32:
                v = v.bitcast(F32)
            names = "abcd"[:len(shape)]
            if len(shape) > 1:
                v = v.rearrange(f"p ({' '.join(names)}) -> p {' '.join(names)}",
                                **{m: s for m, s in zip(names[1:], shape[1:])})
            return v

        E, F = b1_in.shape
        MF = F // P
        W1_F16 = KD * F
        W2_F16 = MF * D
        w1 = arena[:, 0:2 * E * W1_F16]
        w2 = arena[:, 2 * E * W1_F16:2 * E * (W1_F16 + W2_F16)]
        EARLY = E - 1
        ATTN = 28 * 1024
        cursor[0] = ATTN

        wraw = room([3, KD, D], F32)
        wa = [room([3, KD, D], F16) for _ in range(2)]
        xn = [room([D], F32) for _ in range(2 * NR)]
        qT = [room([KD, S], F16) for _ in range(2)]
        kT = [room([KD, S], F16) for _ in range(2)]
        va = [room([TB, D], F16) for _ in range(2)]
        p32 = [room([S], F32) for _ in range(2)]
        pT = [[room([TB, P], F16) for _ in range(2)] for _ in range(2)]
        negmax = room([TB], F32)
        nmax = room([TB], F32)
        den = room([TB], F32)
        rden = room([TB], F32)
        ctx_sb = room([B, D], F32)[0:C]
        cz = room([B, D], F32)[0:C]

        SELF_END = cursor[0]
        HD = 64
        HW = 2 * HD
        NP = wq_in.shape[1] // HW
        KT = TB + 1
        A_SLOTS = 2 * KT
        cursor[0] = ATTN
        wxraw = room([3, KD, HW], F32)
        woraw = room([D], F32)
        wx = [room([3, KD, HW], F16) for _ in range(2)]
        wo = [room([D], F16) for _ in range(2)]
        qn = [room([S], F16) for _ in range(2)]
        kn = [room([SK], F16) for _ in range(2)]
        qA = [[room([S], F16) for _ in range(2)] for _ in range(B)]
        kA = [[room([SK], F16) for _ in range(2)] for _ in range(B)]
        PX, PR = 3, 4
        px = [room([S], F32) for _ in range(PX)]
        pr = [[room([S], F16) for _ in range(2)] for _ in range(PR)]
        o32 = room([TB, HW], F32)
        oT = [room([TB, P], F16) for _ in range(2)]
        cursor[0] = max(cursor[0], SELF_END)
        qB = [[room([S], F16) for _ in range(2)] for _ in range(B)]
        kB = [[room([SK], F16) for _ in range(2)] for _ in range(B)]
        vh = [room([KT, 2, HD + 1], F16) for _ in range(B)]
        vl = [room([KT, 2, HD], F16) for _ in range(B)]
        pc = [room([S], F16) for _ in range(2)]
        mx3 = sb("mx3", [P, 2 * TB, 3], F32)
        m16 = sb("m16", [P, 2 * TB], F32)
        mT = sb("mT", [2 * TB, P], F16)
        rden8 = sb("rden8", [P, TB], F32)
        ROW_B1 = 4 * KD
        ROW_GATE = ROW_B1 + E * MF
        ROWS = ROW_GATE + E * KD
        rows_sb = sb("rows_sb", [ROWS, P], F32)
        cols_sb = sb("cols_sb", [P, ROWS], F32)

        def gain_shift(which, k):
            at = which * 2 * KD + k
            return dict(scale=cols_sb[:, at:at + 1], bias=cols_sb[:, at + KD:at + KD + 1])

        zn = [px[i // 4][:, i % 4 * D:(i % 4 + 1) * D] for i in range(2 * NR)]
        t32 = [pr[i][0].rearrange("p (n) -> p n", n=S).bitcast(F32) for i in range(NR)]
        cstats = sb("cstats", [C, B, 6], F32)
        cmv = sb("cmv", [C, B, 2], F32)
        cveps = sb("cveps", [C, B], F32)
        crstd = sb("crstd", [C, B], F32)
        ct32 = sb("ct32", [P, KD, B, C], F32)

        raw = [sb(f"raw{i}", [P, 2 * CH], F32) for i in range(2)]
        cursor[0] = 2 * E * (W1_F16 + W2_F16)
        xb = [room([D], F32) for _ in range(2)]
        xbT = [[room([KD, P], F16) for _ in range(2)] for _ in range(2)]
        h32 = [room([MF, P], F32) for _ in range(2)]
        hT = [[room([MF, P], F16) for _ in range(2)] for _ in range(2)]
        yb = [room([D], F32) for _ in range(2)]
        cursor[0] = 2 * E * (W1_F16 + W2_F16)
        gT = [[l_sb[:, (TB + 2 * i) * 2 * D:(TB + 2 * i + 2) * 2 * D].bitcast(F32).rearrange("p (k n) -> p k n", k=KD)
               for i in range(2)], [room([KD, 2 * P], F32) for _ in range(2)]]
        lg0 = l_sb[:, NT * 2 * D:NT * 2 * D + 2 * TB * E].bitcast(F32)
        probs8 = room([NT, E], F32)
        ex8 = room([NT, E], F32)
        mx8 = room([NT], F32)
        sum8 = room([NT], F32)
        rec8 = room([NT], F32)
        top8 = sb("top8", [P, NT, 8], F32)
        idx8 = sb("idx8", [P, NT, 8], U32)
        idxf = room([NT, 2], F32)
        oh = [room([NT, E], F32) for _ in range(2)]
        wm = sb("wm", [P, NT, E], F32)[:, :, :]
        wm1 = room([NT, E], F32)
        mask = room([NT, E], F16)
        tot = room([E, NT], F32)
        inc = room([E, NT], F32)
        slotf = room([NT, E], F32)
        sl = [room([NT, E], F32) for _ in range(2)]
        sfl = room([2, NT], F32)
        nblk = room([3, E], F32)
        wmT = w1[0:E, 0:2 * NT * P].bitcast(F32)
        late_raw = raw + [room([2 * CH], F32) for _ in range(4)]
        LATE = len(late_raw)
        slot_u = sb("slot_u", [P, 2, NT], U32)
        nblk_i = sb("nblk_i", [P, 2, E], I32)
        SLOTS_MAX = NT * P * 2 // P + E - 1
        eid_f = sb("eid_f", [1, SLOTS_MAX, E], F32)
        STEP = 6
        eid_s = room([2, SLOTS_MAX + STEP], F32)[0:1]
        eid = sb("eid", [1, SLOTS_MAX], I32)
        EBITS = (E - 1).bit_length()
        packed_f = room([2, SLOTS_MAX], F32)[0:1]
        packed = sb("packed", [1, SLOTS_MAX], I32)
        iota8 = sb("iota8", [P, E], F32)
        iota128 = sb("iota128", [P, P], F16)
        block_no = sb("block_no", [P, SLOTS_MAX], F32)
        token_no = sb("token_no", [P, NT], F32)
        slot_i = sb("slot_i", [P, 2, 2, NT], I32)
        slot_blk = room([2, NT], F32)
        slot_row = room([2, NT], F32)
        rows_u = sb("rows_u", [P, SLOTS_MAX], U32)
        tick = sb("tick", [P, 1], F32)
        rows_cur = sb("rows_cur", [P, 2], U32)
        is_row = l_sb[:, 0:2 * NT * P].rearrange("p (a t r) -> p a t r", a=2, r=P)
        is_blk = arena[:, 2 * E * (W1_F16 + W2_F16):2 * E * (W1_F16 + W2_F16) + 2 * NT * SLOTS_MAX].rearrange(
            "p (a t j) -> p a t j", a=2, j=SLOTS_MAX)
        upper = sb("upper", [P, P], F16)
        ones16 = sb("ones16", [P, P], F16)
        noreset = sb("noreset", [P, E, NT], F32)
        b2_sb = sb("b2_sb", [E, D], F32)
        b1cur = sb("b1cur", [P, 2, MF], F32)
        xn3 = [l_sb[:, t * 2 * D:(t + 1) * 2 * D].bitcast(F32) for t in range(NT)]
        yt = [h32[i // 2].rearrange("p m n -> p (m n)")[:, i % 2 * 2 * D:(i % 2 + 1) * 2 * D].rearrange("p (a d) -> p a d", a=2) for i in range(4)]
        xn_d = nc.dram_tensor("xn_d", (NT * P, D), F32, kind="Internal").ap()
        yg = nc.dram_tensor("yg", (SLOTS_MAX * P, D), F32, kind="Internal").ap()

        x_loaded = [sem(f"x_loaded_{g}") for g in range(NT // NG)]
        wa_loaded = sem("wa_loaded")
        wa_split = sem("wa_split")
        consts = sem("consts")
        consts0 = sem("consts0")
        stat_a = sem("stat_a")
        var_ready = sem("var_ready")
        rstd_ready = sem("rstd_ready")
        xn_ready = sem("xn_ready")
        xnT_filled = sem("xnT_filled")
        xnT_hi = sem("xnT_hi")
        xnT_done = sem("xnT_done")
        proj_filled = sem("proj_filled")
        proj_hi = sem("proj_hi")
        proj_done = sem("proj_done")
        a_scores = sem("a_scores")
        a_negmax = sem("a_negmax")
        a_max = sem("a_max")
        a_probs = sem("a_probs")
        a_pT = sem("a_pT")
        a_pT_hi = sem("a_pT_hi")
        a_pT_lo = sem("a_pT_lo")
        a_out = sem("a_out")
        a_rden = sem("a_rden")
        a_added = sem("a_added")
        out_done = sem("out_done")
        rows_loaded = sem("rows_loaded")
        cols_filled = sem("cols_filled")
        cols_ready = sem("cols_ready")
        ctx_loaded = sem("ctx_loaded")
        c_stat = sem("c_stat")
        c_rstd = sem("c_rstd")
        c_norm = sem("c_norm")
        c_filled = sem("c_filled")
        c_t32 = sem("c_t32")
        c_hi = sem("c_hi")
        c_done = sem("c_done")
        z_stat = sem("z_stat")
        z_var = sem("z_var")
        z_rstd = sem("z_rstd")
        z_norm = sem("z_norm")
        z_filled = sem("z_filled")
        z_t32 = sem("z_t32")
        z_hi = sem("z_hi")
        z_done = sem("z_done")
        x_consts = sem("x_consts")
        wx_loaded = sem("wx_loaded")
        wo_loaded = sem("wo_loaded")
        wx_split = sem("wx_split")
        wo_split = sem("wo_split")
        task_filled = sem("task_filled")
        task_hi = sem("task_hi")
        task_done = sem("task_done")
        m_reduced = sem("m_reduced")
        qk_spread = [sem(f"qk_spread_{i}") for i in range(3)]
        m_spread = sem("m_spread")
        scores = sem("scores")
        probs = sem("probs")
        raw_loaded = [sem(f"raw_loaded{i}") for i in range(2)]
        late_loaded = [sem(f"late_loaded{i}") for i in range(LATE)]
        raw_hi = sem("raw_hi")
        raw_split = sem("raw_split")
        late_hi = sem("late_hi")
        late_split = [sem("late_split_pool"), sem("late_split_dve")]
        f_consts0 = sem("f_consts0")
        f_consts = sem("f_consts")
        b2_loaded = sem("b2_loaded")
        g_stat = sem("g_stat")
        g_var = sem("g_var")
        g_rstd = sem("g_rstd")
        g_norm = sem("g_norm")
        g_filled = sem("g_filled")
        g_turned = sem("g_turned")
        g_logits = sem("g_logits")
        g_copied = sem("g_copied")
        ex_ready = sem("ex_ready")
        ex_done = sem("ex_done")
        route = sem("route")
        mask_ready = sem("mask_ready")
        counted = sem("counted")
        slots_ready = sem("slots_ready")
        onehots_ready = sem("onehots_ready")
        rows_filled = sem("rows_filled")
        rows_ready = sem("rows_ready")
        picked = sem("picked")
        ticked = sem("ticked")
        xn_stored = [sem(f"xn_stored_{b}") for b in range(B)]
        eid_ready = sem("eid_ready")
        wm_ready = sem("wm_ready")
        wmT_filled = sem("wmT_filled")
        wmT_ready = sem("wmT_ready")
        b2_filled = sem("b2_filled")
        b2_added = sem("b2_added")
        xb_loaded = [sem(f"xb_loaded{i}") for i in range(2)]
        e_T = sem("e_T")
        e_T_hi = sem("e_T_hi")
        e_T_lo = sem("e_T_lo")
        e_h = sem("e_h")
        e_h32 = sem("e_h32")
        e_hT_hi = sem("e_hT_hi")
        e_hT_lo = sem("e_hT_lo")
        e_y = sem("e_y")
        e_yb = sem("e_yb")
        e_bias = sem("e_bias")
        y_stored = [sem(f"y_stored{i}") for i in range(2)]
        gathered = [sem(f"gathered{i}") for i in range(4)]
        combined = sem("combined")
        probs_hi = sem("probs_hi")
        probs_lo = sem("probs_lo")
        mixed = sem("mixed")
        o_rden = sem("o_rden")
        o_done = sem("o_done")

        LAG = 3
        AT_QKV, MAX0, AT_M, AT_FINISH = [0, 2, 3, 5, 7, 66, 68, 70], 15, 65, [12, 13, 16, 20, 24, 28]
        IT = 2 * A_SLOTS
        MC = 3
        MW = SK // MC
        PREP = ([("q", c) for c in range(2)] + [("k", c) for c in range(MC)] + [("v", i) for i in range(3)]
                + [("max", h, j, c) for h in range(2) for j in range(TB) for c in range(MC)] + [("m",)])
        FINISH = [("oT", i) for i in range(2)] + [("wo", i) for i in range(TB // 2)]
        HI_TASKS = ("q", "k", "v", "oT")

        def unit_tasks(finish, prep):
            out = []
            if prep is not None:
                at = AT_QKV + [MAX0 + n for n in range(2 * TB * MC)] + [AT_M]
                out += [(q, (prep, *t)) for q, t in zip(at, PREP)]
            if finish is not None:
                out += [(q, (finish, *t)) for q, t in zip(AT_FINISH, FINISH)]
            return sorted(out, key=lambda w: w[0])

        def iteration_tasks(first, last):
            a = unit_tasks(None if first else 1, 1)
            b = unit_tasks(0, None if last else 0)
            return a + [(q + 4 * A_SLOTS, t) for q, t in b]

        LAST_TASK = 2 * NP * (len(PREP) + len(FINISH))

        class Iteration:

            def __init__(self, hp, first, last):
                self.hp, self.first, self.last = hp, first, last
                self.slots = hp * IT
                self.units = hp * 2
                n, f = len(PREP), len(FINISH)
                self.task0 = n if first else hp * 2 * (n + f) + n - f
                self.hi0 = 8 if first else hp * 20 + 6
                self.tasks, hi = [], 0
                for i, (q, t) in enumerate(iteration_tasks(first, last)):
                    self.tasks.append((q, t, i, hi))
                    hi += t[1] in HI_TASKS

            def of(self, slot, *quarters):
                return [w[1:] for w in self.tasks if w[0] // 4 == slot and w[0] % 4 in quarters]

            def number(self, b, *task):
                return next(i for _, t, i, _ in self.tasks if t == (b, *task)) + self.task0 + 1

            def turned(self, t):
                return self.number(t[0], "oT", 1) if t[1:] == ("wo", 0) else 0

        PROLOGUE = [((0, *t), i, min(i, 8)) for i, t in enumerate(PREP)]

        Z_BATCH = TB // 2
        Z_TASKS = 2 * (Z_BATCH - 1)

        QKV = 5 + 3
        WIDE = 2 * TB

        def beside_z(p):
            return PROLOGUE[2 * (p - Z_BATCH - 1):2 * (p - Z_BATCH)] if p > Z_BATCH else []

        CONSTANTS = 11 * B

        def bank(task0, i):
            return 6 + (i + (task0 if isinstance(task0, int) else 1)) % 2

        def wait(eng, sem, value):
            if not isinstance(value, int) or value > 0:
                eng.wait_ge(sem, value)

        def lat_slot(n):
            return n // TB * KT + n % TB

        G_STATS, G_POW, G_NORMAL, G_TURN = (A_SLOTS + i for i in (8, 9, 10, 11))
        GB = TB // 2

        def g_banks(g):
            return (6, 7) if g < GB else (g % 2, 2)

        def over_pairs(eng, body):
            body(Iteration(0, True, False))
            with eng.Fori(1, NP - 1) as hp:
                body(Iteration(hp, False, False))
            body(Iteration(NP - 1, False, True))

        LEAD = 2
        TURNS = (SLOTS_MAX - 2 - LEAD) // STEP

        def over_blocks(eng, body, ahead=None):
            def stretch(j, n, looped):
                extra = () if ahead is None else (ahead(j, n + 1 if looped else min(n + 1, SLOTS_MAX - j)),)
                for c in range(n):
                    body(j + c, c % 2, looped, *(() if ahead is None else (c, *extra)))
            stretch(0, LEAD, False)
            with eng.Fori(0, TURNS) as i:
                stretch(i * STEP + LEAD, STEP, True)
            stretch(LEAD + TURNS * STEP, SLOTS_MAX - LEAD - TURNS * STEP, False)

        def chunk(n):
            if n < 2 * E:
                e, k = n // 2, n % 2
                src = w1_in[e, k * P:(k + 1) * P, :]
                at = [((e * 2 + h) * KD + k) * F for h in range(2)]
                return src, [w1[:, a:a + F] for a in at]
            e, g = (n - 2 * E) // 2, n % 2
            src = w2_in[e, g * 4 * P:(g + 1) * 4 * P, :].rearrange("(m p) d -> p m d", p=P)
            at = [((e * 2 + h) * MF + g * 4) * D for h in range(2)]
            return src, [w2[:, a:a + 4 * D] for a in at]

        EARLY_CHUNKS = 2 * EARLY
        CHUNKS = 4 * E

        LATE_CHUNKS = CHUNKS - EARLY_CHUNKS
        AHEAD, BEHIND = (0, 2, 4), tuple(range(LATE_CHUNKS - 3, LATE_CHUNKS))
        BY_POOL = [m for m in range(LATE_CHUNKS) if m not in AHEAD + BEHIND]

        def late_done(m):
            return (late_split[0], BY_POOL.index(m) + 1) if m in BY_POOL else (late_split[1], (AHEAD + BEHIND).index(m) + 1)

        def raw_as(n):
            r = (raw[n % 2] if n < EARLY_CHUNKS else late_raw[(n - EARLY_CHUNKS) % LATE])[:, :]
            return r if n < 2 * E else r.rearrange("p (m d) -> p m d", d=D)

        block = es.enter_context(nc.Block())
        x_v = x_in.rearrange("b (t p) d -> p (b t) d", p=P)
        out_v = out.rearrange("b (t p) d -> p (b t) d", p=P)

        @block.sync
        def _(sp):
            for g in range(NT // NG):
                sp.dma_start(x[:, g * NG:(g + 1) * NG, :], x_v[:, g * NG:(g + 1) * NG, :]).then_inc(x_loaded[g], 16)
            sp.dma_start(wraw, attn_w.rearrange("w (k p) e -> p w k e", p=P)).then_inc(wa_loaded, 16)
            for i, row in enumerate((ln1_g, ln1_b, ln2_g, ln2_b)):
                sp.dma_start(rows_sb[i * KD:(i + 1) * KD, :], row.rearrange("(k p) -> k p", p=P)).then_inc(rows_loaded, 16)
            sp.dma_start(rows_sb[ROW_B1:ROW_GATE, :], b1_in.rearrange("e (m p) -> (e m) p", p=P)).then_inc(rows_loaded, 16)
            sp.dma_start(rows_sb[ROW_GATE:ROWS, :], gate_in.rearrange("e (k p) -> (e k) p", p=P)).then_inc(rows_loaded, 16)
            sp.dma_start(ctx_sb[:, :, :], ctx_in.rearrange("b c d -> c b d")).then_inc(ctx_loaded, 16)

            wq_v = wq_in.rearrange("(k p) n -> p k n", p=P)
            wkv_v = wkv_in.rearrange("(k p) n -> p k n", p=P)

            def at_pair(hp, start=0):
                at = hp * HW + start
                return slice(at, at + HW) if isinstance(hp, int) else bass.ds(sp.snap(at), HW)

            def load_wx(hp, free):
                where = [at_pair(hp), at_pair(hp), at_pair(hp, NP * HW)]
                wait(sp, wx_split, free)
                for i, (src, cols) in enumerate(zip((wq_v, wkv_v, wkv_v), where)):
                    sp.dma_start(wxraw[:, i, :, :], src[:, :, cols]).then_inc(wx_loaded, 16)

            def load_wo(hp):
                rows = at_pair(hp)
                wait(sp, wo_split, hp * 2)
                sp.dma_start(woraw, wo_in[rows, :]).then_inc(wo_loaded, 16)

            def spread_qk(b, q_task, k_task):
                lo, hi = slice(0, HD), slice(HD, P)
                sp.wait_ge(task_done, q_task)
                for dst, src in ((qA[b][0][lo], qn[0][lo]), (qA[b][0][hi], qn[1][lo])):
                    sp.dma_start(dst, src).then_inc(qk_spread[0], 16)
                sp.wait_ge(task_done, k_task)
                for dst, src in ((kA[b][0][lo], kn[0][lo]), (kA[b][0][hi], kn[0][lo])):
                    sp.dma_start(dst, src).then_inc(qk_spread[0], 16)
                for dst, src in ((qA[b][1][lo], qn[1][hi]), (qA[b][1][hi], qn[0][hi]),
                                 (kA[b][1][lo], kn[0][hi]), (kA[b][1][hi], kn[0][hi])):
                    sp.dma_start(dst, src).then_inc(qk_spread[1], 16)
                for dst, src in ((qB[b][0][lo], qn[0][lo]), (qB[b][1][hi], qn[0][hi]),
                                 (kB[b][0][lo], kn[1][lo]), (kB[b][1][hi], kn[1][hi])):
                    sp.dma_start(dst, src).then_inc(qk_spread[2], 16)

            def spread_m(b, m_task):
                sp.wait_ge(task_done, m_task)
                for h, row in ((0, HD), (1, 0)):
                    sp.dma_start(qB[b][h][row:row + 1, :].rearrange("a (j n) -> a j n", n=P),
                                 mT[h * TB:(h + 1) * TB, :]).then_inc(m_spread, 16)

            sp.dma_start(b2_sb[:, :], b2_in).then_inc(b2_loaded, 16)
            sp.wait_ge(a_added, NT)
            load_wx(0, 0)
            sp.wait_ge(x_consts, CONSTANTS)
            spread_qk(0, 2, 5)
            spread_m(0, len(PREP))

            def pair(it):
                if not it.last:
                    load_wx(it.hp + 1, (it.hp + 1) * 4)
                load_wo(it.hp)
                spread_qk(1, it.number(1, "q", 1), it.number(1, "k", MC - 1))
                spread_m(1, it.number(1, "m"))
                if not it.last:
                    spread_qk(0, it.number(0, "q", 1), it.number(0, "k", MC - 1))
                    spread_m(0, it.number(0, "m"))

            def load_late(m):
                n = m + EARLY_CHUNKS
                if m >= LATE:
                    sp.wait_ge(*late_done(m - LATE))
                sp.dma_start(raw_as(n), chunk(n)[0]).then_inc(late_loaded[m % LATE], 16)
            sp.wait_ge(raw_split, EARLY_CHUNKS)
            for m in range(2):
                load_late(m)
            over_pairs(sp, pair)
            def store_xn(b):
                sp.wait_ge(g_norm, (b + 1) * TB)
                sp.dma_start(xn_d[b * S:(b + 1) * S, :].rearrange("(t p) d -> p t d", p=P),
                             l_sb[:, b * TB * 2 * D:(b + 1) * TB * 2 * D].bitcast(F32).rearrange("p (t d) -> p t d", d=D)).then_inc(xn_stored[b], 16)
            store_xn(0)
            sp.wait_ge(task_done, LAST_TASK)

            for m in range(2, LATE_CHUNKS):
                load_late(m)
                if m == LATE - 1:
                    store_xn(1)

            def store_block(j, c, looped):
                rows = slice(j * P, (j + 1) * P) if isinstance(j, int) else bass.ds(sp.snap(j * P), P)
                sp.wait_ge(e_yb, j + 1)
                sp.dma_start(yg[rows, :], yb[c]).then_inc(y_stored[c], 16)
            over_blocks(sp, store_block)
            for g in range(NT // 2):
                sp.wait_ge(combined, 2 * (g * 2 + 2))
                sp.dma_start(out_v[:, g * 2:g * 2 + 2, :], x[:, g * 2:g * 2 + 2, :]).then_inc(out_done, 16)
            sp.wait_ge(out_done, NT // 2 * 16)

        def split_early(pool, n):
            pool.wait_ge(raw_loaded[n % 2], (n // 2 + 1) * 16)
            dst = [d.rearrange("p (m d) -> p m d", d=D) if n >= 2 * E else d for d in chunk(n)[1]]
            pool.tensor_copy(dst[0], raw_as(n)).then_inc(raw_hi, 1)
            pool.wait_ge(raw_hi, n + 1)
            pool.tensor_tensor(dst[1], raw_as(n), dst[0], ALU.subtract).then_inc(raw_split, 1)

        def split_late(eng, m):
            n = m + EARLY_CHUNKS
            dst = [d if n < 2 * E else d.rearrange("p (m d) -> p m d", d=D) for d in chunk(n)[1]]
            eng.wait_ge(late_hi, m + 1)
            eng.tensor_tensor(dst[1], raw_as(n), dst[0], ALU.subtract).then_inc(late_done(m)[0], 1)

        @block.gpsimd
        def _(pool):
            pool.memset(identf[:, :], 0.0).then_inc(consts0, 1)
            pool.memset(half[:, :], -0.5).then_inc(consts0, 1)
            pool.wait_ge(consts0, 2)
            pool.affine_select(out=identf[:, :], in_=identf[:, :], compare_op=ALU.not_equal, fill=1.0,
                               base=0, pattern=[[-1, P]], channel_multiplier=1).then_inc(consts, 1)
            pool.iota(iota8[:, :], pattern=[[1, E]], base=0, channel_multiplier=0,
                      allow_small_or_imprecise_dtypes=True).then_inc(f_consts, 1)
            pool.iota(block_no[:, :], pattern=[[1, SLOTS_MAX]], base=0, channel_multiplier=0,
                      allow_small_or_imprecise_dtypes=True).then_inc(f_consts, 1)
            pool.iota(iota128[:, :], pattern=[[1, P]], base=0, channel_multiplier=0,
                      allow_small_or_imprecise_dtypes=True).then_inc(f_consts, 1)
            pool.iota(token_no[:, :], pattern=[[P, NT]], base=0, channel_multiplier=1,
                      allow_small_or_imprecise_dtypes=True).then_inc(f_consts, 1)
            pool.memset(ones16[:, :], 1.0).then_inc(f_consts0, 1)
            pool.memset(noreset[:, :, :], 1.0).then_inc(f_consts0, 1)
            pool.wait_ge(f_consts0, 2)
            pool.memset(noreset[:, :, 0:1], 0.0).then_inc(f_consts, 1)
            pool.affine_select(out=upper[:, :], in_=ones16[:, :], compare_op=ALU.is_gt, fill=0.0,
                               base=0, pattern=[[1, P]], channel_multiplier=-1).then_inc(f_consts, 1)
            def split_wa(w):
                pool.wait_ge(wa_split, 1)
                pool.tensor_tensor(wa[1][:, w], wraw[:, w], wa[0][:, w], ALU.subtract).then_inc(wa_split, 1)

            for g in range(NT // NG):
                if g == 2:
                    split_wa(1)
                pool.wait_ge(var_ready, g + 1)
                pool.tensor_tensor(rstd[:, g * NG:(g + 1) * NG], veps[:, g * NG:(g + 1) * NG],
                                   half[:, g * NG:(g + 1) * NG], ALU.pow).then_inc(rstd_ready, 1)

            split_wa(0)
            split_wa(2)
            pool.wait_ge(c_stat, 2 * B + 1)
            pool.tensor_tensor(crstd[:, :], cveps[:, :], half[0:C, 0:B], ALU.pow).then_inc(c_rstd, 1)
            for n in range(EARLY_CHUNKS):
                if n >= 2:
                    pool.wait_ge(raw_split, n - 1)
                pool.dma_start(raw_as(n), chunk(n)[0]).then_inc(raw_loaded[n % 2], 16)
                if n >= 1:
                    split_early(pool, n - 1)
            split_early(pool, EARLY_CHUNKS - 1)

            constants = []
            for b in range(B):
                for h, rows in ((0, slice(HD, P)), (1, slice(0, HD))):
                    constants += [(kB[b][h][rows], 0.0), (qB[b][h][rows], 0.0)]
                constants += [(v[HD:P, TB, :, :], 0.0) for v in (vh[b], vl[b])]
                constants.append((pc[b][HD:P], 0.0))
            for b in range(B):
                constants += [(kB[b][h][row:row + 1], -8.0) for h, row in ((0, HD), (1, 0))]
                constants.append((vh[b][:, 0:TB, :, HD:HD + 1], 1.0))
                constants.append((vh[b][0:C, TB, :, HD:HD + 1], 1.0))
            pool.wait_ge(raw_split, EARLY_CHUNKS)
            for i, (buf, value) in enumerate(constants):
                if i > 0:
                    pool.wait_ge(x_consts, i)
                pool.memset(buf, value).then_inc(x_consts, 1)

            for g in range(NT // NG):
                pool.wait_ge(z_var, g + 1)
                pool.tensor_tensor(rstd[:, g * NG:(g + 1) * NG], veps[:, g * NG:(g + 1) * NG],
                                   half[:, g * NG:(g + 1) * NG], ALU.pow).then_inc(z_rstd, 1)


            def wx_low(hp, v):
                part = slice(2, 3) if v else slice(0, 2)
                pool.wait_ge(wx_split, hp * 4 + 2 * v + 1)
                pool.tensor_tensor(wx[1][:, part], wxraw[:, part], wx[0][:, part], ALU.subtract).then_inc(wx_split, 1)

            for v in range(2):
                wx_low(0, v)

            def low_half(it, s):
                n = it.slots + s
                head, kt = s // KT, s % KT
                rows = slice(0, P if kt < TB else C)
                if kt < TB:
                    dst = pr[(head * TB + kt) % PR]
                    wait(pool, mixed, it.slots + lat_slot(head * TB + kt - PR) + 1)
                else:
                    dst = pc
                    wait(pool, mixed, n - KT + 1)
                pool.wait_ge(probs_hi, n + 1)
                pool.tensor_tensor(dst[1][rows], px[s % PX][rows], dst[0][rows], ALU.subtract).then_inc(probs_lo, 1)

            def rstd_of(g):
                pool.wait_ge(g_var, g + 1)
                pool.tensor_tensor(rstd[:, g * NG:(g + 1) * NG], veps[:, g * NG:(g + 1) * NG],
                                   half[:, g * NG:(g + 1) * NG], ALU.pow).then_inc(g_rstd, 1)

            def pair(it):
                for s in range(IT):
                    low_half(it, s)
                    if it.last and s == G_POW:
                        for g in range(2):
                            rstd_of(g)
                    if not it.last and s in (9, A_SLOTS + 4):
                        wx_low(it.hp + 1, s > A_SLOTS)
                    if s == 12:
                        pool.wait_ge(wo_split, it.hp * 2 + 1)
                        pool.tensor_tensor(wo[1], woraw, wo[0], ALU.subtract).then_inc(wo_split, 1)
            over_pairs(pool, pair)
            for g in range(2, NT // NG):
                rstd_of(g)
            for m in BY_POOL:
                split_late(pool, m)
            for b in range(B):
                pool.wait_ge(xn_stored[b], 16)

            def fetch(j, c):
                pool.wait_ge(picked, j + 1)
                wait(pool, e_T, j - 1)
                wait(pool, ticked, j)
                pool.tensor_tensor(tick[:, :], half[:, 0:1], half[:, 1:2], ALU.add).then_inc(ticked, 1)
                pool.indirect_dma_start(out=xb[c], out_offset=None, in_=xn_d[:, :],
                                        in_offset=bass.IndirectOffsetOnAxis(ap=rows_cur[:, c:c + 1], axis=0)).then_inc(xb_loaded[c], 16)
            fetch(0, 0)
            fetch(1, 1)

            def fetch_next(j, c, looped):
                if looped or j + 2 < SLOTS_MAX:
                    fetch(j + 2, c)
            over_blocks(pool, fetch_next)
            pool.wait_ge(slots_ready, 1)
            pool.wait_ge(y_stored[0], (SLOTS_MAX + 1) // 2 * 16)
            pool.wait_ge(y_stored[1], SLOTS_MAX // 2 * 16)
            for t in range(NT):
                if t >= 4:
                    pool.wait_ge(combined, 2 * (t - 3))
                for a in range(2):
                    pool.indirect_dma_start(out=yt[t % 4][:, a, :], out_offset=None, in_=yg[:, :],
                                            in_offset=bass.IndirectOffsetOnAxis(ap=slot_u[:, a, t:t + 1], axis=0)).then_inc(gathered[t % 4], 16)

        PROJ = 12

        @block.scalar
        def _(act):
            def hi_of_xnT():
                for t in range(0, NT, 2):
                    act.wait_ge(xnT_filled, t // 2 + 1)
                    b, j = t // TB, t % TB
                    act.activation(lT[0][:, :, b, j * P:(j + 2) * P],
                                   ps[:, t // 2 % NR, :].rearrange("p (k n) -> p k n", k=KD),
                                   ACT.Copy).then_inc(xnT_hi, 1)
                    if t == 2:
                        act.wait_ge(wa_loaded, 16)
                        act.activation(wa[0], wraw, ACT.Copy).then_inc(wa_split, 1)
            hi_of_xnT()
            act.wait_ge(cols_filled, 1)
            act.activation(cols_sb[:, :], ps[:, 3, 0:ROWS], ACT.Copy).then_inc(cols_ready, 1)
            act.wait_ge(cols_ready, 1)
            with act.Fori(0, B) as b:
                for n in range(PROJ):
                    act.wait_ge(proj_filled, b * PROJ + n + 1)
                    if n < 8:
                        dst = (qT, kT)[n // 4][0][:, n % 4 // 2, n % 2 * CH:(n % 2 + 1) * CH]
                        src = ps[:, 6 + n % 2, :]
                    else:
                        dst = va[0][:, (n - 8) * 2:(n - 8) * 2 + 2, :]
                        src = ps[:, 6 + n % 2, :].rearrange("p (j d) -> p j d", j=2)
                    act.activation(dst, src, ACT.Copy).then_inc(proj_hi, 1)

                def exp(j):
                    act.wait_ge(a_max, b * TB + j + 1)
                    if j >= 2:
                        act.wait_ge(a_pT, b * TB + j - 1)
                    act.activation(p32[j % 2], ps[:, j % 2 * 2:j % 2 * 2 + 2, :], ACT.Exp, scale=1.0 / 16,
                                   bias=nmax[:, j:j + 1], accum_out=den[:, j:j + 1]).then_inc(a_probs, 1)
                exp(0)
                exp(1)
                for j in range(TB):
                    act.wait_ge(a_pT, b * TB + j + 1)
                    if j >= 2:
                        act.wait_ge(a_out, b * TB + j - 1)
                    act.activation(pT[j % 2][0], ps[:, 4:6, :].rearrange("p a (c n) -> p (a c) n", n=P),
                                   ACT.Copy).then_inc(a_pT_hi, 1)
                    if j + 2 < TB:
                        exp(j + 2)

            def wx_high(hp, v):
                part = slice(2, 3) if v else slice(0, 2)
                wait(act, wx_split, hp * 4 + 2 * v)
                act.activation(wx[0][:, part], wxraw[:, part], ACT.Copy).then_inc(wx_split, 1)

            def z_affine(p):
                act.wait_ge(z_filled, p + 1)
                wait(act, z_done, p - NR + 1)
                for k in range(KD):
                    act.activation(t32[p % NR][:, k * 2 * P:(k + 1) * 2 * P], ps[:, p % NR, k * 2 * P:(k + 1) * 2 * P],
                                   ACT.Identity, **gain_shift(1, k)).then_inc(z_t32, 1)

            def task(it_task0, it_hi0, t, i, hi, units):
                b, kind = t[0], t[1]
                src = ps[:, bank(it_task0, i), :]
                if kind in HI_TASKS:
                    act.wait_ge(task_filled, it_task0 + i + 1)
                if kind == "q":
                    if t[2] == 0:
                        for spread in qk_spread:
                            wait(act, spread, units * 64)
                    act.activation(qn[0][:, t[2] * CH:(t[2] + 1) * CH], src, ACT.Copy).then_inc(task_hi, 1)
                elif kind == "k":
                    act.activation(kn[0][:, t[2] * MW:(t[2] + 1) * MW], src[:, 0:MW], ACT.Copy).then_inc(task_hi, 1)
                elif kind == "v":
                    if t[2] == 0:
                        wait(act, mixed, (units - 1) * A_SLOTS)
                    if t[2] < 2:
                        act.activation(vh[b][:, t[2] * 4:t[2] * 4 + 4, :, 0:HD],
                                       src.rearrange("p (j h d) -> p j h d", j=4, h=2), ACT.Copy).then_inc(task_hi, 1)
                    else:
                        act.activation(vh[b][0:C, TB, :, 0:HD], src[0:C, 0:HW].rearrange("p (h d) -> p h d", h=2),
                                       ACT.Copy).then_inc(task_hi, 1)
                elif kind == "oT":
                    act.activation(oT[0][:, t[2] * 4:t[2] * 4 + 4, :], src.rearrange("p (j n) -> p j n", n=P),
                                   ACT.Copy).then_inc(task_hi, 1)

            act.wait_ge(c_filled, 1)
            for b in range(B):
                for k in range(KD):
                    act.activation(ct32[:, k, b, :], ps[:, 5, :].rearrange("p (k b n) -> p k b n", k=KD, b=B)[:, k, b, 0:C],
                                   ACT.Identity, **gain_shift(0, k)).then_inc(c_t32, 1)
            for p in range(NT // 2):
                z_affine(p)
                if p == Z_BATCH - 1:
                    act.wait_ge(wx_loaded, 48)
                    wx_high(0, 0)
                    wx_high(0, 1)
                    act.wait_ge(x_consts, CONSTANTS)
                for t, i, hi in beside_z(p):
                    task(0, 0, t, i, hi, 0)
            for t, i, hi in PROLOGUE[Z_TASKS:QKV]:
                task(0, 0, t, i, hi, 0)

            def probs_of(it, s):
                n = it.slots + s
                head, kt = s // KT, s % KT
                rows = slice(0, P if kt < TB else C)
                act.wait_ge(scores, n + 1)
                wait(act, probs_lo, n - PX + 1)
                act.activation(px[s % PX][rows], ps[rows, s % 2 * 2:s % 2 * 2 + 2, :], ACT.Exp,
                               scale=0.125).then_inc(probs, 1)

            def high_half(it, s):
                n = it.slots + s
                head, kt = s // KT, s % KT
                rows = slice(0, P if kt < TB else C)
                if kt < TB:
                    dst = pr[(head * TB + kt) % PR][0]
                    wait(act, mixed, it.slots + lat_slot(head * TB + kt - PR) + 1)
                else:
                    dst = pc[0]
                    wait(act, mixed, n - KT + 1)
                act.wait_ge(probs, n + 1)
                act.activation(dst[rows], px[s % PX][rows], ACT.Copy).then_inc(probs_hi, 1)

            def g_turn(g):
                act.wait_ge(g_filled, g + 1)
                wait(act, g_logits, 2 * (g - 1))
                act.activation(gT[g // GB][g % 2], ps[:, g_banks(g)[0], :].rearrange("p (k n) -> p k n", k=KD),
                               ACT.Copy).then_inc(g_turned, 1)

            def pair(it):
                for s in range(IT):
                    units = it.units + 1 + (s >= A_SLOTS)
                    for step, quarters in ((None, (0,)), (probs_of, (1,)), (high_half, (2, 3))):
                        if step is not None:
                            step(it, s)
                        for t, i, hi in it.of(s, *quarters):
                            task(it.task0, it.hi0, t, i, hi, units)
                    if it.last and s >= G_TURN and (s - G_TURN) % 2 == 0:
                        g_turn((s - G_TURN) // 2)
                    if s == 8 and not it.last:
                        act.wait_ge(wx_loaded, (it.hp + 2) * 48)
                        act.wait_ge(task_done, it.number(1, "k", MC - 1))
                        wx_high(it.hp + 1, 0)
                    if s == A_SLOTS + 3 and not it.last:
                        act.wait_ge(task_done, it.number(1, "v", 2))
                        wx_high(it.hp + 1, 1)
                    if s == 11:
                        act.wait_ge(wo_loaded, (it.hp + 1) * 16)
                        if not it.first:
                            act.wait_ge(task_done, it.number(1, "wo", TB // 2 - 1))
                        act.activation(wo[0], woraw, ACT.Copy).then_inc(wo_split, 1)
            over_pairs(act, pair)
            act.wait_ge(g_logits, TB)
            act.activation(lg0, ps[:, 7, 0:TB * E], ACT.Copy).then_inc(g_copied, 1)
            for i, t in enumerate(FINISH):
                task(LAST_TASK - len(FINISH), 0, (1, *t), i, 0, 2 * NP)

            act.wait_ge(task_done, LAST_TASK)

            def late_high(m):
                n = m + EARLY_CHUNKS
                act.wait_ge(late_loaded[m % LATE], (m // LATE + 1) * 16)
                dst = chunk(n)[1][0]
                act.activation(dst if n < 2 * E else dst.rearrange("p (m d) -> p m d", d=D), raw_as(n), ACT.Copy).then_inc(late_hi, 1)

            for g in range(GB, NT // 2):
                g_turn(g)
                for m in ((0, 1), (2, 3), (4,), (5,))[g - GB]:
                    late_high(m)
            act.wait_ge(ex_ready, 1)
            act.activation(probs8, ex8, ACT.Exp).then_inc(ex_done, 1)
            for m in range(6, LATE_CHUNKS):
                late_high(m)

            def turn_hi(j, c, looped):
                act.wait_ge(e_T, j + 1)
                wait(act, e_h, j - 1)
                act.activation(xbT[c][0], ps[:, c, 0:2 * P].rearrange("p (k n) -> p k n", k=KD), ACT.Copy).then_inc(e_T_hi, 1)

            def hidden(j, c):
                act.wait_ge(e_h, j + 1)
                act.wait_ge(e_bias, j + 1)
                wait(act, e_hT_lo, j - 1)
                for m in range(MF):
                    op = act.activation(h32[c][:, m, :], ps[:, 2 + c * 2 + m // 4, m % 4 * P:(m % 4 + 1) * P], ACT.Relu,
                                        bias=b1cur[:, c, m:m + 1])
                op.then_inc(e_h32, 1)

            turn_hi(0, 0, False)
            turn_hi(1, 1, False)
            hidden(0, 0)

            def block_act(j, c, looped):
                if looped or j + 2 < SLOTS_MAX:
                    turn_hi(j + 2, c, looped)
                if looped or j + 1 < SLOTS_MAX:
                    hidden(j + 1, 1 - c)
                act.wait_ge(e_y, j + 1)
                wait(act, y_stored[c], (j - c) * 8)
                act.activation(yb[c], ps[:, 6 + c, 0:D], ACT.Copy).then_inc(e_yb, 1)
            over_blocks(act, block_act)
            for q in range(NT // 4):
                act.wait_ge(wmT_filled, q + 1)
                act.activation(wmT[:, q * 4 * P:(q + 1) * 4 * P], ps[0:E, q, :], ACT.Copy).then_inc(wmT_ready, 1)

        @block.vector
        def _(dve):
            def x_stats(g):
                dve.wait_ge(x_loaded[g], 16)
                for t in range(g * NG, (g + 1) * NG):
                    dve.bn_stats(stats[:, t, :], x[:, t, :]).then_inc(stat_a, 1)
                for t in range(g * NG, (g + 1) * NG):
                    dve.wait_ge(stat_a, g * NG * 2 + t - g * NG + 1)
                    dve.bn_aggr(mv[:, t, :], stats[:, t, :]).then_inc(stat_a, 1)
                dve.wait_ge(stat_a, (g + 1) * NG * 2)
                dve.tensor_scalar(veps[:, g * NG:(g + 1) * NG], mv[:, g * NG:(g + 1) * NG, 1], EPS, None,
                                  ALU.add).then_inc(var_ready, 1)

            def x_normal(p):
                dve.wait_ge(rstd_ready, 2 * p // NG + 1)
                wait(dve, xnT_filled, p - NR + 1)
                for t in (2 * p, 2 * p + 1):
                    dve.tensor_scalar(xn[t % (2 * NR)], x[:, t, :], mv[:, t, 0:1], rstd[:, t:t + 1],
                                      ALU.subtract, ALU.mult).then_inc(xn_ready, 1)

            def lo_of_xnT(p):
                dve.wait_ge(xnT_hi, p + 1)
                b, j = 2 * p // TB, 2 * p % TB
                dve.tensor_tensor(lT[1][:, :, b, j * P:(j + 2) * P],
                                  ps[:, p % NR, :].rearrange("p (k n) -> p k n", k=KD),
                                  lT[0][:, :, b, j * P:(j + 2) * P], ALU.subtract).then_inc(xnT_done, 1)

            x_stats(0)
            x_stats(1)
            for p in range(NT // 2):
                x_normal(p)
                if p >= 2:
                    lo_of_xnT(p - 2)
                if p in (1, 3):
                    x_stats(p // 2 + 2)
            lo_of_xnT(NT // 2 - 2)
            lo_of_xnT(NT // 2 - 1)
            dve.wait_ge(ctx_loaded, 16)
            for b in range(B):
                dve.bn_stats(cstats[:, b, :], ctx_sb[:, b, :]).then_inc(c_stat, 1)
            for b in range(B):
                dve.wait_ge(c_stat, b + 1)
                dve.bn_aggr(cmv[:, b, :], cstats[:, b, :]).then_inc(c_stat, 1)
            dve.wait_ge(c_stat, 2 * B)
            dve.tensor_scalar(cveps[:, :], cmv[:, :, 1], EPS, None, ALU.add).then_inc(c_stat, 1)
            dve.wait_ge(c_rstd, 1)
            for b in range(B):
                dve.tensor_scalar(cz[:, b, :], ctx_sb[:, b, :], cmv[:, b, 0:1], crstd[:, b:b + 1],
                                  ALU.subtract, ALU.mult).then_inc(c_norm, 1)
            with dve.Fori(0, B) as b:
                for n in range(PROJ):
                    dve.wait_ge(proj_hi, b * PROJ + n + 1)
                    if n < 8:
                        dst = [h[:, n % 4 // 2, n % 2 * CH:(n % 2 + 1) * CH] for h in (qT, kT)[n // 4]]
                        src = ps[:, 6 + n % 2, :]
                    else:
                        dst = [h[:, (n - 8) * 2:(n - 8) * 2 + 2, :] for h in va]
                        src = ps[:, 6 + n % 2, :].rearrange("p (j d) -> p j d", j=2)
                    dve.tensor_tensor(dst[1], src, dst[0], ALU.subtract).then_inc(proj_done, 1)

                def rowmax(j):
                    dve.wait_ge(a_scores, b * TB + j + 1)
                    dve.tensor_reduce(negmax[:, j:j + 1], ps[:, j % 2 * 2:j % 2 * 2 + 2, :], AX.XY, ALU.max,
                                      negate=True).then_inc(a_negmax, 1)
                    dve.wait_ge(a_negmax, b * TB + j + 1)
                    dve.tensor_scalar(nmax[:, j:j + 1], negmax[:, j:j + 1], 1.0 / 16, None,
                                      ALU.mult).then_inc(a_max, 1)
                rowmax(0)
                rowmax(1)
                for j in range(TB):
                    dve.wait_ge(a_pT_hi, b * TB + j + 1)
                    dve.tensor_tensor(pT[j % 2][1], ps[:, 4:6, :].rearrange("p a (c n) -> p (a c) n", n=P),
                                      pT[j % 2][0], ALU.subtract).then_inc(a_pT_lo, 1)
                    if j + 2 < TB:
                        rowmax(j + 2)
                    dve.reciprocal(rden[:, j:j + 1], den[:, j:j + 1]).then_inc(a_rden, 1)
                    dve.wait_ge(a_rden, b * TB + j + 1)
                    dve.wait_ge(a_out, b * TB + j + 1)
                    xt = x[:, bass.ds(b * TB + j, 1), :].rearrange("p a d -> p (a d)")
                    dve.scalar_tensor_tensor(out=xt, in0=ps[:, 6 + j % 2, 0:D], scalar=rden[:, j:j + 1],
                                             in1=xt, op0=ALU.mult, op1=ALU.add).then_inc(a_added, 1)

            dve.wait_ge(a_added, NT)

            def z_stats(g):
                gs = slice(g * NG, (g + 1) * NG)
                for t in range(g * NG, (g + 1) * NG):
                    dve.bn_stats(stats[:, t, :], x[:, t, :]).then_inc(z_stat, 1)
                for t in range(g * NG, (g + 1) * NG):
                    dve.wait_ge(z_stat, g * NG * 2 + t - g * NG + 1)
                    dve.bn_aggr(mv[:, t, :], stats[:, t, :]).then_inc(z_stat, 1)
                dve.wait_ge(z_stat, (g + 1) * NG * 2)
                dve.tensor_scalar(veps[:, gs], mv[:, gs, 1], 1 + EPS, EPS * EPS, ALU.mult, ALU.add).then_inc(z_var, 1)

            def z_normal(p):
                for t in (2 * p, 2 * p + 1):
                    dve.wait_ge(z_rstd, t // NG + 1)
                    wait(dve, z_filled, p - NR + 1)
                    dve.tensor_scalar(zn[t % (2 * NR)], x[:, t, :], mv[:, t, 0:1], rstd[:, t:t + 1],
                                      ALU.subtract, ALU.mult).then_inc(z_norm, 1)

            def z_halves(p):
                b, j = 2 * p // TB, 2 * p % TB
                src = t32[p % NR].rearrange("p (k n) -> p k n", k=KD)
                dst = [lT[h][:, :, b, j * P:(j + 2) * P] for h in range(2)]
                dve.wait_ge(z_t32, 2 * p + 2)
                dve.tensor_copy(dst[0], src).then_inc(z_hi, 1)
                dve.wait_ge(z_hi, p + 1)
                dve.tensor_tensor(dst[1], src, dst[0], ALU.subtract).then_inc(z_done, 1)

            def task(it_task0, it_hi0, t, i, hi, units):
                b, kind = t[0], t[1]
                src = ps[:, bank(it_task0, i), :]
                if kind in HI_TASKS:
                    dve.wait_ge(task_hi, it_hi0 + hi + 1)
                else:
                    dve.wait_ge(task_filled, it_task0 + i + 1)
                if kind == "q":
                    cols = slice(t[2] * CH, (t[2] + 1) * CH)
                    op = dve.tensor_tensor(qn[1][:, cols], src, qn[0][:, cols], ALU.subtract)
                elif kind == "k":
                    cols = slice(t[2] * MW, (t[2] + 1) * MW)
                    op = dve.tensor_tensor(kn[1][:, cols], src[:, 0:MW], kn[0][:, cols], ALU.subtract)
                elif kind == "v" and t[2] < 2:
                    js = slice(t[2] * 4, t[2] * 4 + 4)
                    op = dve.tensor_tensor(vl[b][:, js, :, :], src.rearrange("p (j h d) -> p j h d", j=4, h=2),
                                           vh[b][:, js, :, 0:HD], ALU.subtract)
                elif kind == "v":
                    op = dve.tensor_tensor(vl[b][0:C, TB, :, :], src[0:C, 0:HW].rearrange("p (h d) -> p h d", h=2),
                                           vh[b][0:C, TB, :, 0:HD], ALU.subtract)
                elif kind == "oT":
                    js = slice(t[2] * 4, t[2] * 4 + 4)
                    op = dve.tensor_tensor(oT[1][:, js, :], src.rearrange("p (j n) -> p j n", n=P),
                                           oT[0][:, js, :], ALU.subtract)
                elif kind == "max":
                    _, _, h, j, c = t
                    op = dve.tensor_reduce(mx3[:, h * TB + j, c:c + 1], src[:, 0:MW], AX.X, ALU.max)
                elif kind == "m":
                    wait(dve, m_spread, units * 32)
                    op = dve.tensor_scalar(mT[:, :], src[0:2 * TB, 0:P], 0.125, None, ALU.mult)
                elif kind == "wo":
                    xt = x[:, b * TB + t[2] * 2:b * TB + t[2] * 2 + 2, :]
                    op = dve.tensor_tensor(xt, src.rearrange("p (a d) -> p a d", a=2), xt, ALU.add)
                op.then_inc(task_done, 1)
                if kind == "max" and t[2:] == (1, TB - 1, MC - 1):
                    dve.wait_ge(task_done, it_task0 + i + 1)
                    dve.tensor_reduce(m16[:, :], mx3[:, :, :], AX.X, ALU.max).then_inc(m_reduced, 1)

            def head_out(it, head):
                n = it.units * 2 + head
                dve.wait_ge(mixed, it.slots + (head + 1) * KT)
                acc = ps[:, 4:6, 0:4 * (HD + 1)].rearrange("p a (j d) -> p a j d", d=HD + 1)
                dve.reciprocal(rden8[:, :].rearrange("p (a j) -> p a j", a=2), acc[:, :, :, HD]).then_inc(o_rden, 1)
                dve.wait_ge(o_rden, n + 1)
                for a in range(2):
                    dve.tensor_tensor(o32[:, a * 4:a * 4 + 4, head % 2 * HD:(head % 2 + 1) * HD], acc[:, a, :, 0:HD],
                                      rden8[:, a * 4:a * 4 + 4, None].to_broadcast([P, 4, HD]), ALU.mult).then_inc(o_done, 1)

            z_stats(0)
            z_stats(1)
            dve.wait_ge(c_filled, 1)
            for p in range(NT // 2):
                z_normal(p)
                if p == 2:
                    dve.wait_ge(c_t32, KD * B)
                    dve.tensor_copy(lT[0][:, :, :, S:SK], ct32[:, :, :, :]).then_inc(c_hi, 1)
                    dve.wait_ge(c_hi, 1)
                    dve.tensor_tensor(lT[1][:, :, :, S:SK], ct32[:, :, :, :], lT[0][:, :, :, S:SK],
                                      ALU.subtract).then_inc(c_done, 1)
                if p >= 2:
                    z_halves(p - 2)
                if p in (1, 2):
                    z_stats(p + 1)
                for t, i, hi in beside_z(p):
                    task(0, 0, t, i, hi, 0)
            z_halves(NT // 2 - 2)
            z_halves(NT // 2 - 1)
            for t, i, hi in PROLOGUE[Z_TASKS:QKV]:
                task(0, 0, t, i, hi, 0)
            for n in range(WIDE):
                dve.wait_ge(task_filled, QKV + MC * (n + 1))
                dve.tensor_reduce(mx3[:, n, 0:1], ps[:, n % 2 * MC:(n % 2 + 1) * MC, 0:MW], AX.XY, ALU.max).then_inc(task_done, MC)
            dve.wait_ge(task_done, QKV + MC * WIDE)
            dve.tensor_copy(m16[:, :], mx3[:, :, 0]).then_inc(m_reduced, 1)
            for t, i, hi in PROLOGUE[-1:]:
                task(0, 0, t, i, hi, 0)

            def g_stats(g):
                tiles = range(g * NG, (g + 1) * NG)
                gs = slice(g * NG, (g + 1) * NG)
                for t in tiles:
                    dve.bn_stats(stats[:, t, :], x[:, t, :]).then_inc(g_stat, 1)
                for t in tiles:
                    dve.wait_ge(g_stat, g * NG * 2 + t - g * NG + 1)
                    dve.bn_aggr(mv[:, t, :], stats[:, t, :]).then_inc(g_stat, 1)
                dve.wait_ge(g_stat, (g + 1) * NG * 2)
                dve.tensor_scalar(veps[:, gs], mv[:, gs, 1], EPS, None, ALU.add).then_inc(g_var, 1)

            def g_normal(t):
                dve.wait_ge(g_rstd, t // NG + 1)
                dve.tensor_scalar(xn3[t], x[:, t, :], mv[:, t, 0:1], rstd[:, t:t + 1],
                                  ALU.subtract, ALU.mult).then_inc(g_norm, 1)

            def pair(it):
                for s in range(IT):
                    if it.last and s == G_STATS:
                        dve.wait_ge(task_done, it.number(0, "wo", TB // 2 - 1))
                        for g in range(2):
                            g_stats(g)
                    if it.last and s == G_NORMAL:
                        for t in range(NT // 2):
                            g_normal(t)
                    units = it.units + 1 + (s >= A_SLOTS)
                    for quarter in range(4):
                        if quarter == 3:
                            for head in range(4):
                                if s == head * KT + KT + LAG - 1:
                                    head_out(it, head)
                            if s == LAG - 1 and not it.first:
                                head_out(Iteration(it.hp - 1, False, False), 3)
                        for t, i, hi in it.of(s, quarter):
                            task(it.task0, it.hi0, t, i, hi, units)
            over_pairs(dve, pair)
            head_out(Iteration(NP - 1, False, True), 3)
            for i, t in enumerate(FINISH):
                task(LAST_TASK - len(FINISH), 20 * NP - 2, (1, *t), i, i, 2 * NP)

            dve.wait_ge(task_done, LAST_TASK)
            for g in range(2, NT // NG):
                g_stats(g)
            dve.wait_ge(g_logits, TB)
            for t in range(NT // 2, NT):
                g_normal(t)
            for m in AHEAD:
                split_late(dve, m)

            step = [0]

            def then(ins):
                step[0] += 1
                ins.then_inc(route, 1)
                dve.wait_ge(route, step[0])

            dve.wait_ge(g_logits, NT)
            dve.wait_ge(g_copied, 1)
            along_e = lambda v: v[:, :, None].to_broadcast([P, v.shape[1], E])
            logits = [v.rearrange("p (t e) -> p t e", e=E) for v in (lg0, ps[:, 2, 0:TB * E])]
            for b, lg in enumerate(logits):
                ins = dve.tensor_reduce(mx8[:, b * TB:(b + 1) * TB], lg, AX.X, ALU.max)
            then(ins)
            for b, lg in enumerate(logits):
                ins = dve.tensor_tensor(ex8[:, b * TB:(b + 1) * TB, :], lg, along_e(mx8[:, b * TB:(b + 1) * TB]), ALU.subtract)
            ins.then_inc(ex_ready, 1)
            dve.wait_ge(ex_done, 1)
            then(dve.tensor_reduce(sum8, probs8, AX.X, ALU.add))
            then(dve.reciprocal(rec8, sum8))
            then(dve.tensor_tensor(ex8, probs8, along_e(rec8), ALU.mult))
            for t in range(NT):
                ins = dve.max(top8[:, t, :], ex8[:, t, :])
            then(ins)
            for t in range(NT):
                ins = dve.max_index(out=idx8[:, t, :], in_max=top8[:, t, :], in_values=ex8[:, t, :])
            then(ins)
            then(dve.tensor_copy(idxf, idx8[:, :, 0:2]))
            dve.wait_ge(f_consts, 6)
            for a in range(2):
                then(dve.tensor_tensor(oh[a], iota8[:, None, :].to_broadcast([P, NT, E]), along_e(idxf[:, :, a]), ALU.is_equal))
            dve.tensor_tensor(mask, oh[0], oh[1], ALU.add).then_inc(mask_ready, 1)
            then(dve.tensor_tensor(wm, oh[0], along_e(top8[:, :, 0]), ALU.mult))
            then(dve.tensor_tensor(wm1, oh[1], along_e(top8[:, :, 1]), ALU.mult))
            dve.tensor_tensor(wm, wm, wm1, ALU.add).then_inc(wm_ready, 1)
            dve.wait_ge(counted, 1)
            before = ps[:, 0, 0:NT * E].rearrange("p (t e) -> p t e", e=E)
            total = ps[:, 0, NT * E:2 * NT * E].rearrange("p (t e) -> p e t", e=E)
            then(dve.tensor_copy(tot, total))
            flat = lambda v: v.rearrange("p e t -> p (e t)")
            then(dve.tensor_tensor_scan(flat(inc), flat(noreset[:, :, :]), flat(tot), 0.0, ALU.mult, ALU.add))
            then(dve.tensor_scalar(nblk_i[:, 0, :], inc[:, :, NT - 1], float(P - 1), None, ALU.add))
            then(dve.tensor_scalar(nblk_i[:, 1, :], nblk_i[:, 0, :], 7, None, ALU.arith_shift_right))
            then(dve.tensor_copy(nblk[:, 0, :], nblk_i[:, 1, :]))
            then(dve.tensor_tensor_scan(nblk[:, 1, :], noreset[:, 0:1, 1:1 + E].rearrange("p a e -> p (a e)"), nblk[:, 0, :], 0.0, ALU.mult, ALU.add))
            then(dve.tensor_tensor(nblk[:, 2, :], nblk[:, 1, :], nblk[:, 0, :], ALU.subtract))
            then(dve.tensor_scalar(nblk[:, 2, :], nblk[:, 2, :], float(P), None, ALU.mult))
            then(dve.tensor_tensor(inc, inc, tot, ALU.subtract))
            then(dve.tensor_tensor(inc, inc, nblk[:, 2, :][:, :, None].to_broadcast([P, E, NT]), ALU.add))
            then(dve.tensor_tensor(slotf, before, inc.rearrange("p e t -> p t e"), ALU.add))
            for a in range(2):
                then(dve.tensor_tensor(sl[a], oh[a], slotf, ALU.mult))
                then(dve.tensor_reduce(sfl[:, a, :], sl[a], AX.X, ALU.add))
            then(dve.tensor_copy(slot_i[:, 0, :, :], sfl))
            then(dve.tensor_scalar(slot_i[:, 1, :, :], slot_i[:, 0, :, :], 7, None, ALU.arith_shift_right))
            then(dve.tensor_copy(slot_blk, slot_i[:, 1, :, :]))
            then(dve.scalar_tensor_tensor(out=slot_row, in0=slot_blk, scalar=float(-P), in1=sfl, op0=ALU.mult, op1=ALU.add))
            dve.wait_ge(xn_stored[0], 16)
            dve.tensor_tensor(is_row, iota128[:, None, None, :].to_broadcast([P, 2, NT, P]),
                              slot_row[:, :, :, None].to_broadcast([P, 2, NT, P]), ALU.is_equal)
            then(dve.tensor_tensor(is_blk, block_no[:, None, None, :].to_broadcast([P, 2, NT, SLOTS_MAX]),
                                   slot_blk[:, :, :, None].to_broadcast([P, 2, NT, SLOTS_MAX]), ALU.is_equal))
            dve.tensor_tensor(is_blk, is_blk, token_no[:, None, :, None].to_broadcast([P, 2, NT, SLOTS_MAX]),
                              ALU.mult).then_inc(onehots_ready, 1)
            dve.tensor_copy(slot_u[:, :, :], sfl).then_inc(slots_ready, 1)
            then(dve.tensor_tensor(eid_f[:, :, :], block_no[0:1, :, None].to_broadcast([1, SLOTS_MAX, E]),
                                   nblk[0:1, 1, :][:, None, :].to_broadcast([1, SLOTS_MAX, E]), ALU.is_ge))
            dve.memset(eid_s[:, :, SLOTS_MAX:], 0.0)
            then(dve.tensor_reduce(eid_s[:, 0, 0:SLOTS_MAX], eid_f[:, :, :], AX.X, ALU.add))
            then(dve.tensor_scalar(eid_s[:, 1, 0:SLOTS_MAX], eid_s[:, 0, 0:SLOTS_MAX], float(E - 1), None, ALU.min))
            then(dve.tensor_copy(eid[:, :], eid_s[:, 1, 0:SLOTS_MAX]))
            acc = eid_s[:, 1, STEP:]
            for i in range(STEP - 1, -1, -1):
                to = packed_f[:, i % 2, :] if i else packed[:, :]
                ins = dve.scalar_tensor_tensor(out=to, in0=acc, scalar=float(1 << EBITS), in1=eid_s[:, 1, i:i + SLOTS_MAX],
                                               op0=ALU.mult, op1=ALU.add)
                if i:
                    then(ins)
                acc = to
            ins.then_inc(eid_ready, 1)
            dve.wait_ge(rows_filled, 1)
            dve.tensor_copy(rows_u[:, :], ps[:, 1, 0:SLOTS_MAX]).then_inc(rows_ready, 1)
            dve.wait_ge(rows_ready, 1)

            def pick(j, c):
                wait(dve, xb_loaded[c], (j - c) * 8)
                dve.tensor_copy(rows_cur[:, c:c + 1], rows_u[:, j:j + 1] if isinstance(j, int) else
                                rows_u[:, bass.ds(j, 1)]).then_inc(picked, 1)
            pick(0, 0)
            pick(1, 1)
            for m in BEHIND:
                split_late(dve, m)

            def turn_lo(j, c):
                dve.wait_ge(e_T_hi, j + 1)
                dve.tensor_tensor(xbT[c][1], ps[:, c, 0:2 * P].rearrange("p (k n) -> p k n", k=KD), xbT[c][0],
                                  ALU.subtract).then_inc(e_T_lo, 1)

            def bias(j, c):
                wait(dve, e_h32, j - 1)
                e = dve.value_load(eid[0:1, j:j + 1] if isinstance(j, int) else eid[0:1, bass.ds(j, 1)], min_val=0, max_val=E - 1)
                dve.tensor_copy(b1cur[:, c, :], cols_sb[:, bass.ds(e * MF + ROW_B1, MF)]).then_inc(e_bias, 1)

            def split_hidden(j, c):
                dve.wait_ge(e_h32, j + 1)
                wait(dve, e_y, j - 1)
                dve.tensor_copy(hT[c][0], h32[c]).then_inc(e_hT_hi, 1)
                dve.wait_ge(e_hT_hi, j + 1)
                dve.tensor_tensor(hT[c][1], h32[c], hT[c][0], ALU.subtract).then_inc(e_hT_lo, 1)

            turn_lo(0, 0)
            pick(2, 0)
            bias(0, 0)
            turn_lo(1, 1)
            pick(3, 1)
            split_hidden(0, 0)

            def block_dve(j, c, looped):
                if looped or j + 1 < SLOTS_MAX:
                    bias(j + 1, 1 - c)
                if looped or j + 2 < SLOTS_MAX:
                    turn_lo(j + 2, c)
                if looped or j + 4 < SLOTS_MAX:
                    pick(j + 4, c)
                if looped or j + 1 < SLOTS_MAX:
                    split_hidden(j + 1, 1 - c)
            over_blocks(dve, block_dve)
            for t in range(NT):
                if t % 2 == 0:
                    dve.wait_ge(b2_filled, t // 2 + 1)
                    dve.tensor_tensor(x[:, t:t + 2, :], ps[:, 4 + t // 2 % 4, :].rearrange("p (a d) -> p a d", a=2),
                                      x[:, t:t + 2, :], ALU.add).then_inc(b2_added, 1)
                    dve.wait_ge(b2_added, t // 2 + 1)
                dve.wait_ge(gathered[t % 4], (t // 4 + 1) * 32)
                for a in range(2):
                    if a == 1:
                        dve.wait_ge(combined, 2 * t + 1)
                    dve.scalar_tensor_tensor(out=x[:, t, :], in0=yt[t % 4][:, a, :], scalar=top8[:, t, a:a + 1],
                                             in1=x[:, t, :], op0=ALU.mult, op1=ALU.add).then_inc(combined, 1)

        @block.tensor
        def _(pe):
            pe.wait_ge(consts, 1)
            for p in range(NT // 2):
                pe.wait_ge(xn_ready, 2 * p + 2)
                wait(pe, xnT_done, p - NR + 1)
                for k in range(KD):
                    for u in (2 * p, 2 * p + 1):
                        mm = pe.transpose(ps[:, p % NR, k * 2 * P + u % 2 * P:k * 2 * P + u % 2 * P + P],
                                          xn[u % (2 * NR)][:, k * P:(k + 1) * P], identf[:, :])
                mm.then_inc(xnT_filled, 1)
            pe.wait_ge(xnT_done, NT // 2)
            pe.wait_ge(rows_loaded, 6 * 16)
            pe.transpose(ps[:, 3, 0:ROWS], rows_sb[:, :], identf[0:ROWS, 0:ROWS]).then_inc(cols_filled, 1)
            EXACT = ((0, 0), (1, 0), (0, 1))

            with pe.Fori(0, B) as b:
                def tokens(half, k, at, n):
                    return lT[half][:, k, bass.ds(b, 1), at:at + n].rearrange("p a n -> p (a n)")
                for n in range(PROJ):
                    if n % 4 == 0:
                        pe.wait_ge(wa_split, 2 + n // 4)
                    if n >= 2:
                        pe.wait_ge(proj_done, b * PROJ + n - 1)
                    if n < 8:
                        w, m, c = (1, 0)[n // 4], n % 4 // 2, n % 2
                        parts = [(h, k) for h in EXACT for k in range(KD)]
                        for i, ((hw, hx), k) in enumerate(parts):
                            mm = pe.matmul(ps[:, 6 + n % 2, :], wa[hw][:, w, k, m * P:(m + 1) * P],
                                           tokens(hx, k, c * CH, CH), start=(i == 0), stop=(i == len(parts) - 1))
                    else:
                        for j in range(2):
                            parts = [(h, k) for h in EXACT for k in range(KD)]
                            for i, ((hx, hw), k) in enumerate(parts):
                                mm = pe.matmul(ps[:, 6 + n % 2, j * D:(j + 1) * D],
                                               tokens(hx, k, ((n - 8) * 2 + j) * P, P), wa[hw][:, 2, k, :],
                                               start=(i == 0), stop=(i == len(parts) - 1))
                    mm.then_inc(proj_filled, 1)

                def self_scores(j):
                    if j < 2:
                        pe.wait_ge(proj_done, b * PROJ + 8)
                    else:
                        pe.wait_ge(a_probs, b * TB + j - 1)
                    for c in range(S // CH):
                        parts = [(h, k) for h in EXACT for k in range(KD)]
                        for i, ((hq, hk), k) in enumerate(parts):
                            mm = pe.matmul(ps[:, j % 2 * 2 + c, :], qT[hq][:, k, j * P:(j + 1) * P],
                                           kT[hk][:, k, c * CH:(c + 1) * CH],
                                           start=(i == 0), stop=(i == len(parts) - 1))
                    mm.then_inc(a_scores, 1)
                self_scores(0)
                self_scores(1)
                for j in range(TB):
                    pe.wait_ge(a_probs, b * TB + j + 1)
                    if j > 0:
                        pe.wait_ge(a_pT_lo, b * TB + j)
                    for c in range(TB):
                        mm = pe.transpose(ps[:, 4 + c // 4, c % 4 * P:(c % 4 + 1) * P],
                                          p32[j % 2][:, c * P:(c + 1) * P], identf[:, :])
                    mm.then_inc(a_pT, 1)
                    if j + 2 < TB:
                        self_scores(j + 2)
                    pe.wait_ge(a_pT_lo, b * TB + j + 1)
                    if j < 2:
                        pe.wait_ge(proj_done, (b + 1) * PROJ)
                    else:
                        pe.wait_ge(a_added, b * TB + j - 1)
                    parts = [(h, c) for c in range(TB) for h in EXACT]
                    for i, ((hp, hv), c) in enumerate(parts):
                        mm = pe.matmul(ps[:, 6 + j % 2, 0:D], pT[j % 2][hp][:, c, :], va[hv][:, c, :],
                                       start=(i == 0), stop=(i == len(parts) - 1))
                    mm.then_inc(a_out, 1)
                pe.wait_ge(a_added, (b + 1) * TB)

            pe.wait_ge(c_norm, B)
            for b in range(B):
                for k in range(KD):
                    mm = pe.transpose(ps[:, 5, :].rearrange("p (k b n) -> p k b n", k=KD, b=B)[:, k, b, 0:C],
                                      cz[:, b, k * P:(k + 1) * P], identf[0:C, 0:C])
            mm.then_inc(c_filled, 1)

            def product(dst, pairs):
                for i, (stationary, moving) in enumerate(pairs):
                    mm = pe.matmul(dst, stationary, moving, start=(i == 0), stop=(i == len(pairs) - 1))
                return mm

            def task(it_task0, t, i, units, turned=0):
                b, kind = t[0], t[1]
                dst = ps[:, bank(it_task0, i), :]
                wait(pe, task_done, it_task0 + i - 1)
                if kind == "q":
                    if t[2] == 0:
                        pe.wait_ge(wx_split, units // 2 * 4 + 2)
                    cols = slice(t[2] * CH, (t[2] + 1) * CH)
                    mm = product(dst, [(wx[hw][:, 0, k, :], lT[hx][:, k, b, cols])
                                       for hw, hx in EXACT for k in range(KD)])
                elif kind == "k":
                    cols = slice(t[2] * MW, (t[2] + 1) * MW)
                    mm = product(dst[:, 0:MW], [(wx[hw][:, 1, k, :], lT[hx][:, k, b, cols])
                                                for hw, hx in EXACT for k in range(KD)])
                elif kind == "v":
                    if t[2] == 0:
                        pe.wait_ge(wx_split, units // 2 * 4 + 4)
                    for j in range(4 if t[2] < 2 else 1):
                        at = (t[2] * 4 + j) * P
                        n = min(P, SK - at)
                        mm = product(dst[0:n, j * HW:(j + 1) * HW],
                                     [(lT[hx][:, k, b, at:at + n], wx[hw][:, 2, k, :])
                                      for hx, hw in EXACT for k in range(KD)])
                elif kind == "max":
                    _, _, h, j, c = t
                    if (j, c) == (0, 0):
                        pe.wait_ge(qk_spread[h], (units + 1) * 64)
                    mm = pe.matmul(dst[:, 0:MW], qA[b][h][:, j * P:(j + 1) * P], kA[b][h][:, c * MW:(c + 1) * MW],
                                   start=True, stop=True)
                elif kind == "m":
                    pe.wait_ge(m_reduced, units + 1)
                    mm = pe.transpose(dst[0:2 * TB, 0:P], m16[:, :], identf[:, :])
                elif kind == "oT":
                    if t[2] == 0:
                        pe.wait_ge(o_done, (units - 1) * 4)
                    for j in range(4):
                        mm = pe.transpose(dst[:, j * P:(j + 1) * P], o32[:, t[2] * 4 + j, :], identf[:, :])
                elif kind == "wo":
                    if t[2] == 0:
                        pe.wait_ge(wo_split, units // 2 * 2)
                        pe.wait_ge(task_done, turned)
                    for j in range(2):
                        mm = product(dst[:, j * D:(j + 1) * D], [(oT[ho][:, t[2] * 2 + j, :], wo[hw])
                                                                for ho, hw in EXACT])
                mm.then_inc(task_filled, 1)

            for p in range(NT // 2):
                pe.wait_ge(z_norm, 2 * p + 2)
                wait(pe, z_t32, 2 * (p - NR + 1))
                for k in range(KD):
                    for u in (2 * p, 2 * p + 1):
                        mm = pe.transpose(ps[:, p % NR, k * 2 * P + u % 2 * P:k * 2 * P + u % 2 * P + P],
                                          zn[u % (2 * NR)][:, k * P:(k + 1) * P], identf[:, :])
                mm.then_inc(z_filled, 1)
                if p == Z_BATCH + 1:
                    pe.wait_ge(z_done, Z_BATCH)
                    pe.wait_ge(c_done, 1)
                for t, i, _ in beside_z(p):
                    task(0, t, i, 0)
            pe.wait_ge(z_done, NT // 2)
            for t, i, _ in PROLOGUE[Z_TASKS:QKV]:
                task(0, t, i, 0)
            for n in range(WIDE):
                h, j = n // TB, n % TB
                if j == 0:
                    pe.wait_ge(qk_spread[h], 64)
                if n >= 2:
                    pe.wait_ge(task_done, QKV + MC * (n - 1))
                for c in range(MC):
                    mm = pe.matmul(ps[:, n % 2 * MC + c, 0:MW], qA[0][h][:, j * P:(j + 1) * P],
                                   kA[0][h][:, c * MW:(c + 1) * MW], start=True, stop=True)
                mm.then_inc(task_filled, MC)
            for t, i, _ in PROLOGUE[-1:]:
                task(0, t, i, 0)

            def score(it, s, c):
                n = it.slots + s
                b, head, kt = s // A_SLOTS, s // KT % 2, s % KT
                if s % A_SLOTS == 0 and c == 0:
                    pe.wait_ge(qk_spread[2], (it.units + b + 1) * 64)
                    pe.wait_ge(m_spread, (it.units + b + 1) * 32)
                if c == 0:
                    wait(pe, probs, n - 1)
                keys = slice(kt * P, min((kt + 1) * P, SK))
                rows = slice(0, keys.stop - keys.start)
                cols = slice(c * CH, (c + 1) * CH)
                mm = product(ps[rows, s % 2 * 2 + c, :], [(kA[b][head][:, keys], qA[b][head][:, cols]),
                                                          (kB[b][head][:, keys], qB[b][head][:, cols])])
                if c == S // CH - 1:
                    mm.then_inc(scores, 1)

            def mix(it, s, a):
                n = it.slots + s
                b, head, kt = s // A_SLOTS, s // KT, s % KT
                if a == 0:
                    pe.wait_ge(probs_lo, n + 1)
                if kt == 0 and a == 0:
                    wait(pe, o_done, (it.units * 2 + head) * 2)
                p = pr[(head * TB + kt) % PR] if kt < TB else pc
                for j in range(a * 4, a * 4 + 4):
                    dst = ps[:, 4 + j // 4, j % 4 * (HD + 1):(j % 4 + 1) * (HD + 1)]
                    cols = slice(j * P, (j + 1) * P)
                    last = kt == KT - 1
                    pe.matmul(dst, p[0][:, cols], vh[b][:, kt, head % 2, :], start=(kt == 0 and j % 4 == 0),
                              stop=False, skip_group_check=True)
                    pe.matmul(dst[:, 0:HD], p[0][:, cols], vl[b][:, kt, head % 2, :], start=False,
                              stop=False, skip_group_check=True)
                    mm = pe.matmul(dst, p[1][:, cols], vh[b][:, kt, head % 2, :], start=False,
                                   stop=last, skip_group_check=True)
                if a == 1:
                    mm.then_inc(mixed, 1)

            def turn_rows(g):
                pe.wait_ge(g_norm, 2 * g + 2)
                wait(pe, g_turned, g if g < GB else g - 1 if g >= GB + 2 else 0)
                for k in range(KD):
                    for u in range(2):
                        mm = pe.transpose(ps[:, g_banks(g)[0], (k * 2 + u) * P:(k * 2 + u + 1) * P],
                                          xn3[g * 2 + u][:, k * P:(k + 1) * P], identf[:, :])
                mm.then_inc(g_filled, 1)

            def logits(g):
                pe.wait_ge(g_turned, g + 1)
                for u in range(2):
                    t = g * 2 + u
                    product(ps[:, g_banks(g)[1], t % TB * E:(t % TB + 1) * E],
                            [(gT[g // GB][g % 2][:, k, u * P:(u + 1) * P],
                              cols_sb[:, ROW_GATE:ROWS].rearrange("p (e k) -> p k e", k=KD)[:, k, :])
                             for k in range(KD)]).then_inc(g_logits, 1)

            def pair(it):
                for s in range(IT):
                    units = it.units + 1 + (s >= A_SLOTS)
                    for quarter in range(4):
                        if quarter < 2:
                            score(it, s, quarter)
                        elif s >= LAG:
                            mix(it, s - LAG, quarter - 2)
                        elif not it.first:
                            mix(Iteration(it.hp - 1, False, False), s - LAG + IT, quarter - 2)
                        for t, i, _ in it.of(s, quarter):
                            task(it.task0, t, i, units, it.turned(t))
                    if it.last and s >= G_TURN:
                        (turn_rows, logits)[(s - G_TURN) % 2]((s - G_TURN) // 2)
            over_pairs(pe, pair)
            for s in range(IT - LAG, IT):
                for a in range(2):
                    mix(Iteration(NP - 1, False, True), s, a)
                if s == IT - LAG:
                    logits(GB - 1)
            pe.wait_ge(g_copied, 1)
            for i, t in enumerate(FINISH):
                task(LAST_TASK - len(FINISH), (1, *t), i, 2 * NP + 1, LAST_TASK - len(FINISH) + 2)

            pe.wait_ge(task_done, LAST_TASK)

            for g in range(GB, NT // 2):
                turn_rows(g)
                if g > GB:
                    logits(g - 1)
            logits(NT // 2 - 1)
            pe.wait_ge(mask_ready, 1)
            m2 = mask.rearrange("p t e -> p (t e)")
            pe.matmul(ps[:, 0, 0:NT * E], upper[:, :], m2, start=True, stop=True)
            pe.matmul(ps[:, 0, NT * E:2 * NT * E], ones16[:, :], m2, start=True, stop=True).then_inc(counted, 1)
            pe.wait_ge(onehots_ready, 1)
            product(ps[:, 1, 0:SLOTS_MAX], [(is_row[:, a, t, :], is_blk[:, a, t, :])
                                            for a in range(2) for t in range(NT)]).then_inc(rows_filled, 1)
            pe.wait_ge(eid_ready, 1)

            def turn(j, c):
                pe.wait_ge(xb_loaded[c], (j - c) * 8 + 16)
                wait(pe, e_T_lo, j - 1)
                for k in range(KD):
                    mm = pe.transpose(ps[:, c, k * P:(k + 1) * P], xb[c][:, k * P:(k + 1) * P], identf[:, :])
                mm.then_inc(e_T, 1)

            def experts_from(j, n):
                v = pe.value_load(packed[0:1, j:j + 1] if isinstance(j, int) else packed[0:1, bass.ds(j, 1)],
                                  min_val=0, max_val=(1 << EBITS * (STEP + 1)) - 1)
                return [(v >> (EBITS * i)) & ((1 << EBITS) - 1) for i in range(n)]

            def up(j, c, e):
                mine = w1[:, bass.ds(e * (2 * W1_F16), 2 * W1_F16)]
                pe.wait_ge(e_T_lo, j + 1)
                wait(pe, e_h32, j - 1)
                for m in range(MF):
                    mm = product(ps[:, 2 + c * 2 + m // 4, m % 4 * P:(m % 4 + 1) * P],
                                 [(mine[:, (hw * KD + k) * F + m * P:(hw * KD + k) * F + (m + 1) * P], xbT[c][hx][:, k, :])
                                  for hw, hx in EXACT for k in range(KD)])
                mm.then_inc(e_h, 1)

            def down(j, c, e):
                mine = w2[:, bass.ds(e * (2 * W2_F16), 2 * W2_F16)]
                pe.wait_ge(e_hT_lo, j + 1)
                wait(pe, e_yb, j - 1)
                product(ps[:, 6 + c, 0:D],
                        [(hT[c][hh][:, m, :], mine[:, (hw * MF + m) * D:(hw * MF + m + 1) * D])
                         for m in range(MF) for hh, hw in EXACT]).then_inc(e_y, 1)

            turn(0, 0)
            turn(1, 1)
            pe.wait_ge(raw_split, EARLY_CHUNKS)
            for m in (BY_POOL[-1], BEHIND[-1]):
                pe.wait_ge(*late_done(m))
            up(0, 0, experts_from(0, 1)[0])

            def block_pe(j, c, looped, n, experts):
                if looped or j + 2 < SLOTS_MAX:
                    turn(j + 2, c)
                if looped or j + 1 < SLOTS_MAX:
                    up(j + 1, 1 - c, experts[n + 1])
                down(j, c, experts[n])
            over_blocks(pe, block_pe, experts_from)

            pe.wait_ge(wm_ready, 1)
            pe.wait_ge(b2_loaded, 16)
            pe.wait_ge(e_yb, SLOTS_MAX)
            for q in range(NT // 4):
                for t in range(4 * q, 4 * q + 4):
                    mm = pe.transpose(ps[0:E, q, t % 4 * P:(t % 4 + 1) * P], wm[:, t, :], identf[:, :])
                mm.then_inc(wmT_filled, 1)
            for p in range(NT // 2):
                pe.wait_ge(wmT_ready, p // 2 + 1)
                wait(pe, b2_added, p - 3)
                for t in (2 * p, 2 * p + 1):
                    mm = pe.matmul(ps[:, 4 + p % 4, t % 2 * D:(t % 2 + 1) * D], wmT[:, t * P:(t + 1) * P], b2_sb[:, :],
                                   start=True, stop=True)
                mm.then_inc(b2_filled, 1)


_INS = ["x", "ctx_1024", "L0_attn_kernel", "L0_xattn_ln1_g", "L0_xattn_ln1_b", "L0_xattn_ln2_g",
        "L0_xattn_ln2_b", "L0_xattn_Wq", "L0_xattn_Wkv", "L0_xattn_Wo", "L0_ffn_gate_w",
        "L0_ffn_w1", "L0_ffn_b1", "L0_ffn_w2", "L0_ffn_b2"]


def kernel(**inputs):
    import numpy as _np
    import concourse.bacc as _bacc
    from concourse import mybir as _mybir
    from concourse.bass_utils import run_bass_kernel_spmd as _run

    nc = _bacc.Bacc("TRN2", target_bir_lowering=False, num_devices=1)
    arrays, args = {}, []
    for name in _INS:
        a = _np.ascontiguousarray(inputs[name])
        arrays[f"in_{name}"] = a
        args.append(nc.dram_tensor(f"in_{name}", a.shape, _mybir.dt.from_np(a.dtype), kind="ExternalInput").ap())
    shape = inputs["x"].shape
    args.append(nc.dram_tensor("out_y", shape, _mybir.dt.float32, kind="ExternalOutput").ap())
    build(nc, *args)
    r = _run(nc, [arrays], core_ids=[0])
    return r.results[0]["out_y"]
```
